# Optimizing a Trainium2 kernel written in Bass

```python
import numpy as np
import jax
import jax.numpy as jnp

def _softmax(x, axis=-1):
    return jax.nn.softmax(x, axis=axis)

def _gelu(x):
    return jax.nn.gelu(x, approximate=True)

def _silu(x):
    return jax.nn.silu(x)

def _sigmoid(x):
    return jax.nn.sigmoid(x)

def _layernorm(x, axis=-1, eps=1e-05):
    m = jnp.mean(x, axis=axis, keepdims=True)
    v = jnp.var(x, axis=axis, keepdims=True)
    return (x - m) / jnp.sqrt(v + eps)

def _scatter_add(tgt, idx, src, axis=0):
    return tgt.at[idx].add(src)

def _segment_sum(src, seg, n):
    return jax.ops.segment_sum(src, seg, n)
kernel_name = 'mk_adaln_d2_jaxref_r8_d7b011'

def setup_inputs(seed: int=0):
    np.random.seed(seed)
    _w = jnp.asarray

    def _L0_attn_setup():
        import jax, jax.numpy as jnp
        import numpy as np
        NUM_HEADS = 16
        HEAD_SIZE = 128

        def _alibi_mask(seq_len: int, num_heads: int) -> jnp.ndarray:
            if num_heads <= 8:
                slopes = jnp.asarray([1.0 / 2.0 ** i for i in range(num_heads)], dtype=jnp.float32)
            else:
                slopes = jnp.asarray([1.0 / 2.0 ** (i / 2.0) for i in range(num_heads)], dtype=jnp.float32)
            i = jnp.arange(seq_len)[:, None]
            j = jnp.arange(seq_len)[None, :]
            base = jnp.where(j <= i, -(i - j).astype(jnp.float32), -jnp.inf)
            return slopes[:, None, None] * base
        key = jax.random.key(seed)
        ks = jax.random.split(key, 5)
        H = 256
        s = 0.02
        return {'x': jax.random.normal(ks[0], (2, 256, H), dtype=jnp.float32), 'qkv_w': jax.random.normal(ks[1], (H, 3 * NUM_HEADS * HEAD_SIZE), dtype=jnp.float32) * s, 'qkv_b': jax.random.normal(ks[2], (3 * NUM_HEADS * HEAD_SIZE,), dtype=jnp.float32) * s, 'out_w': jax.random.normal(ks[3], (NUM_HEADS * HEAD_SIZE, H), dtype=jnp.float32) * s, 'out_b': jax.random.normal(ks[4], (H,), dtype=jnp.float32) * s}
    _L0_attn_in = _L0_attn_setup()

    def _L0_ffn_setup():
        import jax, jax.numpy as jnp
        import numpy as np
        import math
        B, S, D = (2, 256, 256)
        P = 4
        PW = 2
        L = 2
        STD = 0.02
        EPS = 1e-05

        def _layer_norm(x, g, b):
            m = jnp.mean(x, axis=-1, keepdims=True)
            v = jnp.mean(jnp.square(x - m), axis=-1, keepdims=True)
            return (x - m) * jax.lax.rsqrt(v + EPS) * g + b
        key = jax.random.key(seed)
        ks = jax.random.split(key, 16)
        n = lambda k, shape: jax.random.normal(k, shape, dtype=jnp.float32) * STD
        inp = {'x': jax.random.normal(ks[0], (B, S, D), dtype=jnp.float32), 'amp_w': n(ks[1], (D, D)), 'amp_b': jnp.zeros((D,), jnp.float32), 'ph_w': n(ks[2], (D, D)), 'ph_b': jnp.zeros((D,), jnp.float32), 'ent_w': n(ks[3], (L, D, P * D)), 'ent_b': jnp.zeros((L, P * D), jnp.float32), 'ent_pw': n(ks[4], (L, P * D, D)), 'ent_pb': jnp.zeros((L, D), jnp.float32), 'path_w': n(ks[5], (L, PW, D, D)), 'path_b': jnp.zeros((L, PW, D), jnp.float32), 'phase': jax.random.normal(ks[6], (L, PW, D), dtype=jnp.float32), 'ln3_g': jnp.ones((L, D), jnp.float32), 'ln3_b': jnp.zeros((L, D), jnp.float32), 'ln4_g': jnp.ones((L, D), jnp.float32), 'ln4_b': jnp.zeros((L, D), jnp.float32)}
        return inp
    _L0_ffn_in = _L0_ffn_setup()
    _L0_c = _w((lambda *s: np.random.randn(*s).astype(np.float32) * 0.05)(4, 256))
    _L0_wmod = _w((lambda *s: np.random.randn(*s).astype(np.float32) * 0.05)(256, 6 * 256) * 256 ** (-0.5))

    def _L1_attn_setup():
        import jax, jax.numpy as jnp
        import numpy as np
        B, S, H = (4, 256, 256)
        key = jax.random.key(seed)
        k1, k2, k3 = jax.random.split(key, 3)
        xav_qkv = float(np.sqrt(6.0 / (H + 3 * H)))
        xav_out = float(np.sqrt(6.0 / (H + H)))
        return {'hidden_states': jax.random.normal(k1, (B, S, H), dtype=jnp.float32), 'w_qkv': jax.random.uniform(k2, (3 * H, H), minval=-xav_qkv, maxval=xav_qkv, dtype=jnp.float32), 'b_qkv': jnp.zeros((3 * H,), dtype=jnp.float32), 'w_out': jax.random.uniform(k3, (H, H), minval=-xav_out, maxval=xav_out, dtype=jnp.float32), 'b_out': jnp.zeros((H,), dtype=jnp.float32)}
    _L1_attn_in = _L1_attn_setup()

    def _L1_ffn_setup():
        import jax, jax.numpy as jnp
        import numpy as np
        HIDDEN = 256
        INTER = 688
        LUT_SIZE = 16

        def _ghost_linear(x, idx, lut):
            w = lut[idx]
            return jnp.einsum('bsh,oh->bso', x, w)
        key = jax.random.key(seed)
        k_x, k_lut, k_g, k_u, k_d = jax.random.split(key, 5)
        x = jax.random.normal(k_x, (2, 512, HIDDEN), dtype=jnp.float32)
        lut = jax.random.normal(k_lut, (LUT_SIZE,), dtype=jnp.float32) * 0.02
        gate_idx = jax.random.randint(k_g, (INTER, HIDDEN), 0, LUT_SIZE, dtype=jnp.int32)
        up_idx = jax.random.randint(k_u, (INTER, HIDDEN), 0, LUT_SIZE, dtype=jnp.int32)
        down_idx = jax.random.randint(k_d, (HIDDEN, INTER), 0, LUT_SIZE, dtype=jnp.int32)
        return {'x': x, 'lut': lut, 'gate_idx': gate_idx, 'up_idx': up_idx, 'down_idx': down_idx}
    _L1_ffn_in = _L1_ffn_setup()
    _L1_c = _w((lambda *s: np.random.randn(*s).astype(np.float32) * 0.05)(4, 256))
    _L1_wmod = _w((lambda *s: np.random.randn(*s).astype(np.float32) * 0.05)(256, 6 * 256) * 256 ** (-0.5))
    _d = {'L0_attn_x': _L0_attn_in['x'], 'L0_attn_qkv_w': _L0_attn_in['qkv_w'], 'L0_attn_qkv_b': _L0_attn_in['qkv_b'], 'L0_attn_out_w': _L0_attn_in['out_w'], 'L0_attn_out_b': _L0_attn_in['out_b'], 'L0_ffn_amp_w': _L0_ffn_in['amp_w'], 'L0_ffn_amp_b': _L0_ffn_in['amp_b'], 'L0_ffn_ph_w': _L0_ffn_in['ph_w'], 'L0_ffn_ph_b': _L0_ffn_in['ph_b'], 'L0_ffn_ent_w': _L0_ffn_in['ent_w'], 'L0_ffn_ent_b': _L0_ffn_in['ent_b'], 'L0_ffn_ent_pw': _L0_ffn_in['ent_pw'], 'L0_ffn_ent_pb': _L0_ffn_in['ent_pb'], 'L0_ffn_path_w': _L0_ffn_in['path_w'], 'L0_ffn_path_b': _L0_ffn_in['path_b'], 'L0_ffn_phase': _L0_ffn_in['phase'], 'L0_ffn_ln3_g': _L0_ffn_in['ln3_g'], 'L0_ffn_ln3_b': _L0_ffn_in['ln3_b'], 'L0_ffn_ln4_g': _L0_ffn_in['ln4_g'], 'L0_ffn_ln4_b': _L0_ffn_in['ln4_b'], 'L0_c': _L0_c, 'L0_wmod': _L0_wmod, 'L1_attn_w_qkv': _L1_attn_in['w_qkv'], 'L1_attn_b_qkv': _L1_attn_in['b_qkv'], 'L1_attn_w_out': _L1_attn_in['w_out'], 'L1_attn_b_out': _L1_attn_in['b_out'], 'L1_ffn_lut': _L1_ffn_in['lut'], 'L1_ffn_gate_idx': _L1_ffn_in['gate_idx'], 'L1_ffn_up_idx': _L1_ffn_in['up_idx'], 'L1_ffn_down_idx': _L1_ffn_in['down_idx'], 'L1_c': _L1_c, 'L1_wmod': _L1_wmod}
    _x0 = _d['L0_attn_x']
    _d['L0_attn_x'] = jax.random.normal(jax.random.fold_in(jax.random.key(seed), 1), (4, 512, 256), dtype=_x0.dtype)
    del _x0
    return _d

def reference(L0_attn_x, L0_attn_qkv_w, L0_attn_qkv_b, L0_attn_out_w, L0_attn_out_b, L0_ffn_amp_w, L0_ffn_amp_b, L0_ffn_ph_w, L0_ffn_ph_b, L0_ffn_ent_w, L0_ffn_ent_b, L0_ffn_ent_pw, L0_ffn_ent_pb, L0_ffn_path_w, L0_ffn_path_b, L0_ffn_phase, L0_ffn_ln3_g, L0_ffn_ln3_b, L0_ffn_ln4_g, L0_ffn_ln4_b, L0_c, L0_wmod, L1_attn_w_qkv, L1_attn_b_qkv, L1_attn_w_out, L1_attn_b_out, L1_ffn_lut, L1_ffn_gate_idx, L1_ffn_up_idx, L1_ffn_down_idx, L1_c, L1_wmod):

    def _L0_attn_ref(x, qkv_w, qkv_b, out_w, out_b):
        import jax, jax.numpy as jnp
        import numpy as np
        NUM_HEADS = 16
        HEAD_SIZE = 128

        def _alibi_mask(seq_len: int, num_heads: int) -> jnp.ndarray:
            if num_heads <= 8:
                slopes = jnp.asarray([1.0 / 2.0 ** i for i in range(num_heads)], dtype=jnp.float32)
            else:
                slopes = jnp.asarray([1.0 / 2.0 ** (i / 2.0) for i in range(num_heads)], dtype=jnp.float32)
            i = jnp.arange(seq_len)[:, None]
            j = jnp.arange(seq_len)[None, :]
            base = jnp.where(j <= i, -(i - j).astype(jnp.float32), -jnp.inf)
            return slopes[:, None, None] * base
        b, s, h = x.shape
        qkv = x @ qkv_w + qkv_b
        q, k, v = jnp.split(qkv, 3, axis=-1)

        def to_heads(t):
            return t.reshape(b, s, NUM_HEADS, HEAD_SIZE).transpose(0, 2, 1, 3)
        q, k, v = (to_heads(q), to_heads(k), to_heads(v))
        scores = jnp.einsum('bhid,bhjd->bhij', q, k) + _alibi_mask(s, NUM_HEADS)[None]
        attn = jax.nn.softmax(scores, axis=-1)
        ctx = jnp.einsum('bhij,bhjd->bhid', attn, v)
        ctx = ctx.transpose(0, 2, 1, 3).reshape(b, s, NUM_HEADS * HEAD_SIZE)
        return ctx @ out_w + out_b

    def _L0_ffn_ref(x, amp_w, amp_b, ph_w, ph_b, ent_w, ent_b, ent_pw, ent_pb, path_w, path_b, phase, ln3_g, ln3_b, ln4_g, ln4_b):
        import jax, jax.numpy as jnp
        import numpy as np
        import math
        B, S, D = (2, 256, 256)
        P = 4
        PW = 2
        L = 2
        STD = 0.02
        EPS = 1e-05

        def _layer_norm(x, g, b):
            m = jnp.mean(x, axis=-1, keepdims=True)
            v = jnp.mean(jnp.square(x - m), axis=-1, keepdims=True)
            return (x - m) * jax.lax.rsqrt(v + EPS) * g + b
        amp = jax.nn.sigmoid(x @ amp_w + amp_b)
        ph = jnp.tanh(x @ ph_w + ph_b) * math.pi
        h = (jnp.cos(ph) + jnp.sin(ph)) * amp
        for l in range(L):
            e = h @ ent_w[l] + ent_b[l]
            ent = e @ ent_pw[l] + ent_pb[l]
            h = _layer_norm(h + ent, ln3_g[l], ln3_b[l])
            t = jnp.einsum('bsd,pdf->pbsf', h, path_w[l]) + path_b[l][:, None, None, :]
            mod = jnp.cos(phase[l]) + jnp.sin(phase[l])
            interf = jnp.sum(t * mod[:, None, None, :], axis=0)
            h = _layer_norm(h + interf, ln4_g[l], ln4_b[l])
        return h

    def _L1_attn_ref(hidden_states, w_qkv, b_qkv, w_out, b_out):
        import jax, jax.numpy as jnp
        import numpy as np
        B, S, H = (4, 256, 256)
        Bc, Sc, Hc = hidden_states.shape
        scaling = jnp.sqrt(jnp.asarray(Hc, hidden_states.dtype))
        qkv = jnp.einsum('bsh,oh->bso', hidden_states, w_qkv) + b_qkv
        q, k, v = jnp.split(qkv, 3, axis=-1)
        scores = jnp.einsum('bqh,bkh->bqk', q, k) / scaling
        probs = jax.nn.softmax(scores, axis=-1)
        context = jnp.einsum('bqk,bkh->bqh', probs, v)
        out = jnp.einsum('bsh,oh->bso', context, w_out) + b_out
        return out

    def _L1_ffn_ref(x, lut, gate_idx, up_idx, down_idx):
        import jax, jax.numpy as jnp
        import numpy as np
        HIDDEN = 256
        INTER = 688
        LUT_SIZE = 16

        def _ghost_linear(x, idx, lut):
            w = lut[idx]
            return jnp.einsum('bsh,oh->bso', x, w)
        gate = _ghost_linear(x, gate_idx, lut)
        up = _ghost_linear(x, up_idx, lut)
        h = jax.nn.silu(gate) * up
        return _ghost_linear(h, down_idx, lut)
    x = L0_attn_x
    mod = (_silu(L0_c) @ L0_wmod).reshape(L0_c.shape[0], 6, 1, -1)
    sa, ca, ga, sb, cb, gb = (mod[:, 0], mod[:, 1], mod[:, 2], mod[:, 3], mod[:, 4], mod[:, 5])
    ga = (2 * (ga >= 0) - 1) * jnp.maximum(jnp.abs(ga), 0.25)
    gb = (2 * (gb >= 0) - 1) * jnp.maximum(jnp.abs(gb), 0.25)
    h = _layernorm(x, axis=-1) * (1 + ca) + sa
    x = x + ga * _L0_attn_ref(h, L0_attn_qkv_w, L0_attn_qkv_b, L0_attn_out_w, L0_attn_out_b)
    h = _layernorm(x, axis=-1) * (1 + cb) + sb
    x = x + gb * _L0_ffn_ref(h, L0_ffn_amp_w, L0_ffn_amp_b, L0_ffn_ph_w, L0_ffn_ph_b, L0_ffn_ent_w, L0_ffn_ent_b, L0_ffn_ent_pw, L0_ffn_ent_pb, L0_ffn_path_w, L0_ffn_path_b, L0_ffn_phase, L0_ffn_ln3_g, L0_ffn_ln3_b, L0_ffn_ln4_g, L0_ffn_ln4_b)
    mod = (_silu(L1_c) @ L1_wmod).reshape(L1_c.shape[0], 6, 1, -1)
    sa, ca, ga, sb, cb, gb = (mod[:, 0], mod[:, 1], mod[:, 2], mod[:, 3], mod[:, 4], mod[:, 5])
    ga = (2 * (ga >= 0) - 1) * jnp.maximum(jnp.abs(ga), 0.25)
    gb = (2 * (gb >= 0) - 1) * jnp.maximum(jnp.abs(gb), 0.25)
    h = _layernorm(x, axis=-1) * (1 + ca) + sa
    x = x + ga * _L1_attn_ref(h, L1_attn_w_qkv, L1_attn_b_qkv, L1_attn_w_out, L1_attn_b_out)
    h = _layernorm(x, axis=-1) * (1 + cb) + sb
    x = x + gb * _L1_ffn_ref(h, L1_ffn_lut, L1_ffn_gate_idx, L1_ffn_up_idx, L1_ffn_down_idx)
    return x

_drawn_inputs = setup_inputs


def setup_inputs(seed=0):
    import zlib

    import numpy as np

    out = dict(_drawn_inputs(seed))
    spreads = {'L0_ffn_amp_b': (0.0, 0.637),
     'L0_ffn_ph_b': (0.0, 0.1),
     'L0_ffn_ent_b': (0.0, 0.1),
     'L0_ffn_ent_pb': (0.0, 0.1),
     'L0_ffn_path_b': (0.0, 0.1),
     'L0_ffn_ln3_g': (1.0, 0.2),
     'L0_ffn_ln3_b': (0.0, 0.1),
     'L0_ffn_ln4_g': (1.0, 0.2),
     'L0_ffn_ln4_b': (0.0, 0.1),
     'L1_attn_b_qkv': (0.0, 0.336),
     'L1_attn_b_out': (0.0, 0.334)}
    factors = {'L0_attn_qkv_b': 8.0, 'L0_attn_out_b': 8.0, 'L1_ffn_lut': 5.629}
    for name, (base, spread) in spreads.items():
        noise = np.random.default_rng([zlib.crc32(name.encode()), seed]).standard_normal(out[name].shape)
        drawn = base * np.exp(spread * noise) if base else spread * noise
        out[name] = jnp.asarray(drawn.astype(out[name].dtype))
    for name, factor in factors.items():
        out[name] = (out[name] * factor).astype(out[name].dtype)
    return out
```

```python
import concourse.bass as bass
from concourse import mybir

F32 = mybir.dt.float32
F16 = mybir.dt.float16
I32 = mybir.dt.int32
ALU = mybir.AluOpType
ACT = mybir.ActivationFunctionType
AX = mybir.AxisListType
ds = bass.ds

P = 128
B, S, D = 4, 512, 256
KT = D // P
TB = S // P
NT = B * TB
H = 16
HD = 128
QKW, VW = 2 * H * HD, H * HD
LE, PWN, EW = 2, 2, 1024
EC = EW // P
INTER = 688
IC = -(-INTER // P)
LASTI = INTER - (IC - 1) * P
LUTN = 16
IDXW = 2 * KT * INTER + IC * D
EPS = 1e-5
WS = 16.0
PS = 16.0
MASKED = 1e30
VALUE_UNITS = B * H
NSTEP = B * H
CHUNK = 1024
C_QKVB = 0
C_AMPB = C_QKVB + 3 * H
C_PHB = C_AMPB + KT
C_LN = C_PHB + KT
C_B1 = C_LN + 4 * LE * KT
C_ENTB = C_B1 + 3 * KT
NCOL = C_ENTB + LE * EC
R_OUTB, R_ENTPB, R_PATHB, R_PHASE, R_LN4G, R_LN4B, R_BOUT = 0, 1, 3, 7, 11, 12, 13
NROW = 14
DCHUNK = IDXW // 4
QTILES = (3, 2, 0, 1)
SOFF = {3: 0, 2: 512, 0: 896, 1: 1024}
SW = 1280
JOFF = {0: 0, 1: 512, 2: 896, 3: 1152}
PT_UNITS = ((1,), (2, 3), (0,))


class Kit:

    def __init__(self, nc):
        self.nc = nc
        self.n = 0

    def sem(self, name):
        self.n += 1
        return self.nc.alloc_semaphore(name)

    def sb(self, name, shape, dt):
        return self.nc.alloc_sbuf_tensor(name, shape, dt)

    def at(self, name, shape, dt, offset):
        return self.nc.alloc_sbuf_tensor_at(name, shape, dt, offset=offset)


def wait_apart(e, sem, value, passed):
    e.wait_ge(sem, value)
    if not isinstance(value, int):
        e.sem_inc(passed, 1)


def split3(pe, out, pairs, **kw):
    terms = []
    for (ah, al), (bh, bl) in pairs:
        terms += [(ah, bh), (ah, bl), (al, bh)]
    for i, (a, b) in enumerate(terms):
        ins = pe.matmul(out, a, b, start=(i == 0), stop=(i == len(terms) - 1), **kw)
    return ins


def build(nc, A, upto=9):
    k = Kit(nc)
    base = nc.sbuf_base + 31 & ~31
    slab = nc.alloc_sbuf_tensor("slab", [P, (nc.sbuf_usable_end - base) // 4 - 24], F32)
    base = base
    cur = [base]

    def place(name, shape, dt, at=None):
        n = 1
        for d in shape[1:]:
            n *= d
        n *= 2 if dt == F16 else 4
        if at is None:
            at = cur[0]
            cur[0] = (at + n + 31) & ~31
        assert at + n <= nc.sbuf_usable_end, (name, at + n)
        t = k.at(name, shape, dt, at)
        return t, at, at + ((n + 31) & ~31)

    def new(name, shape, dt):
        return place(name, shape, dt)[0]

    def region(nbytes):
        at = cur[0]
        cur[0] = (at + nbytes + 31) & ~31
        return at

    x = new("x", [P, NT, D], F32)
    hT_hi = new("hT_hi", [P, KT, B * S], F16)
    hT_lo = new("hT_lo", [P, KT, B * S], F16)
    cols = new("cols", [P, NCOL], F32)
    modT = new("modT", [P, 2, 12, B], F32)
    ident = new("ident", [P, P], F32)
    ones16 = new("ones16", [1, P], F16)
    mhalf = new("mhalf", [P, NT], F32)
    stats = new("stats", [P, NT, 6], F32)
    mean = new("mean", [P, NT], F32)
    half_var = new("half_var", [P, 4, NT], F32)
    vareps = new("vareps", [P, NT], F32)
    rstd = new("rstd", [P, NT], F32)
    gate = new("gate", [P, B * D], F32)
    slopes = new("slopes", [P, H], F32)
    entry = new("entry", [P, LUTN], F32)
    lutb = new("lutb", [P, 3, LUTN], F32)
    lut16 = new("lut16", [P, LUTN], F16)

    BIG = region(128 * 1024)
    DEC = region(2 * IDXW * 2)
    WORK = region(21 * 1024)
    end = cur[0]
    assert end <= nc.sbuf_usable_end, end - nc.sbuf_usable_end

    def layout(start):
        p = [start]

        def f(name, shape, dt):
            t, _, p[0] = place(name, shape, dt, p[0])
            return t
        f.pos = p
        return f

    big0 = layout(BIG)
    wqk_hi = big0("wqk_hi", [P, KT, QKW], F16)
    wqk_lo = big0("wqk_lo", [P, KT, QKW], F16)
    wv_hi = big0("wv_hi", [P, KT, VW], F16)
    wv_lo = big0("wv_lo", [P, KT, VW], F16)
    wo_hi = big0("wo_hi", [P, H, D], F16)
    wo_lo = big0("wo_lo", [P, H, D], F16)
    VREG = big0.pos[0]
    v_hi = big0("v_hi", [P, TB, VW], F16)
    v_lo = big0("v_lo", [P, TB, VW], F16)
    STAGE = big0.pos[0]
    lnbuf = layout(VREG)
    xn0 = lnbuf("xn0", [P, NT, D], F32)
    tmp0 = lnbuf("tmp0", [P, KT, B * S], F32)
    stg = layout(STAGE)
    NSTAGE = 4
    stage = [stg(f"stage{i}", [P, KT * CHUNK], F32) for i in range(NSTAGE)]

    decoded = layout(DEC)
    wdec_hi = decoded("wdec_hi", [P, IDXW], F16)
    wdec_lo = decoded("wdec_lo", [P, IDXW], F16)
    idx32 = layout(DEC)("idx32", [P, IDXW], I32)
    wk0 = layout(WORK)
    q_hi = wk0("q_hi", [P, S], F16)
    q_lo = wk0("q_lo", [P, S], F16)
    k_hi = wk0("k_hi", [P, S], F16)
    k_lo = wk0("k_lo", [P, S], F16)
    prob = wk0("prob", [P, SW], F32)
    pt_hi = wk0("pt_hi", [P, SW], F16)
    pt_lo = wk0("pt_lo", [P, SW], F16)
    ctx_hi = wk0("ctx_hi", [P, S], F16)
    ctx_lo = wk0("ctx_lo", [P, S], F16)
    alibi = wk0("alibi", [P, S], F32)
    dist = wk0("dist", [P, S], F32)
    smin = wk0("smin", [P, TB], F32)
    ssum = wk0("ssum", [P, TB], F32)
    sinv = wk0("sinv", [P, TB], F32)
    nbias = wk0("nbias", [P, 3 * H], F32)
    assert wk0.pos[0] <= end, wk0.pos[0] - end
    wkm = layout(DEC)
    wmod = wkm("wmod", [P, 2, KT, 6 * D], F32)
    cT = wkm("cT", [P, 2 * KT * B], F32)
    sil = wkm("sil", [P, 2 * KT * B], F32)
    sig = wkm("sig", [P, 2 * KT * B], F32)
    gcol = wkm("gcol", [P, 2 * 2 * B * KT], F32)
    gsgn = wkm("gsgn", [P, 2 * 2 * B * KT], F32)
    grow = wkm("grow", [2 * 2 * B * KT, P], F32)
    assert wkm.pos[0] <= end
    bank = [nc.alloc_psum_tensor(f"bank{i}", [P, 512], F32) for i in range(8)]
    gate_rows = nc.dram_tensor("gate_rows", [2 * 2 * B * KT, P], F32, kind="Internal").ap()

    SA, CA, GA, SB, CB, GB = (KT * i for i in range(6))

    s_passed = k.sem("waits_passed")

    def load_gate(sp, layer, which, sem):
        r0 = (layer * 2 + which) * B * KT
        src = gate_rows[r0:r0 + B * KT, :].rearrange("r d -> (r d)")
        return sp.dma_start(gate[:], bass.AP(tensor=src.tensor, offset=src.offset, ap=[[0, P], [1, B * D]])
                            ).then_inc(sem, 16)

    class LayerNormSems:
        def __init__(self, tag):
            self.stats = k.sem(f"{tag}_stats")
            self.aggr = k.sem(f"{tag}_aggr")
            self.vareps = k.sem(f"{tag}_vareps")
            self.rstd = k.sem(f"{tag}_rstd")
            self.xn = k.sem(f"{tag}_xn")
            self.turned = k.sem(f"{tag}_turned")
            self.tmp = k.sem(f"{tag}_tmp")
            self.hi = k.sem(f"{tag}_hi")
            self.lo = k.sem(f"{tag}_lo")

    def combine_stats(v, sem, b, done, eps):
        tiles = ds(b * TB, TB)
        even_mean, even_m2 = stats[:, tiles, 1], stats[:, tiles, 2]
        odd_mean, odd_m2 = stats[:, tiles, 4], stats[:, tiles, 5]
        dif, tot, m2, dd = (half_var[:, i, tiles] for i in range(4))
        v.tensor_tensor(dif, even_mean, odd_mean, ALU.subtract).then_inc(sem, 1)
        v.tensor_tensor(tot, even_mean, odd_mean, ALU.add).then_inc(sem, 1)
        v.scalar_tensor_tensor(m2, even_m2, D * eps, odd_m2, ALU.add, ALU.add).then_inc(sem, 1)
        v.wait_ge(sem, done + 2)
        v.tensor_scalar(mean[:, tiles], tot, 0.5, None, ALU.mult).then_inc(sem, 1)
        v.scalar_tensor_tensor(dd, dif, 0.25, dif, ALU.mult, ALU.mult).then_inc(sem, 1)
        v.wait_ge(sem, done + 5)
        return v.scalar_tensor_tensor(vareps[:, tiles], m2, 1.0 / D, dd, ALU.mult, ALU.add)

    def ln_vector(v, s, xn, src, eps, tile_ready=None):
        with v.Fori(0, B) as b:
            for t in range(TB):
                if tile_ready is not None:
                    tile_ready(v, b, t)
                v.bn_stats(stats[:, b * TB + t, :], src(b, t)).then_inc(s.stats, 1)
            v.wait_ge(s.stats, b * TB + TB)
            combine_stats(v, s.aggr, b, 5 * b, eps).then_inc(s.vareps, 1)
        with v.Fori(0, B) as b:
            v.wait_ge(s.rstd, b + 1)
            for t in range(TB):
                v.tensor_scalar(xn[:, b * TB + t, :], src(b, t), mean[:, ds(b * TB + t, 1)],
                                rstd[:, ds(b * TB + t, 1)], ALU.subtract, ALU.mult).then_inc(s.xn, 1)

    def ln_pow(g, s):
        with g.Fori(0, B) as b:
            g.wait_ge(s.vareps, b + 1)
            g.tensor_tensor(rstd[:, ds(b * TB, TB)], vareps[:, ds(b * TB, TB)], mhalf[:, ds(b * TB, TB)],
                            ALU.pow).then_inc(s.rstd, 1)

    def ln_turn(pe, s, xn, step=0):
        for b in range(B):
            for c in range(KT):
                for t in range(TB):
                    if c == 0:
                        pe.wait_ge(s.xn, b * TB + t + 1)
                    ins = pe.transpose(bank[2 * b + c][:, t * P:(t + 1) * P],
                                       xn[:, b * TB + t, c * P:(c + 1) * P], ident[:, :])
                ins.then_inc(s.turned, 1)

    def ln_modulate(v, s, tmp, scale, bias):
        for b in range(B):
            for c in range(KT):
                v.wait_ge(s.turned, b * KT + c + 1)
                v.tensor_scalar(tmp[:, c, b * S:(b + 1) * S], bank[2 * b + c][:, :], scale(b, c), bias(b, c),
                                ALU.mult, ALU.add).then_inc(s.tmp, 1)

    def parts_hi(act, s, tmp):
        with act.Fori(0, B) as b:
            for c in range(KT):
                act.wait_ge(s.tmp, b * KT + c + 1)
                act.activation(hT_hi[:, c, ds(b * S, S)], tmp[:, c, ds(b * S, S)], ACT.Copy).then_inc(s.hi, 1)

    def parts_lo(g, s, tmp):
        with g.Fori(0, B) as b:
            for c in range(KT):
                g.wait_ge(s.hi, b * KT + c + 1)
                g.tensor_tensor(hT_lo[:, c, ds(b * S, S)], tmp[:, c, ds(b * S, S)],
                                hT_hi[:, c, ds(b * S, S)], ALU.subtract).then_inc(s.lo, 1)

    s_x, s_cols, s_c, s_wmod = (k.sem(n) for n in ("x_in", "cols_in", "c_in", "wmod_in"))
    s_slp = k.sem("slopes_in")
    s_stage = [k.sem(f"stage_in{i}") for i in range(NSTAGE)]
    s_whi, s_wlo = k.sem("w_hi"), k.sem("w_lo")
    s_const, s_sig, s_sil, s_modp, s_mod, s_gcol, s_gturn, s_grow, s_gout = (
        k.sem(n) for n in ("consts", "sigmoid", "silu", "mod_psum", "mod_done", "gate_cols", "gate_turned",
                           "gate_row", "gate_out"))
    ln0 = LayerNormSems("ln0")
    chunks = [(A["wv"], c, wv_hi, wv_lo, 1.0) for c in range(0, VW, CHUNK)]
    chunks += [(A["wqk"], c, wqk_hi, wqk_lo, -1.0 if c < H * HD else 1.0) for c in range(0, QKW, CHUNK)]
    chunks += [(A["wo"], c, wo_hi, wo_lo, 1.0) for c in range(0, H, H // 2)]

    def chunk_view(t, c):
        if t is wo_hi or t is wo_lo:
            return t[:, c:c + H // 2, :]
        return t[:, :, c:c + CHUNK]

    def stage_view(i, t):
        if t is wo_hi or t is wo_lo:
            return stage[i % NSTAGE][:, :].rearrange("p (h n) -> p h n", h=H // 2)
        return stage[i % NSTAGE][:, :].rearrange("p (k n) -> p k n", k=KT)

    with nc.Block() as block:
        @block.sync
        def _(sp):
            sp.dma_start(cT[:], A["cT"]).then_inc(s_c, 16)
            sp.dma_start(cols[:], A["cols"]).then_inc(s_cols, 16)
            sp.dma_start(wmod[:], A["wmod"]).then_inc(s_wmod, 16)
            sp.dma_start(x[:], A["x"]).then_inc(s_x, 16)
            sp.dma_start(slopes[:], A["slopes"]).then_inc(s_slp, 16)
            for i, (src, c, hi, lo, sign) in enumerate(chunks):
                if i >= NSTAGE:
                    sp.wait_ge(s_wlo, i - NSTAGE + 1)
                view = src[:, c:c + H // 2, :] if hi is wo_hi else src[:, :, c:c + CHUNK]
                sp.dma_start(stage_view(i, hi), view).then_inc(s_stage[i % NSTAGE], 16)
            sp.wait_ge(s_grow, 1)
            sp.dma_start(gate_rows, grow[:]).then_inc(s_gout, 16)
            sp.wait_ge(s_gout, 16)
            load_gate(sp, 0, 0, s_gout)
            sp.wait_ge(s_gout, 32)
            sp.wait_ge(s_slp, 16)

        @block.gpsimd
        def _(g):
            g.memset(ident[:], 0.0).then_inc(s_const, 1)
            for i in range(LUTN):
                g.memset(entry[:, i:i + 1], float(i)).then_inc(s_const, 1)
            g.memset(ones16[:], 1.0).then_inc(s_const, 1)
            g.memset(mhalf[:], -0.5).then_inc(s_const, 1)
            g.wait_ge(s_const, LUTN + 3)
            g.affine_select(out=ident[:], in_=ident[:], pattern=[[-1, P]], compare_op=ALU.not_equal, fill=1.0,
                            base=0, channel_multiplier=1).then_inc(s_const, 1)
            ln_pow(g, ln0)
            parts_lo(g, ln0, tmp0)

        @block.scalar
        def _(act):
            act.preload_act_table(ACT.Exp)
            act.wait_ge(s_c, 16)
            act.activation(sig[:], cT[:], ACT.Exp, scale=-1.0).then_inc(s_sig, 1)
            for i, (src, c, hi, lo, sign) in enumerate(chunks):
                act.wait_ge(s_stage[i % NSTAGE], 16 * (i // NSTAGE + 1))
                act.activation(chunk_view(hi, c), stage_view(i, hi), ACT.Copy, scale=sign * WS).then_inc(s_whi, 1)
                if i == 3:
                    parts_hi(act, ln0, tmp0)
                    act.preload_act_table(ACT.Exp)

        @block.tensor
        def _(pe):
            pe.wait_ge(s_sil, 1)
            pe.wait_ge(s_wmod, 16)
            for layer in range(2):
                for j in range(12):
                    for c in range(KT):
                        ins = pe.matmul(bank[layer][:, j * B:(j + 1) * B],
                                        wmod[:, layer, c, j * P:(j + 1) * P],
                                        sil[:, (layer * KT + c) * B:(layer * KT + c + 1) * B],
                                        start=(c == 0), stop=(c == KT - 1))
                ins.then_inc(s_modp, 1)
            pe.wait_ge(s_gcol, 1)
            pe.wait_ge(s_const, LUTN + 4)
            pe.transpose(bank[2][0:32, 0:P], gcol[:, :], ident[:, :]).then_inc(s_gturn, 1)
            pe.wait_ge(s_grow, 1)
            pe.wait_ge(s_mod, 2)
            ln_turn(pe, ln0, xn0)

        @block.vector
        def _(v):
            v.wait_ge(s_sig, 1)
            v.tensor_scalar(sig[:], sig[:], 1.0, None, ALU.add).then_inc(s_sig, 1)
            v.wait_ge(s_sig, 2)
            v.reciprocal(sig[:], sig[:]).then_inc(s_sig, 1)
            v.wait_ge(s_sig, 3)
            v.tensor_tensor(sil[:], sig[:], cT[:], ALU.mult).then_inc(s_sil, 1)
            for layer in range(2):
                v.wait_ge(s_modp, layer + 1)
                v.tensor_copy(modT[:, layer, :, :].rearrange("p j b -> p (j b)"),
                              bank[layer][:, 0:12 * B]).then_inc(s_mod, 1)
            v.wait_ge(s_mod, 2)
            for layer in range(2):
                for n, j in enumerate((GA, GB)):
                    o = (layer * 2 + n) * B * KT
                    v.tensor_copy(gcol[:, o:o + B * KT].rearrange("p (b c) -> p b c", b=B),
                                  modT[:, layer, j:j + KT, :].rearrange("p c b -> p b c")).then_inc(s_mod, 1)
                for j in (CA, CB):
                    v.tensor_scalar(modT[:, layer, j:j + KT, :], modT[:, layer, j:j + KT, :], 1.0, None,
                                    ALU.add).then_inc(s_mod, 1)
            v.wait_ge(s_mod, 10)
            v.tensor_scalar(gsgn[:], gcol[:], 0.0, 2.0, ALU.is_ge, ALU.mult).then_inc(s_mod, 1)
            v.wait_ge(s_mod, 11)
            v.scalar_tensor_tensor(gcol[:], gsgn[:], -1.0, gcol[:], ALU.add, ALU.mult).then_inc(s_mod, 1)
            v.wait_ge(s_mod, 12)
            v.tensor_scalar(gcol[:], gcol[:], 0.25, None, ALU.max).then_inc(s_mod, 1)
            v.wait_ge(s_mod, 13)
            v.scalar_tensor_tensor(gcol[:], gsgn[:], -1.0, gcol[:], ALU.add, ALU.mult).then_inc(s_gcol, 1)
            v.wait_ge(s_gturn, 1)
            v.tensor_copy(grow[:], bank[2][0:32, 0:P]).then_inc(s_grow, 1)
            v.wait_ge(s_x, 16)
            v.wait_ge(s_const, LUTN + 4)
            ln_vector(v, ln0, xn0, lambda b, t: x[:, b * TB + t, :], EPS)
            ln_modulate(v, ln0, tmp0, lambda b, c: modT[:, 0, CA + c, b:b + 1],
                        lambda b, c: modT[:, 0, SA + c, b:b + 1])
            for i, (src, c, hi, lo, sign) in enumerate(chunks):
                v.wait_ge(s_whi, i + 1)
                v.scalar_tensor_tensor(chunk_view(lo, c), stage_view(i, hi), sign * WS, chunk_view(hi, c),
                                       ALU.mult, ALU.subtract).then_inc(s_wlo, 1)

    if upto == 0:
        s_dbg = k.sem("dbg")
        with nc.Block() as block:
            @block.sync
            def _(sp):
                sp.dma_start(A["dbg16"].rearrange("p (a n) -> p a n", a=4)[:, 0:2, :], hT_hi[:]).then_inc(s_dbg, 16)
                sp.dma_start(A["dbg16"].rearrange("p (a n) -> p a n", a=4)[:, 2:4, :], hT_lo[:]).then_inc(s_dbg, 16)
                sp.dma_start(A["out"], x[:]).then_inc(s_dbg, 16)
                sp.dma_start(A["dbg"], gate[:]).then_inc(s_dbg, 16)
                sp.wait_ge(s_dbg, 64)
        return

    pr, sc, tr, oa = bank[0:2], bank[2:4], bank[4:6], bank[6:8]
    turned_bank = (tr[1], pr[1], tr[0])
    score_out = {3: sc[0][:, 0:512], 2: sc[1][:, 0:384], 0: sc[1][:, 384:512], 1: tr[1][:, 0:256]}
    st1 = layout(STAGE)
    bcol = st1("bcol", [P, 3 * H], F32)
    idx16 = st1("idx16", [P, IDXW], F16)
    onehot = st1("onehot", [P, 2, DCHUNK], F16)
    outb = st1("outb", [P, D], F32)
    gob = st1("gob", [P, B, D], F32)
    osum = st1("osum", [P, TB, D], F32)
    s_idx, s_lut, s_dec = (k.sem(n) for n in ("idx_in", "lut_in", "decoded"))
    s_rows, s_bcol, s_dist, s_gob = (k.sem(n) for n in ("outb_in", "bias_cols", "dist", "gate_bias"))
    (s_vmm, s_vhi, s_vlo, s_qmm, s_qhi, s_qlo, s_kmm, s_khi, s_klo) = (
        k.sem(n) for n in ("v_mm", "v_hi_done", "v_lo_done", "q_mm", "q_hi_done", "q_lo_done", "k_mm",
                           "k_hi_done", "k_lo_done"))
    (s_alibi, s_scored, s_masked, s_exp, s_inv, s_norm, s_turned, s_pthi, s_ptlo) = (
        k.sem(n) for n in ("alibi_ready", "scored", "masked", "exp_done", "sum_inverse", "normalised",
                           "prob_turned", "pt_hi_done", "pt_lo_done"))
    s_cmm, s_chi, s_clo, s_omm, s_oread, s_xadd = (
        k.sem(n) for n in ("ctx_mm", "ctx_hi_done", "ctx_lo_done", "out_mm", "out_read", "x_added"))

    def walk(step):
        def group(eng_n, b, g, r, kind):
            n = eng_n + r
            nxt_b, nxt_h = b, 4 * g + r + 1
            if r == 3 and kind in ("values", "last_loop"):
                nxt_b, nxt_h = (4 * b + g + 1) // 4, (4 * g + 4) % 16
            prev_h = 4 * g + r - 1
            values = None
            if kind == "values":
                values = (b + 1, g - 1)
            elif kind == "boundary":
                values = (b, 3)
                if r == 0:
                    prev_h = H - 1
            step(n, r % 2, nxt_b=nxt_b, nxt_h=nxt_h, prev_h=prev_h, values=values, tt=r,
                 boundary=(kind == "boundary" and r == 0), out_first=(kind == "boundary" and r == 1),
                 b=b, m=4 * b + g, no_values=(kind == "last_loop"))
        return group

    def run_steps(e, step):
        group = walk(step)
        for r in range(4):
            if r == 0:
                step(0, 0, nxt_b=0, nxt_h=1, prev_h=None, values=(0, 3), tt=0, boundary=False,
                     out_first=False, b=0, m=0, no_values=False)
            else:
                step(r, r % 2, nxt_b=0, nxt_h=r + 1, prev_h=r - 1, values=(0, 3), tt=r, boundary=False,
                     out_first=(r == 1), b=0, m=0, no_values=False)
        with e.Fori(0, B - 1) as b:
            with e.Fori(1, 4) as g:
                for r in range(4):
                    group(16 * b + 4 * g, b, g, r, "values")
            for r in range(4):
                group(16 * b + 16, b + 1, 0, r, "boundary")
        with e.Fori(1, 3) as g:
            for r in range(4):
                group(16 * (B - 1) + 4 * g, B - 1, g, r, "last_loop")
        for r in range(4):
            n = NSTEP - 4 + r
            step(n, r % 2, nxt_b=(B - 1 if r < 3 else None), nxt_h=13 + r, prev_h=11 + r, values=None, tt=r,
                 boundary=False, out_first=False, b=B - 1, m=LUTN - 1, no_values=True)
        step(NSTEP, 0, nxt_b=None, nxt_h=None, prev_h=H - 1, values=None, tt=0, boundary=True,
             out_first=False, b=B, m=None, no_values=True, last=True)

    def gate_pair():
        return gate[:].rearrange("p (b d) -> p b d", b=B)

    with nc.Block() as block:
        @block.sync
        def _(sp):
            sp.dma_start(outb[:], bass.AP(tensor=A["rows"].tensor, offset=R_OUTB * D, ap=[[0, P], [1, D]])
                         ).then_inc(s_rows, 16)
            sp.dma_start(idx32[:], A["idx"]).then_inc(s_idx, 16)
            sp.dma_start(lutb[:, 0, :], bass.AP(tensor=A["lut"].tensor, offset=0, ap=[[0, P], [1, LUTN]])
                         ).then_inc(s_lut, 16)
            sp.wait_ge(s_rows, 16)

        @block.gpsimd
        def _(g):
            g.iota(dist[:], pattern=[[-1, S]], base=S - P, channel_multiplier=1,
                   allow_small_or_imprecise_dtypes=True).then_inc(s_dist, 1)
            g.wait_ge(s_dist, 1)
            g.affine_select(out=dist[:], in_=dist[:], pattern=[[-1, S]], compare_op=ALU.is_ge, fill=MASKED,
                            base=S - P, channel_multiplier=1).then_inc(s_dist, 1)
            g.tensor_scalar(slopes[:], slopes[:], WS * WS, 1.0, ALU.mult, ALU.mult).then_inc(s_dist, 1)
            g.wait_ge(s_dist, 3)

            def alibi_of(head):
                g.tensor_tensor(alibi[:], dist[:], slopes[:, ds(head, 1)].broadcast_to([P, S]), ALU.mult
                                ).then_inc(s_alibi, 1)

            alibi_of(0)
            g.wait_ge(s_rows, 16)
            for b in range(B):
                g.tensor_tensor(gob[:, b, :], gate[:, b * D:(b + 1) * D], outb[:], ALU.mult).then_inc(s_gob, 1)
            g.wait_ge(s_idx, 16)
            g.tensor_copy(idx16[:], idx32[:]).then_inc(s_idx, 1)
            g.wait_ge(s_idx, 17)
            for w in (wdec_hi, wdec_lo):
                g.memset(w[:].bitcast(F32), 0.0).then_inc(s_idx, 1)

            def step(n, s, nxt_b, nxt_h, prev_h, boundary, b, last=False, **_):
                if not last:
                    wait_apart(g, s_inv, n + 1, s_passed)
                    for t in QTILES:
                        part = prob[:, SOFF[t]:SOFF[t] + (t + 1) * P]
                        g.tensor_scalar(part, part, sinv[:, t:t + 1], PS, ALU.mult, ALU.mult
                                        ).then_inc(s_norm, 1)
                if nxt_b is not None:
                    alibi_of(nxt_h)
                if boundary:
                    xb = x[:, ds(TB * (b - 1), TB), :]
                    for t in range(TB):
                        xt = x[:, TB * (b - 1) + t, :]
                        if t == 0:
                            g.wait_ge(s_gob, B)
                        g.tensor_tensor(xt, xt, gob[:, b - 1, :], ALU.add).then_inc(s_xadd, 1)
                    g.wait_ge(s_oread, 2 * b)
                    wait_apart(g, s_xadd, 5 * (b - 1) + TB, s_passed)
                    g.tensor_tensor(xb, xb, osum[:], ALU.add).then_inc(s_xadd, 1)
            run_steps(g, step)

        @block.scalar
        def _(act):
            act.preload_act_table(ACT.Exp)
            act.wait_ge(s_bcol, 3)
            def value_parts(tt, g, u):
                act.wait_ge(s_vmm, u + 1)
                return lambda bk: act.activation(v_hi[:, tt, ds(g * 512, 512)], bk[:, :], ACT.Copy
                                                 ).then_inc(s_vhi, 1)
            for tt in range(4):
                value_parts(tt, 0, tt)(pr[tt % 2])
            with act.Fori(1, 3) as g:
                for tt in range(4):
                    value_parts(tt, g, 4 * g + tt)(pr[tt % 2])

            def q_part(n1, head):
                act.wait_ge(s_qmm, n1 + 1)
                act.activation(q_hi[:], pr[1][:, :], ACT.Identity, bias=bcol[:, ds(head, 1)]).then_inc(s_qhi, 1)

            def k_part(n1, head):
                act.wait_ge(s_kmm, n1 + 1)
                act.activation(k_hi[:], pr[0][:, :], ACT.Identity, bias=bcol[:, ds(H + head, 1)]
                               ).then_inc(s_khi, 1)
            q_part(0, 0)
            k_part(0, 0)

            def step(n, s, nxt_b, nxt_h, prev_h, values, tt, last=False, **_):
                if not last:
                    for i, t in enumerate(QTILES):
                        act.wait_ge(s_masked, 4 * n + i + 1)
                        part = prob[:, SOFF[t]:SOFF[t] + (t + 1) * P]
                        act.activation(part, part, ACT.Exp, bias=smin[:, t:t + 1], scale=-1.0,
                                       accum_out=ssum[:, t:t + 1]).then_inc(s_exp, 1)
                if prev_h is not None:
                    act.wait_ge(s_cmm, n)
                    act.activation(ctx_hi[:], pr[0][:, :], ACT.Identity, bias=bcol[:, ds(2 * H + prev_h, 1)]
                                   ).then_inc(s_chi, 1)
                if nxt_b is not None:
                    q_part(n + 1, nxt_h)
                if values is not None:
                    value_parts(tt, values[1], n + 12)(tr[0])
                if nxt_b is not None:
                    k_part(n + 1, nxt_h)
                if not last:
                    for u, unit in enumerate(PT_UNITS):
                        act.wait_ge(s_turned, 3 * n + u + 1)
                        w = sum((4 - j) * P for j in unit)
                        act.activation(pt_hi[:, JOFF[unit[0]]:JOFF[unit[0]] + w], turned_bank[u][:, 0:w], ACT.Copy
                                       ).then_inc(s_pthi, 1)
            run_steps(act, step)

        @block.vector
        def _(v):
            v.tensor_scalar(bcol[:, 0:H], cols[:, C_QKVB:C_QKVB + H], -WS, None, ALU.mult).then_inc(s_bcol, 1)
            v.tensor_scalar(bcol[:, H:2 * H], cols[:, C_QKVB + H:C_QKVB + 2 * H], WS, None, ALU.mult
                            ).then_inc(s_bcol, 1)
            v.tensor_scalar(bcol[:, 2 * H:3 * H], cols[:, C_QKVB + 2 * H:C_QKVB + 3 * H], WS * PS, None,
                            ALU.mult).then_inc(s_bcol, 1)
            v.wait_ge(s_bcol, 3)

            def value_lo(tt, g, u, bk):
                v.wait_ge(s_vhi, u + 1)
                v.tensor_tensor(v_lo[:, tt, ds(g * 512, 512)], bk[:, :], v_hi[:, tt, ds(g * 512, 512)],
                                ALU.subtract).then_inc(s_vlo, 1)
            for tt in range(4):
                value_lo(tt, 0, tt, pr[tt % 2])
            with v.Fori(1, 3) as g:
                for tt in range(4):
                    value_lo(tt, g, 4 * g + tt, pr[tt % 2])

            def q_low(n1, head):
                v.wait_ge(s_qhi, n1 + 1)
                v.scalar_tensor_tensor(q_lo[:], pr[1][:, :], bcol[:, ds(head, 1)], q_hi[:], ALU.add,
                                       ALU.subtract).then_inc(s_qlo, 1)

            def k_low(n1, head):
                v.wait_ge(s_khi, n1 + 1)
                v.scalar_tensor_tensor(k_lo[:], pr[0][:, :], bcol[:, ds(H + head, 1)], k_hi[:], ALU.add,
                                       ALU.subtract).then_inc(s_klo, 1)
            q_low(0, 0)
            k_low(0, 0)
            v.wait_ge(s_lut, 16)
            v.tensor_scalar(lutb[:, 0, :], lutb[:, 0, :], WS, None, ALU.mult).then_inc(s_lut, 1)
            v.wait_ge(s_lut, 17)
            v.tensor_copy(lut16[:], lutb[:, 0, :]).then_inc(s_lut, 1)
            v.wait_ge(s_lut, 18)
            v.tensor_copy(lutb[:, 1, :], lut16[:]).then_inc(s_lut, 1)
            v.wait_ge(s_lut, 19)
            v.tensor_tensor(lutb[:, 2, :], lutb[:, 0, :], lutb[:, 1, :], ALU.subtract).then_inc(s_lut, 1)
            v.wait_ge(s_lut, 20)
            v.wait_ge(s_idx, 19)

            def decode_hot(n, m, r):
                if not (isinstance(n, int) and n == 0):
                    v.wait_ge(s_dec, 4 * n)
                for part in range(2):
                    v.tensor_scalar(onehot[:, part, :], idx16[:, r * DCHUNK:(r + 1) * DCHUNK],
                                    entry[:, ds(m, 1)], lutb[:, 1 + part, ds(m, 1)], ALU.is_equal, ALU.mult
                                    ).then_inc(s_dec, 1)

            def decode_add(n, part, r):
                w = (wdec_hi, wdec_lo)[part][:, r * DCHUNK:(r + 1) * DCHUNK]
                v.wait_ge(s_dec, 4 * n + 2)
                v.tensor_tensor(w, w, onehot[:, part, :], ALU.add).then_inc(s_dec, 1)


            def step(n, s, nxt_b, nxt_h, prev_h, values, tt, boundary, b, m, last=False, **_):
                if not last:
                    v.wait_ge(s_alibi, n + 1)
                    for i, t in enumerate(QTILES):
                        w = (t + 1) * P
                        wait_apart(v, s_scored, 4 * n + (1, 3, 3, 4)[i], s_passed)
                        v.tensor_tensor_reduce(prob[:, SOFF[t]:SOFF[t] + w], score_out[t], alibi[:, S - w:S],
                                               1.0 / (WS * WS), 3e38, ALU.add, ALU.min, smin[:, t:t + 1]
                                               ).then_inc(s_masked, 1)
                    decode_hot(n, m, tt)
                    v.wait_ge(s_exp, 4 * n + 4)
                    v.reciprocal(sinv[:], ssum[:]).then_inc(s_inv, 1)
                if prev_h is not None:
                    v.wait_ge(s_chi, n)
                    v.scalar_tensor_tensor(ctx_lo[:], pr[0][:, :], bcol[:, ds(2 * H + prev_h, 1)], ctx_hi[:],
                                           ALU.add, ALU.subtract).then_inc(s_clo, 1)
                if nxt_b is not None:
                    q_low(n + 1, nxt_h)
                if not last:
                    decode_add(n, 0, tt)
                if values is not None:
                    value_lo(tt, values[1], n + 12, tr[0])
                if not last:
                    decode_add(n, 1, tt)
                if nxt_b is not None:
                    k_low(n + 1, nxt_h)
                if not last:
                    for u, unit in enumerate(PT_UNITS):
                        v.wait_ge(s_pthi, 3 * n + u + 1)
                        w = sum((4 - j) * P for j in unit)
                        o = JOFF[unit[0]]
                        v.tensor_tensor(pt_lo[:, o:o + w], turned_bank[u][:, 0:w], pt_hi[:, o:o + w], ALU.subtract
                                        ).then_inc(s_ptlo, 1)
                if boundary:
                    v.wait_ge(s_omm, n)
                    for i in range(2):
                        v.wait_ge(s_xadd, 5 * b - 4)
                        v.scalar_tensor_tensor(osum[:, 2 * i:2 * i + 2, :],
                                               oa[i][:, :].rearrange("p (t d) -> p t d", t=2),
                                               1.0 / (WS * PS * WS),
                                               gate[:, ds((b - 1) * D, D)].unsqueeze(1).broadcast_to([P, 2, D]),
                                               ALU.mult, ALU.mult).then_inc(s_oread, 1)
            run_steps(v, step)

        @block.tensor
        def _(pe):
            def project(out, hi, lo, col, b):
                return split3(pe, out, [((hi[:, c, ds(col, P)], lo[:, c, ds(col, P)]),
                                         (hT_hi[:, c, ds(b * S, S)], hT_lo[:, c, ds(b * S, S)]))
                                        for c in range(KT)])

            def values_of(b, tt, g, bk):
                tok = b * S + tt * P
                return split3(pe, bk[:, :], [((hT_hi[:, c, ds(tok, P)], hT_lo[:, c, ds(tok, P)]),
                                              (wv_hi[:, c, ds(g * 512, 512)], wv_lo[:, c, ds(g * 512, 512)]))
                                             for c in range(KT)]).then_inc(s_vmm, 1)

            for tt in range(4):
                if tt >= 2:
                    pe.wait_ge(s_vlo, tt - 1)
                values_of(0, tt, 0, pr[tt % 2])
            with pe.Fori(1, 3) as g:
                for tt in range(4):
                    pe.wait_ge(s_vlo, 4 * g + tt - 1)
                    values_of(0, tt, g, pr[tt % 2])
            pe.wait_ge(s_vlo, 12)
            project(pr[1][:, :], wqk_hi, wqk_lo, 0, 0).then_inc(s_qmm, 1)
            project(pr[0][:, :], wqk_hi, wqk_lo, H * HD, 0).then_inc(s_kmm, 1)

            def step(n, s, nxt_b, nxt_h, prev_h, values, tt, boundary, out_first, b, no_values, last=False, **_):
                def score(t):
                    w = (t + 1) * P
                    split3(pe, score_out[t], [((q_hi[:, t * P:w], q_lo[:, t * P:w]), (k_hi[:, 0:w], k_lo[:, 0:w]))]
                           ).then_inc(s_scored, 1)

                def turn(u):
                    o = 0
                    for j in PT_UNITS[u]:
                        for t in range(j, TB):
                            ins = pe.transpose(turned_bank[u][:, o:o + P],
                                               prob[:, SOFF[t] + j * P:SOFF[t] + (j + 1) * P], ident[:, :])
                            o += P
                    ins.then_inc(s_turned, 1)

                if not last:
                    pe.wait_ge(s_qlo, n + 1)
                    pe.wait_ge(s_klo, n + 1)
                    if prev_h is not None:
                        pe.wait_ge(s_masked, 4 * n)
                    for t in QTILES:
                        if t == 1 and prev_h is not None:
                            pe.wait_ge(s_ptlo, 3 * n - 2)
                        score(t)
                if prev_h is not None:
                    pe.wait_ge(s_ptlo, 3 * n)
                    col = prev_h * HD
                    terms = []
                    for j in range(TB):
                        o, w = JOFF[j], (TB - j) * P
                        for vp, pp in ((v_hi, pt_hi), (v_hi, pt_lo), (v_lo, pt_hi)):
                            terms.append((j, vp[:, j, ds(col, HD)], pp[:, o:o + w]))
                    for i, (j, a, p_) in enumerate(terms):
                        ins = pe.matmul(pr[0][:, j * P:512], a, p_, start=(i == 0), stop=(i == len(terms) - 1))
                    ins.then_inc(s_cmm, 1)
                if nxt_b is not None:
                    project(pr[1][:, :], wqk_hi, wqk_lo, nxt_h * HD, nxt_b).then_inc(s_qmm, 1)
                if values is not None:
                    values_of(values[0], tt, values[1], tr[0])
                if prev_h is not None:
                    pe.wait_ge(s_clo, n)
                if nxt_b is not None:
                    project(pr[0][:, :], wqk_hi, wqk_lo, (nxt_h + H) * HD, nxt_b).then_inc(s_kmm, 1)
                if not last:
                    pe.wait_ge(s_norm, 4 * n + 4)
                    turn(0)
                    if nxt_b is not None:
                        pe.wait_ge(s_qlo, n + 2)
                    turn(1)
                    if values is not None:
                        pe.wait_ge(s_vlo, n + 13)
                    turn(2)
                if prev_h is not None:
                    if out_first and not isinstance(n, int):
                        pe.wait_ge(s_oread, 2 * b)
                    for t in range(TB):
                        for i, (ch, wh) in enumerate(((ctx_hi, wo_hi), (ctx_hi, wo_lo), (ctx_lo, wo_hi))):
                            ins = pe.matmul(oa[t // 2][:, (t % 2) * D:(t % 2 + 1) * D], ch[:, t * P:(t + 1) * P],
                                            wh[:, prev_h, :], start=(out_first and t % 2 == 0 and i == 0),
                                            stop=False, skip_group_check=True)
                    ins.then_inc(s_omm, 1)
            run_steps(pe, step)

    def dump_x():
        s_dbg = k.sem("dbg")
        with nc.Block() as block:
            @block.sync
            def _(sp):
                sp.dma_start(A["out"], x[:]).then_inc(s_dbg, 16)
                sp.wait_ge(s_dbg, 16)
    if upto == 1:
        dump_x()
        return

    b2 = layout(BIG)
    amph = b2("amph", [P, 2, KT, D], F32)
    amph_hi = b2("amph_hi", [P, 2, KT, D], F16)
    amph_lo = b2("amph_lo", [P, 2, KT, D], F16)
    ENT = b2.pos[0]
    entwT = b2("entwT", [P, LE, EC, D], F32)
    entpw = b2("entpw", [P, LE, EC, D], F32)
    path = b2("path", [P, LE, PWN, KT, D], F32)
    rows = b2("rows", [P, NROW, D], F32)
    wst = b2("wst", [P, KT, D], F32)
    wst_hi = b2("wst_hi", [P, 4, KT, D], F16)
    wst_lo = b2("wst_lo", [P, 4, KT, D], F16)
    gg = b2("gg", [P, B, D], F32)
    XN2 = b2.pos[0]
    xn = b2("xn2", [P, NT, D], F32)
    tmp = b2("tmp2", [P, KT, B * S], F32)
    sigm = layout(XN2)("sigm", [P, KT, B * S], F32)
    turnm = b2("turnm", [P, LE * PWN, D], F32)
    wk2 = layout(WORK)
    tanh = wk2("tanh", [P, KT, B * S], F32)
    wrow = wk2("wrow", [1, D], F32)
    brow_hi = wk2("brow_hi", [1, 4, D], F16)
    brow_lo = wk2("brow_lo", [1, 4, D], F16)
    assert b2.pos[0] <= DEC and wk2.pos[0] <= end, (b2.pos[0] - DEC, wk2.pos[0] - end)
    ln1 = LayerNormSems("ln1")
    (s_amph, s_rows2, s_path, s_ent, s_gate2) = (k.sem(n) for n in ("amph_in", "rows_in", "path_in", "ent_in",
                                                                   "gate2_in"))
    (s_ahi, s_alo, s_ph, s_mod2, s_wp, s_whi2, s_wlo2, s_wmm, s_brow, s_z, s_act2) = (
        k.sem(n) for n in ("amph_hi_done", "amph_lo_done", "phase_turns", "path_mod", "stage_w", "stage_w_hi",
                           "stage_w_lo", "ent_product", "bias_row", "z_psum", "z_act"))
    SQRT2 = 2.0 ** 0.5
    TWO_PI = 6.283185
    PI_ = 3.1415925
    ROUND = 12582912.0

    with nc.Block() as block:
        @block.sync
        def _(sp):
            sp.dma_start(amph[:], A["amph"]).then_inc(s_amph, 16)
            sp.dma_start(rows[:].rearrange("p r d -> p (r d)"),
                         bass.AP(tensor=A["rows"].tensor, offset=0, ap=[[0, P], [1, NROW * D]])
                         ).then_inc(s_rows2, 16)
            sp.dma_start(path[:], A["path"]).then_inc(s_path, 16)
            sp.dma_start(entwT[:], A["entwT"]).then_inc(s_ent, 16)
            sp.dma_start(entpw[:], A["entpw"]).then_inc(s_ent, 16)
            load_gate(sp, 0, 1, s_gate2)
            sp.wait_ge(s_gate2, 16)

        @block.gpsimd
        def _(g):
            ln_pow(g, ln1)
            parts_lo(g, ln1, tmp)

        @block.scalar
        def _(act):
            act.preload_act_table(ACT.Sigmoid)
            act.wait_ge(s_amph, 16)
            act.activation(amph_hi[:], amph[:], ACT.Copy, scale=WS).then_inc(s_ahi, 1)
            parts_hi(act, ln1, tmp)
            with act.Fori(0, B // 2) as b0:
                for sl in range(2):
                    b = 2 * b0 + sl
                    for w in range(2):
                        for f in range(KT):
                            act.wait_ge(s_z, 4 * b + 2 * w + f + 1)
                            dst = (sigm, tanh)[w]
                            bc = (C_AMPB, C_PHB)[w] + f
                            act.activation(dst[:, f, ds(b * S, S)], bank[4 * sl + 2 * w + f][:, :],
                                           (ACT.Sigmoid, ACT.Tanh)[w], bias=cols[:, bc:bc + 1], scale=1.0 / WS
                                           ).then_inc(s_act2, 1)
            act.preload_act_table(ACT.Sin)
            act.wait_ge(s_ph, 2)
            act.activation(turnm[:], turnm[:], ACT.Sin, scale=-TWO_PI).then_inc(s_ph, 1)
            for st in (1, 3, 0, 2):
                i = (1, 3, 0, 2).index(st)
                act.wait_ge(s_wp, i + 1)
                act.activation(wst_hi[:, st, :, :], wst[:], ACT.Copy, scale=WS).then_inc(s_whi2, 1)

        @block.tensor
        def _(pe):
            ln_turn(pe, ln1, xn)
            pe.wait_ge(s_alo, 1)
            with pe.Fori(0, B // 2) as b0:
                for sl in range(2):
                    b = 2 * b0 + sl
                    pe.wait_ge(ln1.lo, KT * b + KT)
                    for w in range(2):
                        for f in range(KT):
                            pe.wait_ge(s_act2, 4 * b + 2 * w + f + 1)
                            split3(pe, bank[4 * sl + 2 * w + f][:, :],
                                   [((amph_hi[:, w, c, f * P:(f + 1) * P], amph_lo[:, w, c, f * P:(f + 1) * P]),
                                     (hT_hi[:, c, ds(b * S, S)], hT_lo[:, c, ds(b * S, S)]))
                                    for c in range(KT)]).then_inc(s_z, 1)
            pe.wait_ge(s_ent, 32)
            pe.wait_ge(s_act2, 8 + 4 * B)
            for l in range(LE):
                for dt in range(KT):
                    for kc in range(EC):
                        ins = pe.matmul(bank[4 * l + dt][:, 0:D], entwT[:, l, kc, dt * P:(dt + 1) * P],
                                        entpw[:, l, kc, :], start=(kc == 0), stop=(kc == EC - 1))
                for kc in range(EC):
                    ins = pe.matmul(bank[4 * l + 2][0:1, 0:D], cols[:, C_ENTB + l * EC + kc:C_ENTB + l * EC + kc + 1],
                                    entpw[:, l, kc, :], start=(kc == 0), stop=(kc == EC - 1))
                ins.then_inc(s_wmm, 1)

        @block.vector
        def _(v):
            ln_vector(v, ln1, xn, lambda b, t: x[:, b * TB + t, :], EPS)
            v.wait_ge(s_ahi, 1)
            v.scalar_tensor_tensor(amph_lo[:].rearrange("p a k d -> p (a k d)"),
                                   amph[:].rearrange("p a k d -> p (a k d)"), WS,
                                   amph_hi[:].rearrange("p a k d -> p (a k d)"),
                                   ALU.mult, ALU.subtract).then_inc(s_alo, 1)
            ln_modulate(v, ln1, tmp, lambda b, c: modT[:, 0, CB + c, b:b + 1],
                        lambda b, c: modT[:, 0, SB + c, b:b + 1])
            v.wait_ge(ln1.tmp, KT * B)
            v.sem_inc(s_act2, 8)
            v.wait_ge(s_rows2, 16)
            ph = rows[:, R_PHASE:R_PHASE + 4, :]
            v.tensor_scalar(ph, ph, 1.0 / 6.283185307179586, 0.125, ALU.mult, ALU.add).then_inc(s_mod2, 1)
            v.wait_ge(s_mod2, 1)
            v.tensor_scalar(turnm[:], ph, ROUND, None, ALU.add).then_inc(s_ph, 1)
            v.wait_ge(s_ph, 1)
            v.scalar_tensor_tensor(turnm[:].rearrange("p a d -> p (a d)"), turnm[:].rearrange("p a d -> p (a d)"),
                                   -ROUND, ph.rearrange("p a d -> p (a d)"), ALU.add, ALU.subtract
                                   ).then_inc(s_ph, 1)
            v.wait_ge(s_ph, 3)
            v.wait_ge(s_path, 16)
            n = 1
            for l in range(LE):
                for p_ in range(PWN):
                    m = turnm[:, l * PWN + p_, :]
                    pw = path[:, l, p_, :, :]
                    for c in range(KT):
                        v.scalar_tensor_tensor(pw[:, c, :], m, SQRT2, pw[:, c, :], ALU.mult, ALU.mult
                                               ).then_inc(s_mod2, 1)
                    pb = rows[0:1, R_PATHB + l * PWN + p_, :]
                    v.scalar_tensor_tensor(pb, turnm[0:1, l * PWN + p_, :], SQRT2, pb, ALU.mult, ALU.mult
                                           ).then_inc(s_mod2, 1)
                    n += 3
            v.wait_ge(s_mod2, n)

            def finish(i, st):
                v.wait_ge(s_whi2, i + 1)
                v.scalar_tensor_tensor(wst_lo[:, st, :, :].rearrange("p k d -> p (k d)"),
                                       wst[:].rearrange("p k d -> p (k d)"), WS,
                                       wst_hi[:, st, :, :].rearrange("p k d -> p (k d)"), ALU.mult, ALU.subtract
                                       ).then_inc(s_wlo2, 1)
                v.tensor_scalar(brow_hi[:, st, :], wrow[:], WS, None, ALU.mult).then_inc(s_brow, 1)
                v.wait_ge(s_brow, 3 * i + 2)
                v.scalar_tensor_tensor(brow_lo[:, st, :], wrow[:], WS, brow_hi[:, st, :], ALU.mult, ALU.subtract
                                       ).then_inc(s_brow, 1)
                v.wait_ge(s_brow, 3 * i + 3)
                v.wait_ge(s_wlo2, i + 1)

            def add_identity(c, n2):
                v.wait_ge(s_mod2, n2)
                return v.tensor_tensor(wst[:, c, c * P:(c + 1) * P], wst[:, c, c * P:(c + 1) * P], ident[:],
                                       ALU.add)
            for i, st in enumerate((1, 3, 0, 2)):
                l = st // 2
                if st % 2:
                    v.tensor_tensor(wst[:], path[:, l, 0, :, :], path[:, l, 1, :, :], ALU.add).then_inc(s_mod2, 1)
                    v.tensor_tensor(wrow[:], rows[0:1, R_PATHB + 2 * l, :], rows[0:1, R_PATHB + 2 * l + 1, :],
                                    ALU.add).then_inc(s_brow, 1)
                    n += 1
                else:
                    v.wait_ge(s_wmm, l + 1)
                    for c in range(KT):
                        v.tensor_copy(wst[:, c, :], bank[4 * l + c][:, 0:D]).then_inc(s_mod2, 1)
                    n += 2
                    v.tensor_tensor(wrow[:], bank[4 * l + 2][0:1, 0:D], rows[0:1, R_ENTPB + l, :], ALU.add
                                    ).then_inc(s_brow, 1)
                v.wait_ge(s_brow, 3 * i + 1)
                add_identity(0, n).then_inc(s_mod2, 1)
                n += 1
                add_identity(1, n).then_inc(s_wp, 1)
                finish(i, st)

    mmb = (bank[0:2], bank[2:4])
    trb = (bank[4:6], bank[6:8])
    xnq = [layout(ENT + i * TB * D * 4)(f"xnq{i}", [P, TB, D], F32) for i in range(2)]
    s_xb2 = k.sem("x_stage_added")
    (s_wrap, s_sin, s_gg, s_xb, s_h, s_hhi, s_hlo, s_mm, s_st, s_ag, s_ve, s_rs, s_xn, s_tn) = (
        k.sem(n) for n in ("wrapped", "sine", "gate_ln4", "x_bias", "h_new", "h_hi", "h_lo", "stage_mm",
                           "stage_stats", "stage_aggr", "stage_vareps", "stage_rstd", "stage_xn",
                           "stage_turned"))
    g4, b4 = rows[:, R_LN4G, :], rows[:, R_LN4B, :]

    with nc.Block() as block:
        @block.gpsimd
        def _(g):
            for b in range(B):
                g.tensor_tensor(gg[:, b, :], gate[:, b * D:(b + 1) * D], g4, ALU.mult).then_inc(s_gg, 1)
            g.wait_ge(s_gg, B)
            for b in range(B):
                gb_ = gate[:, b * D:(b + 1) * D]
                g.tensor_tensor(gb_, gb_, b4, ALU.mult).then_inc(s_gg, 1)
            g.wait_ge(s_gg, 2 * B)

            def h_lo_part(cnt, b):
                for c in range(KT):
                    g.wait_ge(s_hhi, cnt + c + 1)
                    g.tensor_tensor(hT_lo[:, c, ds(b * S, S)], tmp[:, c, ds(b * S, S)],
                                    hT_hi[:, c, ds(b * S, S)], ALU.subtract).then_inc(s_hlo, 1)
            with g.Fori(0, B) as b:
                h_lo_part(KT * b, b)
            with g.Fori(0, B) as b:
                xb = x[:, ds(b * TB, TB), :]
                for t in range(TB):
                    xt = x[:, b * TB + t, :]
                    g.tensor_tensor(xt, xt, gate[:, ds(b * D, D)], ALU.add).then_inc(s_xb, 1)
            for st in range(4):
                with g.Fori(0, B // 2) as b0:
                    for sl in range(2):
                        b = 2 * b0 + sl
                        g.wait_ge(s_ve, B * st + b + 1)
                        g.tensor_tensor(rstd[:, ds(b * TB, TB)], vareps[:, ds(b * TB, TB)],
                                        mhalf[:, ds(b * TB, TB)], ALU.pow).then_inc(s_rs, 1)
                    if st < 3:
                        for sl in range(2):
                            h_lo_part(KT * (B * (st + 1) + 2 * b0 + sl), 2 * b0 + sl)

        @block.scalar
        def _(act):
            act.preload_act_table(ACT.Sin)
            with act.Fori(0, B) as b:
                act.wait_ge(s_wrap, 2 * b + 2)
                act.activation(tanh[:, :, ds(b * S, S)], tanh[:, :, ds(b * S, S)], ACT.Sin, scale=PI_
                               ).then_inc(s_sin, 1)
                for c in range(KT):
                    act.wait_ge(s_h, KT * b + c + 1)
                    act.activation(hT_hi[:, c, ds(b * S, S)], tmp[:, c, ds(b * S, S)], ACT.Copy
                                   ).then_inc(s_hhi, 1)
            for st in range(3):
                with act.Fori(0, B) as b:
                    for c in range(KT):
                        act.wait_ge(s_h, KT * (B * (st + 1) + b) + c + 1)
                        act.activation(hT_hi[:, c, ds(b * S, S)], tmp[:, c, ds(b * S, S)], ACT.Copy
                                       ).then_inc(s_hhi, 1)

        @block.vector
        def _(v):
            v.sem_inc(s_xn, 2 * TB)
            with v.Fori(0, B) as b:
                th = tanh[:, :, ds(b * S, S)]
                v.tensor_scalar(tmp[:, :, ds(b * S, S)], th, 0.75, -2.0, ALU.is_gt, ALU.mult).then_inc(s_wrap, 1)
                v.wait_ge(s_wrap, 2 * b + 1)
                v.scalar_tensor_tensor(th, tmp[:, :, ds(b * S, S)], 0.25, th, ALU.add, ALU.add
                                       ).then_inc(s_wrap, 1)
            with v.Fori(0, B) as b:
                v.wait_ge(s_sin, b + 1)
                for c in range(KT):
                    v.scalar_tensor_tensor(tmp[:, c, ds(b * S, S)], tanh[:, c, ds(b * S, S)], SQRT2,
                                           sigm[:, c, ds(b * S, S)], ALU.mult, ALU.mult).then_inc(s_h, 1)
            for st in range(4):
                l = st // 2
                with v.Fori(0, B // 2) as b0:
                    for sl in range(2):
                        b = 2 * b0 + sl
                        for t in range(TB):
                            v.wait_ge(s_mm, TB * (B * st + b) + 2 * (t // 2) + 2)
                            v.bn_stats(stats[:, b * TB + t, :], mmb[sl][t // 2][:, (t % 2) * D:(t % 2 + 1) * D]
                                       ).then_inc(s_st, 1)
                        v.wait_ge(s_st, TB * (B * st + b) + TB)
                        combine_stats(v, s_ag, b, 5 * (B * st + b), EPS * WS * WS).then_inc(s_ve, 1)
                    for sl in range(2):
                        b = 2 * b0 + sl
                        v.wait_ge(s_rs, B * st + b + 1)
                        if st < 3:
                            v.wait_ge(s_tn, KT * (B * st + b) + KT)
                        for t in range(TB):
                            src = mmb[sl][t // 2][:, (t % 2) * D:(t % 2 + 1) * D]
                            mu, r = mean[:, ds(b * TB + t, 1)], rstd[:, ds(b * TB + t, 1)]
                            if st < 3:
                                v.tensor_scalar(xnq[sl][:, t, :], src, mu, r, ALU.subtract, ALU.mult
                                                ).then_inc(s_xn, 1)
                            else:
                                v.scalar_tensor_tensor(xnq[sl][:, t, :], src, mu, gg[:, b, :],
                                                       ALU.subtract, ALU.mult).then_inc(s_xn, 1)
                    if st < 3:
                        for sl in range(2):
                            b = 2 * b0 + sl
                            for c in range(KT):
                                gcol_ = C_LN + (2 * (st % 2)) * LE * KT + l * KT + c
                                bcol_ = gcol_ + LE * KT
                                v.wait_ge(s_tn, 2 * KT + KT * (B * st + b) + c + 1)
                                v.tensor_scalar(tmp[:, c, ds(b * S, S)], trb[sl][c][:, :],
                                                cols[:, gcol_:gcol_ + 1], cols[:, bcol_:bcol_ + 1],
                                                ALU.mult, ALU.add).then_inc(s_h, 1)
                    else:
                        for sl in range(2):
                            b = 2 * b0 + sl
                            for t in range(TB):
                                xt = x[:, b * TB + t, :]
                                v.wait_ge(s_xn, 2 * TB + TB * (B * st + b) + t + 1)
                                v.wait_ge(s_xb, TB * b + t + 1)
                                v.scalar_tensor_tensor(xt, xnq[sl][:, t, :], rstd[:, ds(b * TB + t, 1)], xt,
                                                       ALU.mult, ALU.add).then_inc(s_xb2, 1)

        @block.tensor
        def _(pe):
            pe.sem_inc(s_tn, 2 * KT)
            for st in range(4):
                with pe.Fori(0, B // 2) as b0:
                    for sl in range(2):
                        b = 2 * b0 + sl
                        pe.wait_ge(s_hlo, KT * (B * st + b) + KT)
                        for t in range(TB):
                            if t % 2 == 0:
                                pe.wait_ge(s_xn, TB * (B * st + b) + t + 2)
                            tok = b * S + t * P
                            out = mmb[sl][t // 2][:, (t % 2) * D:(t % 2 + 1) * D]
                            terms = []
                            for c in range(KT):
                                hh, hl = hT_hi[:, c, ds(tok, P)], hT_lo[:, c, ds(tok, P)]
                                wh, wl = wst_hi[:, st, c, :], wst_lo[:, st, c, :]
                                terms += [(hh, wh), (hh, wl), (hl, wh)]
                            terms += [(ones16[:, :], brow_hi[:, st, :]), (ones16[:, :], brow_lo[:, st, :])]
                            for i, (a, w) in enumerate(terms):
                                ins = pe.matmul(out, a, w, start=(i == 0), stop=(i == len(terms) - 1))
                            ins.then_inc(s_mm, 1)
                    if st < 3:
                        for sl in range(2):
                            b = 2 * b0 + sl
                            pe.wait_ge(s_xn, 2 * TB + TB * (B * st + b) + TB)
                            for c in range(KT):
                                pe.wait_ge(s_h, KT * (B * (st + 1) + b - 2) + c + 1)
                                for t in range(TB):
                                    ins = pe.transpose(trb[sl][c][:, t * P:(t + 1) * P],
                                                       xnq[sl][:, t, c * P:(c + 1) * P], ident[:, :])
                                ins.then_inc(s_tn, 1)

    if upto == 2:
        dump_x()
        return

    b3 = layout(BIG)
    P3 = b3.pos[0]
    wo1 = b3("wo1", [P, KT, D], F32)
    wo1_hi = b3("wo1_hi", [P, KT, D], F16)
    wo1_lo = b3("wo1_lo", [P, KT, D], F16)
    qk1_hi = b3("qk1_hi", [P, 2 * KT, B * S], F16)
    qk1_lo = b3("qk1_lo", [P, 2 * KT, B * S], F16)
    v1_hi = b3("v1_hi", [P, NT, D], F16)
    v1_lo = b3("v1_lo", [P, NT, D], F16)
    bcol1 = b3("bcol1", [P, 3 * KT], F32)
    boutb = b3("boutb", [P, D], F32)
    T3 = b3.pos[0]
    xn3 = b3("xn3", [P, NT, D], F32)
    tmp3 = b3("tmp3", [P, KT, B * S], F32)
    assert b3.pos[0] <= end, b3.pos[0] - end
    w3a = layout(b3.pos[0])
    wq1 = w3a("wq1", [P, KT, 3 * D], F32)
    wq1_hi = w3a("wq1_hi", [P, KT, 3 * D], F16)
    wq1_lo = w3a("wq1_lo", [P, KT, 3 * D], F16)
    assert w3a.pos[0] <= end, w3a.pos[0] - end
    t3 = layout(T3)
    prob1 = t3("prob1", [P, TB, S], F32)
    pt1_hi = t3("pt1_hi", [P, TB, S], F16)
    pt1_lo = t3("pt1_lo", [P, TB, S], F16)
    ctx1_hi = t3("ctx1_hi", [P, KT, S], F16)
    ctx1_lo = t3("ctx1_lo", [P, KT, S], F16)
    osum1 = t3("osum1", [P, TB, D], F32)
    gbo = t3("gbo", [P, B, D], F32)
    assert t3.pos[0] <= w3a.pos[0]
    t3c = layout(t3.pos[0])
    smin1 = t3c("smin1", [P, TB], F32)
    sminb = t3c("sminb", [P, TB], F32)
    ssum1 = t3c("ssum1", [P, TB], F32)
    sinv1 = t3c("sinv1", [P, TB], F32)
    assert t3c.pos[0] <= end, t3c.pos[0] - end
    lnc = LayerNormSems("ln2")
    (s_wq1, s_bout, s_gate3, s_whi3, s_wlo3, s_bc3, s_pmm, s_phi, s_plo) = (
        k.sem(n) for n in ("wq1_in", "bout_in", "gate3_in", "w1_hi", "w1_lo", "bias1_cols",
                           "proj1_mm", "proj1_hi", "proj1_lo"))

    with nc.Block() as block:
        @block.sync
        def _(sp):
            sp.dma_start(wq1[:], A["wqkv1"]).then_inc(s_wq1, 16)
            sp.dma_start(wo1[:], A["wout1"]).then_inc(s_wq1, 16)
            sp.dma_start(boutb[:], bass.AP(tensor=A["rows"].tensor, offset=R_BOUT * D, ap=[[0, P], [1, D]])
                         ).then_inc(s_bout, 16)
            load_gate(sp, 1, 0, s_gate3)
            sp.wait_ge(s_gate3, 16)
            sp.wait_ge(s_bout, 16)

        @block.gpsimd
        def _(g):
            ln_pow(g, lnc)
            parts_lo(g, lnc, tmp3)

        @block.scalar
        def _(act):
            act.preload_act_table(ACT.Exp)
            act.wait_ge(s_wq1, 32)
            act.activation(wq1_hi[:, :, 0:D], wq1[:, :, 0:D], ACT.Copy, scale=-WS).then_inc(s_whi3, 1)
            act.activation(wq1_hi[:, :, D:3 * D], wq1[:, :, D:3 * D], ACT.Copy, scale=WS).then_inc(s_whi3, 1)
            act.activation(wo1_hi[:], wo1[:], ACT.Copy, scale=WS).then_inc(s_whi3, 1)
            parts_hi(act, lnc, tmp3)
            act.wait_ge(s_bc3, 3)
            with act.Fori(0, B) as b:
                for i in range(2 * KT):
                    act.wait_ge(s_pmm, 6 * b + i + 1)
                    act.activation(qk1_hi[:, i, ds(b * S, S)], bank[i][:, :], ACT.Identity,
                                   bias=bcol1[:, i:i + 1]).then_inc(s_phi, 1)
                for i in range(2):
                    act.wait_ge(s_pmm, 6 * b + 4 + i + 1)
                    act.activation(v1_hi[:, ds(b * TB + 2 * i, 2), :], bank[4 + i][:, :].rearrange(
                        "p (t d) -> p t d", t=2), ACT.Copy).then_inc(s_phi, 1)

        @block.vector
        def _(v):
            ln_vector(v, lnc, xn3, lambda b, t: x[:, b * TB + t, :], EPS)
            for i, (o, w, sg) in enumerate(((0, D, -WS), (D, 2 * D, WS))):
                v.wait_ge(s_whi3, i + 1)
                v.scalar_tensor_tensor(wq1_lo[:, :, o:o + w], wq1[:, :, o:o + w], sg, wq1_hi[:, :, o:o + w],
                                       ALU.mult, ALU.subtract).then_inc(s_wlo3, 1)
            v.wait_ge(s_whi3, 3)
            v.scalar_tensor_tensor(wo1_lo[:], wo1[:], WS, wo1_hi[:], ALU.mult, ALU.subtract).then_inc(s_wlo3, 1)
            for i, sc_ in enumerate((-WS, WS, WS * PS)):
                v.tensor_scalar(bcol1[:, KT * i:KT * i + KT], cols[:, C_B1 + KT * i:C_B1 + KT * i + KT], sc_, None,
                                ALU.mult).then_inc(s_bc3, 1)
            v.wait_ge(s_bc3, 3)
            ln_modulate(v, lnc, tmp3, lambda b, c: modT[:, 1, CA + c, b:b + 1],
                        lambda b, c: modT[:, 1, SA + c, b:b + 1])
            v.wait_ge(lnc.tmp, KT * B)
            v.sem_inc(s_plo, 6)
            with v.Fori(0, B) as b:
                for i in range(2 * KT):
                    v.wait_ge(s_phi, 6 * b + i + 1)
                    v.scalar_tensor_tensor(qk1_lo[:, i, ds(b * S, S)], bank[i][:, :], bcol1[:, i:i + 1],
                                           qk1_hi[:, i, ds(b * S, S)], ALU.add, ALU.subtract).then_inc(s_plo, 1)
                for i in range(2):
                    v.wait_ge(s_phi, 6 * b + 4 + i + 1)
                    v.tensor_tensor(v1_lo[:, ds(b * TB + 2 * i, 2), :], bank[4 + i][:, :].rearrange(
                        "p (t d) -> p t d", t=2), v1_hi[:, ds(b * TB + 2 * i, 2), :], ALU.subtract
                        ).then_inc(s_plo, 1)

        @block.tensor
        def _(pe):
            ln_turn(pe, lnc, xn3)
            pe.wait_ge(s_wlo3, 2)
            with pe.Fori(0, B) as b:
                pe.wait_ge(lnc.lo, KT * b + KT)
                for i in range(2 * KT):
                    pe.wait_ge(s_plo, 6 * b + i + 1)
                    split3(pe, bank[i][:, :], [((wq1_hi[:, c, i * P:(i + 1) * P], wq1_lo[:, c, i * P:(i + 1) * P]),
                                                (hT_hi[:, c, ds(b * S, S)], hT_lo[:, c, ds(b * S, S)]))
                                               for c in range(KT)]).then_inc(s_pmm, 1)
                for i in range(2):
                    pe.wait_ge(s_plo, 6 * b + 4 + i + 1)
                    for t in (2 * i, 2 * i + 1):
                        tok = b * S + t * P
                        ins = split3(pe, bank[4 + i][:, (t % 2) * D:(t % 2 + 1) * D],
                                     [((hT_hi[:, c, ds(tok, P)], hT_lo[:, c, ds(tok, P)]),
                                       (wq1_hi[:, c, 2 * D:3 * D], wq1_lo[:, c, 2 * D:3 * D])) for c in range(KT)])
                    ins.then_inc(s_pmm, 1)

    (s_sc1, s_mn1, s_mb1, s_ex1, s_iv1, s_nm1, s_tn1, s_th1, s_tl1, s_cm1, s_ch1, s_cl1, s_om1, s_or1, s_xa1,
     s_gb1) = (
        k.sem(n) for n in ("scored1", "min1", "min1_scaled", "exp1", "inverse1", "normalised1", "turned1",
                           "pt1_hi_done", "pt1_lo_done", "ctx1_mm", "ctx1_hi_done", "ctx1_lo_done", "out1_mm",
                           "out1_read", "x1_added", "gate_bout"))
    SCALE1 = 1.0 / (WS * WS * D ** 0.5)
    TRB = (4, 5, 0, 1)

    def run1(e, step):
        step(0, first=True, last=False)
        with e.Fori(1, B) as i:
            step(i, first=False, last=False)
        step(B, first=False, last=True)

    with nc.Block() as block:
        @block.gpsimd
        def _(g):
            for b in range(B):
                g.tensor_tensor(gbo[:, b, :], gate[:, b * D:(b + 1) * D], boutb[:], ALU.mult).then_inc(s_gb1, 1)
            g.wait_ge(s_gb1, B)

            def step(i, first, last):
                if not last:
                    wait_apart(g, s_iv1, i + 1, s_passed)
                    for t in range(TB):
                        g.tensor_scalar(prob1[:, t, :], prob1[:, t, :], sinv1[:, t:t + 1], PS, ALU.mult, ALU.mult
                                        ).then_inc(s_nm1, 1)
                if not first:
                    for t in range(TB):
                        xt = x[:, TB * (i - 1) + t, :]
                        g.tensor_tensor(xt, xt, gbo[:, i - 1, :], ALU.add).then_inc(s_xa1, 1)
                    g.wait_ge(s_xa1, 5 * i - 1)
                    wait_apart(g, s_or1, 2 * i + 2, s_passed)
                    xb = x[:, ds(TB * (i - 1), TB), :]
                    g.tensor_tensor(xb, xb, osum1[:], ALU.add).then_inc(s_xa1, 1)
            run1(g, step)

        @block.scalar
        def _(act):
            act.preload_act_table(ACT.Exp)

            def step(i, first, last):
                if not last:
                    for t in range(TB):
                        act.wait_ge(s_mb1, TB * i + t + 1)
                        act.activation(prob1[:, t, :], bank[t][:, :], ACT.Exp, bias=sminb[:, t:t + 1],
                                       scale=-SCALE1, accum_out=ssum1[:, t:t + 1]).then_inc(s_ex1, 1)
                if not first:
                    for c in range(KT):
                        act.wait_ge(s_cm1, KT * (i - 1) + c + 1)
                        act.activation(ctx1_hi[:, c, :], bank[6 + c][:, :], ACT.Identity,
                                       bias=bcol1[:, 2 * KT + c:2 * KT + c + 1]).then_inc(s_ch1, 1)
                if not last:
                    for j in range(TB):
                        act.wait_ge(s_tn1, TB * i + j + 1)
                        act.activation(pt1_hi[:, j, :], bank[TRB[j]][:, :], ACT.Copy).then_inc(s_th1, 1)
            run1(act, step)

        @block.vector
        def _(v):
            v.sem_inc(s_or1, 2)
            def step(i, first, last):
                if not last:
                    for t in range(TB):
                        v.wait_ge(s_sc1, TB * i + t + 1)
                        v.tensor_reduce(smin1[:, t:t + 1], bank[t][:, :], AX.X, ALU.min).then_inc(s_mn1, 1)
                        v.wait_ge(s_mn1, TB * i + t + 1)
                        v.tensor_scalar(sminb[:, t:t + 1], smin1[:, t:t + 1], SCALE1, None, ALU.mult
                                        ).then_inc(s_mb1, 1)
                    v.wait_ge(s_ex1, TB * i + TB)
                    v.reciprocal(sinv1[:], ssum1[:]).then_inc(s_iv1, 1)
                if not first:
                    for c in range(KT):
                        v.wait_ge(s_ch1, KT * (i - 1) + c + 1)
                        v.scalar_tensor_tensor(ctx1_lo[:, c, :], bank[6 + c][:, :],
                                               bcol1[:, 2 * KT + c:2 * KT + c + 1], ctx1_hi[:, c, :], ALU.add,
                                               ALU.subtract).then_inc(s_cl1, 1)
                    for q in range(2):
                        v.wait_ge(s_om1, 2 * (i - 1) + q + 1)
                        v.wait_ge(s_xa1, 5 * i - 1)
                        v.scalar_tensor_tensor(osum1[:, 2 * q:2 * q + 2, :],
                                               bank[2 + q][:, :].rearrange("p (t d) -> p t d", t=2),
                                               1.0 / (WS * PS * WS),
                                               gate[:, ds((i - 1) * D, D)].unsqueeze(1).broadcast_to([P, 2, D]),
                                               ALU.mult, ALU.mult).then_inc(s_or1, 1)
                if not last:
                    for j in range(TB):
                        v.wait_ge(s_th1, TB * i + j + 1)
                        v.tensor_tensor(pt1_lo[:, j, :], bank[TRB[j]][:, :], pt1_hi[:, j, :], ALU.subtract
                                        ).then_inc(s_tl1, 1)
            run1(v, step)

        @block.tensor
        def _(pe):
            def step(i, first, last):
                if not last:
                    for t in range(TB):
                        if not first and t < 2:
                            pe.wait_ge(s_tl1, TB * (i - 1) + 3 + t)
                        elif not first:
                            pe.wait_ge(s_or1, 2 * i)
                        split3(pe, bank[t][:, :],
                               [((qk1_hi[:, c, ds(i * S + t * P, P)], qk1_lo[:, c, ds(i * S + t * P, P)]),
                                 (qk1_hi[:, KT + c, ds(i * S, S)], qk1_lo[:, KT + c, ds(i * S, S)]))
                                for c in range(KT)]).then_inc(s_sc1, 1)
                if not first:
                    pe.wait_ge(s_tl1, TB * i)
                    for c in range(KT):
                        split3(pe, bank[6 + c][:, :],
                               [((v1_hi[:, (i - 1) * TB + j, c * P:(c + 1) * P],
                                  v1_lo[:, (i - 1) * TB + j, c * P:(c + 1) * P]),
                                 (pt1_hi[:, j, :], pt1_lo[:, j, :])) for j in range(TB)]).then_inc(s_cm1, 1)
                    pe.wait_ge(s_cl1, KT * i)
                    if not last:
                        pe.wait_ge(s_ex1, TB * i + TB)
                    for q in range(2):
                        for t in (2 * q, 2 * q + 1):
                            ins = split3(pe, bank[2 + q][:, (t % 2) * D:(t % 2 + 1) * D],
                                         [((ctx1_hi[:, c, t * P:(t + 1) * P], ctx1_lo[:, c, t * P:(t + 1) * P]),
                                           (wo1_hi[:, c, :], wo1_lo[:, c, :])) for c in range(KT)])
                        ins.then_inc(s_om1, 1)
                if not last:
                    pe.wait_ge(s_nm1, TB * i + TB)
                    for j in range(TB):
                        for t in range(TB):
                            ins = pe.transpose(bank[TRB[j]][:, t * P:(t + 1) * P],
                                               prob1[:, t, j * P:(j + 1) * P], ident[:, :])
                        ins.then_inc(s_tn1, 1)
            run1(pe, step)

    if upto == 3:
        dump_x()
        return

    b4_ = layout(P3)
    mT_hi = b4_("mT_hi", [P, IC, B * S], F16)
    mT_lo = b4_("mT_lo", [P, IC, B * S], F16)
    X4 = b4_.pos[0]
    xn4 = b4_("xn4", [P, NT, D], F32)
    tmp4 = b4_("tmp4", [P, KT, B * S], F32)
    silu = [b4_(f"silu{i}", [P, S], F32) for i in range(2)]
    prod = [b4_(f"prod{i}", [P, S], F32) for i in range(2)]
    osum4 = b4_("osum4", [P, TB, D], F32)
    assert b4_.pos[0] <= end, b4_.pos[0] - end
    ln3 = LayerNormSems("ln3")
    (s_gate4, s_gmm, s_umm, s_silu, s_prod, s_mhi, s_mlo, s_dmm, s_dread, s_xout, s_stored) = (
        k.sem(n) for n in ("gate4_in", "gate_mm", "up_mm", "silu_done", "product", "m_hi", "m_lo", "down_mm",
                           "down_read", "x_final", "stored"))
    GW = KT * INTER

    def dec(w, which, c, o):
        if which < 2:
            a = which * GW + c * INTER + o * P
            return w[:, a:a + (P if o < IC - 1 else LASTI)]
        return w[0:(P if c < IC - 1 else LASTI), 2 * GW + c * D:2 * GW + (c + 1) * D]

    with nc.Block() as block:
        @block.sync
        def _(sp):
            load_gate(sp, 1, 1, s_gate4)
            with sp.Fori(0, B) as b:
                sp.wait_ge(s_xout, b + 2)
                sp.dma_start(A["out"][:, ds(b * TB, TB), :], x[:, ds(b * TB, TB), :]).then_inc(s_stored, 16)
            sp.wait_ge(s_stored, 16 * B)

        @block.gpsimd
        def _(g):
            ln_pow(g, ln3)
            parts_lo(g, ln3, tmp4)
            g.sem_inc(s_mlo, 2)
            with g.Fori(0, B) as b:
                for oc in range(IC):
                    w = P if oc < IC - 1 else LASTI
                    g.wait_ge(s_mhi, IC * b + oc + 1)
                    g.tensor_tensor(mT_lo[0:w, oc, ds(b * S, S)], prod[oc % 2][0:w, :],
                                    mT_hi[0:w, oc, ds(b * S, S)], ALU.subtract).then_inc(s_mlo, 1)

        @block.scalar
        def _(act):
            act.preload_act_table(ACT.Silu)
            parts_hi(act, ln3, tmp4)

            def silu_of(b, oc):
                w = P if oc < IC - 1 else LASTI
                act.wait_ge(s_gmm, IC * b + oc + 1)
                act.wait_ge(s_prod, IC * b + oc + 1)
                act.activation(silu[oc % 2][0:w, :], bank[oc % 2][0:w, :], ACT.Silu, scale=1.0 / WS
                               ).then_inc(s_silu, 1)

            def hi_of(b, oc):
                w = P if oc < IC - 1 else LASTI
                act.wait_ge(s_prod, 2 + IC * b + oc + 1)
                act.activation(mT_hi[0:w, oc, ds(b * S, S)], prod[oc % 2][0:w, :], ACT.Copy).then_inc(s_mhi, 1)
            with act.Fori(0, B) as b:
                silu_of(b, 0)
                for oc in range(1, IC):
                    silu_of(b, oc)
                    hi_of(b, oc - 1)
                hi_of(b, IC - 1)

        @block.vector
        def _(v):
            ln_vector(v, ln3, xn4, lambda b, t: x[:, b * TB + t, :], EPS)
            ln_modulate(v, ln3, tmp4, lambda b, c: modT[:, 1, CB + c, b:b + 1],
                        lambda b, c: modT[:, 1, SB + c, b:b + 1])
            v.wait_ge(ln3.tmp, KT * B)
            v.sem_inc(s_prod, 2)
            v.sem_inc(s_dread, 2)
            v.sem_inc(s_xout, 1)
            v.wait_ge(s_gate4, 16)

            def products(b):
                for oc in range(IC):
                    w = P if oc < IC - 1 else LASTI
                    v.wait_ge(s_umm, IC * b + oc + 1)
                    v.wait_ge(s_silu, IC * b + oc + 1)
                    v.wait_ge(s_mlo, IC * b + oc + 1)
                    v.scalar_tensor_tensor(prod[oc % 2][0:w, :], bank[2 + oc % 2][0:w, :], 1.0 / WS,
                                           silu[oc % 2][0:w, :], ALU.mult, ALU.mult).then_inc(s_prod, 1)

            def down_out(b):
                v.wait_ge(s_xout, b + 1)
                for q in range(2):
                    v.wait_ge(s_dmm, 2 * b + q + 1)
                    v.scalar_tensor_tensor(osum4[:, 2 * q:2 * q + 2, :],
                                           bank[4 + q][:, :].rearrange("p (t d) -> p t d", t=2), 1.0 / WS,
                                           gate[:, ds(b * D, D)].unsqueeze(1).broadcast_to([P, 2, D]),
                                           ALU.mult, ALU.mult).then_inc(s_dread, 1)
                v.wait_ge(s_dread, 2 + 2 * b + 2)
                xb = x[:, ds(b * TB, TB), :]
                v.tensor_tensor(xb, xb, osum4[:], ALU.add).then_inc(s_xout, 1)
            products(0)
            with v.Fori(1, B) as b:
                products(b)
                down_out(b - 1)
            down_out(B - 1)

        @block.tensor
        def _(pe):
            ln_turn(pe, ln3, xn4)

            def gate_up(b):
                pe.wait_ge(ln3.lo, KT * b + KT)
                for oc in range(IC):
                    w = P if oc < IC - 1 else LASTI
                    wait_apart(pe, s_prod, IC * b + oc + 1, s_passed)
                    for which, sem in ((0, s_gmm), (1, s_umm)):
                        split3(pe, bank[2 * which + oc % 2][0:w, :],
                               [((dec(wdec_hi, which, c, oc), dec(wdec_lo, which, c, oc)),
                                 (hT_hi[:, c, ds(b * S, S)], hT_lo[:, c, ds(b * S, S)])) for c in range(KT)]
                               ).then_inc(sem, 1)

            def down(b):
                pe.wait_ge(s_mlo, 2 + IC * b + IC)
                for q in range(2):
                    pe.wait_ge(s_dread, 2 * b + q + 1)
                    for t in (2 * q, 2 * q + 1):
                        pairs = []
                        for oc in range(IC):
                            w = P if oc < IC - 1 else LASTI
                            tok = b * S + t * P
                            pairs.append(((mT_hi[0:w, oc, ds(tok, P)], mT_lo[0:w, oc, ds(tok, P)]),
                                          (dec(wdec_hi, 2, oc, 0), dec(wdec_lo, 2, oc, 0))))
                        ins = split3(pe, bank[4 + q][:, (t % 2) * D:(t % 2 + 1) * D], pairs)
                    ins.then_inc(s_dmm, 1)
            gate_up(0)
            with pe.Fori(1, B) as b:
                gate_up(b)
                down(b - 1)
            down(B - 1)


def host_layout(inputs):
    import numpy as np
    n = {key: np.asarray(v) for key, v in inputs.items()}

    def feat(w):
        return np.ascontiguousarray(w.reshape(-1, P, w.shape[-1]).transpose(1, 0, 2))

    def col(v):
        return v.reshape(-1, P).T

    a = {}
    a["x"] = np.ascontiguousarray(n["L0_attn_x"].reshape(NT, P, D).transpose(1, 0, 2))
    a["cT"] = np.ascontiguousarray(np.stack([n["L0_c"].T, n["L1_c"].T]).reshape(2, KT, P, B)
                                   .transpose(2, 0, 1, 3).reshape(P, -1))
    a["wmod"] = np.ascontiguousarray(np.stack([n["L0_wmod"], n["L1_wmod"]]).reshape(2, KT, P, 6 * D)
                                     .transpose(2, 0, 1, 3))
    qkv = n["L0_attn_qkv_w"]
    a["wqk"] = feat(qkv[:, :QKW])
    a["wv"] = feat(qkv[:, QKW:])
    a["wo"] = feat(n["L0_attn_out_w"])
    a["cols"] = np.ascontiguousarray(np.concatenate(
        [col(n["L0_attn_qkv_b"]), col(n["L0_ffn_amp_b"]), col(n["L0_ffn_ph_b"])]
        + [col(n[f"L0_ffn_{g}"].reshape(-1)) for g in ("ln3_g", "ln3_b", "ln4_g", "ln4_b")]
        + [col(n["L1_attn_b_qkv"]), col(n["L0_ffn_ent_b"].reshape(-1))], axis=1))
    a["slopes"] = np.tile(np.array([1.0 / 2.0 ** (i / 2.0) for i in range(H)], np.float32), (P, 1))
    a["rows"] = np.ascontiguousarray(np.concatenate(
        [n["L0_attn_out_b"], n["L0_ffn_ent_pb"].reshape(-1), n["L0_ffn_path_b"].reshape(-1),
         n["L0_ffn_phase"].reshape(-1), n["L0_ffn_ln4_g"][-1], n["L0_ffn_ln4_b"][-1], n["L1_attn_b_out"]])
        .reshape(1, -1))
    a["amph"] = np.ascontiguousarray(np.stack([feat(n["L0_ffn_amp_w"]), feat(n["L0_ffn_ph_w"])], axis=1))
    a["entwT"] = np.ascontiguousarray(np.stack([feat(w.T) for w in n["L0_ffn_ent_w"]], axis=1))
    a["entpw"] = np.ascontiguousarray(np.stack([feat(w) for w in n["L0_ffn_ent_pw"]], axis=1))
    a["path"] = np.ascontiguousarray(np.stack([np.stack([feat(w) for w in l], axis=1)
                                               for l in n["L0_ffn_path_w"]], axis=1))
    a["wqkv1"] = feat(n["L1_attn_w_qkv"].T)
    a["wout1"] = feat(n["L1_attn_w_out"].T)
    down = np.zeros((IC * P, D), np.int32)
    down[:INTER] = n["L1_ffn_down_idx"].T
    a["idx"] = np.ascontiguousarray(np.concatenate(
        [feat(n["L1_ffn_gate_idx"].T).reshape(P, -1), feat(n["L1_ffn_up_idx"].T).reshape(P, -1),
         feat(down).reshape(P, -1)], axis=1))
    a["lut"] = np.ascontiguousarray(n["L1_ffn_lut"].reshape(1, -1))
    return a


def kernel(**inputs):
    import concourse.bacc as bacc
    from concourse.bass_utils import run_bass_kernel_spmd

    nc = bacc.Bacc("TRN2", target_bir_lowering=False, num_devices=1)
    arrays = {f"in_{name}": a for name, a in host_layout(inputs).items()}
    aps = {name[3:]: nc.dram_tensor(name, a.shape, mybir.dt.from_np(a.dtype), kind="ExternalInput").ap()
           for name, a in arrays.items()}
    aps["out"] = nc.dram_tensor("out", (P, NT, D), F32, kind="ExternalOutput").ap()
    build(nc, aps)
    r = run_bass_kernel_spmd(nc, [arrays], core_ids=[0])
    y = r.results[0]["out"]
    return y.reshape(P, NT, D).transpose(1, 0, 2).reshape(B, S, D)
```

```python
import concourse.bass as bass
from concourse import mybir

F32 = mybir.dt.float32
F16 = mybir.dt.float16
I32 = mybir.dt.int32
ALU = mybir.AluOpType
ACT = mybir.ActivationFunctionType
AX = mybir.AxisListType
ds = bass.ds

P = 128
B, S, D = 4, 512, 256
KT = D // P
TB = S // P
NT = B * TB
H = 16
HD = 128
QKW, VW = 2 * H * HD, H * HD
LE, PWN, EW = 2, 2, 1024
EC = EW // P
INTER = 688
IC = -(-INTER // P)
LASTI = INTER - (IC - 1) * P
LUTN = 16
IDXW = 2 * KT * INTER + IC * D
EPS = 1e-5
WS = 16.0
PS = 16.0
MASKED = 1e30
VALUE_UNITS = B * H
NSTEP = B * H
CHUNK = 1024
C_QKVB = 0
C_AMPB = C_QKVB + 3 * H
C_PHB = C_AMPB + KT
C_LN = C_PHB + KT
C_B1 = C_LN + 4 * LE * KT
C_ENTB = C_B1 + 3 * KT
NCOL = C_ENTB + LE * EC
R_OUTB, R_ENTPB, R_PATHB, R_PHASE, R_LN4G, R_LN4B, R_BOUT = 0, 1, 3, 7, 11, 12, 13
NROW = 14
DCHUNK = IDXW // 4
QTILES = (3, 2, 0, 1)
SOFF = {3: 0, 2: 512, 0: 896, 1: 1024}
SW = 1280
JOFF = {0: 0, 1: 512, 2: 896, 3: 1152}
PT_UNITS = ((1,), (2, 3), (0,))


class Kit:

    def __init__(self, nc):
        self.nc = nc
        self.n = 0

    def sem(self, name):
        self.n += 1
        return self.nc.alloc_semaphore(name)

    def sb(self, name, shape, dt):
        return self.nc.alloc_sbuf_tensor(name, shape, dt)

    def at(self, name, shape, dt, offset):
        return self.nc.alloc_sbuf_tensor_at(name, shape, dt, offset=offset)


def wait_apart(e, sem, value, passed):
    e.wait_ge(sem, value)
    if not isinstance(value, int):
        e.sem_inc(passed, 1)


def split3(pe, out, pairs, **kw):
    terms = []
    for (ah, al), (bh, bl) in pairs:
        terms += [(ah, bh), (ah, bl), (al, bh)]
    for i, (a, b) in enumerate(terms):
        ins = pe.matmul(out, a, b, start=(i == 0), stop=(i == len(terms) - 1), **kw)
    return ins


def build(nc, A, upto=9):
    k = Kit(nc)
    base = nc.sbuf_base + 31 & ~31
    slab = nc.alloc_sbuf_tensor("slab", [P, (nc.sbuf_usable_end - base) // 4 - 24], F32)
    base = base
    cur = [base]

    def place(name, shape, dt, at=None):
        n = 1
        for d in shape[1:]:
            n *= d
        n *= 2 if dt == F16 else 4
        if at is None:
            at = cur[0]
            cur[0] = (at + n + 31) & ~31
        assert at + n <= nc.sbuf_usable_end, (name, at + n)
        t = k.at(name, shape, dt, at)
        return t, at, at + ((n + 31) & ~31)

    def new(name, shape, dt):
        return place(name, shape, dt)[0]

    def region(nbytes):
        at = cur[0]
        cur[0] = (at + nbytes + 31) & ~31
        return at

    x = new("x", [P, NT, D], F32)
    hT_hi = new("hT_hi", [P, KT, B * S], F16)
    hT_lo = new("hT_lo", [P, KT, B * S], F16)
    cols = new("cols", [P, NCOL], F32)
    modT = new("modT", [P, 2, 12, B], F32)
    ident = new("ident", [P, P], F32)
    ones16 = new("ones16", [1, P], F16)
    mhalf = new("mhalf", [P, NT], F32)
    stats = new("stats", [P, NT, 6], F32)
    mean = new("mean", [P, NT], F32)
    half_var = new("half_var", [P, 4, NT], F32)
    vareps = new("vareps", [P, NT], F32)
    rstd = new("rstd", [P, NT], F32)
    gate = new("gate", [P, B * D], F32)
    slopes = new("slopes", [P, H], F32)
    entry = new("entry", [P, LUTN], F32)
    lutb = new("lutb", [P, 3, LUTN], F32)
    lut16 = new("lut16", [P, LUTN], F16)

    BIG = region(128 * 1024)
    DEC = region(2 * IDXW * 2)
    WORK = region(21 * 1024)
    end = cur[0]
    assert end <= nc.sbuf_usable_end, end - nc.sbuf_usable_end

    def layout(start):
        p = [start]

        def f(name, shape, dt):
            t, _, p[0] = place(name, shape, dt, p[0])
            return t
        f.pos = p
        return f

    big0 = layout(BIG)
    wqk_hi = big0("wqk_hi", [P, KT, QKW], F16)
    wqk_lo = big0("wqk_lo", [P, KT, QKW], F16)
    wv_hi = big0("wv_hi", [P, KT, VW], F16)
    wv_lo = big0("wv_lo", [P, KT, VW], F16)
    wo_hi = big0("wo_hi", [P, H, D], F16)
    wo_lo = big0("wo_lo", [P, H, D], F16)
    v_hi = big0("v_hi", [P, TB, VW], F16)
    v_lo = big0("v_lo", [P, TB, VW], F16)
    STAGE = big0.pos[0]
    stg = layout(STAGE)
    NSTAGE = 3
    stage = [stg(f"stage{i}", [P, KT * CHUNK], F32) for i in range(NSTAGE)]
    xq0 = [stg(f"xq0_{i}", [P, TB, D], F32) for i in range(2)]

    decoded = layout(DEC)
    wdec_hi = decoded("wdec_hi", [P, IDXW], F16)
    wdec_lo = decoded("wdec_lo", [P, IDXW], F16)
    idx32 = layout(DEC)("idx32", [P, IDXW], I32)
    wk0 = layout(WORK)
    q_hi = wk0("q_hi", [P, S], F16)
    q_lo = wk0("q_lo", [P, S], F16)
    k_hi = wk0("k_hi", [P, S], F16)
    k_lo = wk0("k_lo", [P, S], F16)
    prob = wk0("prob", [P, SW], F32)
    pt_hi = wk0("pt_hi", [P, SW], F16)
    pt_lo = wk0("pt_lo", [P, SW], F16)
    ctx_hi = wk0("ctx_hi", [P, S], F16)
    ctx_lo = wk0("ctx_lo", [P, S], F16)
    alibi = wk0("alibi", [P, S], F32)
    dist = wk0("dist", [P, S], F32)
    smin = wk0("smin", [P, TB], F32)
    ssum = wk0("ssum", [P, TB], F32)
    sinv = wk0("sinv", [P, TB], F32)
    nbias = wk0("nbias", [P, 3 * H], F32)
    assert wk0.pos[0] <= end, wk0.pos[0] - end
    wkm = layout(WORK)
    wmod = wkm("wmod", [P, KT, 6 * D], F32)
    cT = wkm("cT", [P, 2 * KT * B], F32)
    sil = wkm("sil", [P, 2 * KT * B], F32)
    sig = wkm("sig", [P, 2 * KT * B], F32)
    gcol = wkm("gcol", [P, 2 * 2 * B * KT], F32)
    gsgn = wkm("gsgn", [P, 2 * 2 * B * KT], F32)
    grow = wkm("grow", [2 * 2 * B * KT, P], F32)
    tq0 = [wkm(f"tq0_{i}", [P, KT, S], F32) for i in range(2)]
    assert wkm.pos[0] <= end, wkm.pos[0] - end
    bank = [nc.alloc_psum_tensor(f"bank{i}", [P, 512], F32) for i in range(8)]
    gate_rows = nc.dram_tensor("gate_rows", [2 * 2 * B * KT, P], F32, kind="Internal").ap()

    SA, CA, GA, SB, CB, GB = (KT * i for i in range(6))

    s_passed = k.sem("waits_passed")

    def load_gate(sp, layer, which, sem):
        r0 = (layer * 2 + which) * B * KT
        src = gate_rows[r0:r0 + B * KT, :].rearrange("r d -> (r d)")
        return sp.dma_start(gate[:], bass.AP(tensor=src.tensor, offset=src.offset, ap=[[0, P], [1, B * D]])
                            ).then_inc(sem, 16)

    class LayerNorm:

        def __init__(self, tag, xq, tq, banks, layer, scale, shift):
            self.xq, self.tq, self.banks = xq, tq, banks
            self.layer, self.scale, self.shift = layer, scale, shift
            self.stats, self.vareps, self.rstd, self.xn, self.turned, self.tmp, self.hi, self.lo = (
                k.sem(f"{tag}_{n}") for n in ("stats", "vareps", "rstd", "xn", "turned", "modulated", "hi", "lo"))

        def free_slots(self, v):
            v.sem_inc(self.turned, 2 * KT)
            v.sem_inc(self.tmp, KT)
            v.sem_inc(self.lo, 2 * KT)

        def vector(self, v, b0):
            self.normalise(v, b0)
            self.modulate(v, b0)

        def normalise(self, v, b0):
            for sl in range(2):
                b = 2 * b0 + sl
                for t in range(TB):
                    v.bn_stats(stats[:, b * TB + t, :], x[:, b * TB + t, :]).then_inc(self.stats, 1)
                v.wait_ge(self.stats, (TB + 5) * b + TB)
                combine_stats(v, self.stats, b, (TB + 5) * b + TB, EPS).then_inc(self.vareps, 1)
            for sl in range(2):
                b = 2 * b0 + sl
                v.wait_ge(self.rstd, b + 1)
                v.wait_ge(self.turned, KT * b + KT)
                for t in range(TB):
                    v.tensor_scalar(self.xq[sl][:, t, :], x[:, b * TB + t, :], mean[:, ds(b * TB + t, 1)],
                                    rstd[:, ds(b * TB + t, 1)], ALU.subtract, ALU.mult).then_inc(self.xn, 1)

        def modulate(self, v, b0):
            for sl in range(2):
                b = 2 * b0 + sl
                for c in range(KT):
                    v.wait_ge(self.turned, 2 * KT + KT * b + c + 1)
                    v.wait_ge(self.lo, KT * b + c + 1)
                    v.tensor_scalar(self.tq[sl][:, c, :], self.banks[c][:, :],
                                    modT[:, self.layer, self.scale + c, ds(b, 1)],
                                    modT[:, self.layer, self.shift + c, ds(b, 1)], ALU.mult, ALU.add
                                    ).then_inc(self.tmp, 1)

        def gpsimd(self, g, b0):
            self.inverse(g, b0)
            self.split_lo(g, b0)

        def inverse(self, g, b0):
            for sl in range(2):
                b = 2 * b0 + sl
                g.wait_ge(self.vareps, b + 1)
                g.tensor_tensor(rstd[:, ds(b * TB, TB)], vareps[:, ds(b * TB, TB)], mhalf[:, ds(b * TB, TB)],
                                ALU.pow).then_inc(self.rstd, 1)

        def split_lo(self, g, b0):
            for sl in range(2):
                b = 2 * b0 + sl
                for c in range(KT):
                    g.wait_ge(self.hi, KT * b + c + 1)
                    g.tensor_tensor(hT_lo[:, c, ds(b * S, S)], self.tq[sl][:, c, :],
                                    hT_hi[:, c, ds(b * S, S)], ALU.subtract).then_inc(self.lo, 1)

        def scalar(self, act, b0):
            for sl in range(2):
                b = 2 * b0 + sl
                for c in range(KT):
                    act.wait_ge(self.tmp, KT + KT * b + c + 1)
                    act.activation(hT_hi[:, c, ds(b * S, S)], self.tq[sl][:, c, :], ACT.Copy).then_inc(self.hi, 1)

        def tensor(self, pe, b0):
            for sl in range(2):
                b = 2 * b0 + sl
                for c in range(KT):
                    pe.wait_ge(self.tmp, KT * b + c + 1)
                    for t in range(TB):
                        if c == 0:
                            pe.wait_ge(self.xn, b * TB + t + 1)
                        ins = pe.transpose(self.banks[c][:, t * P:(t + 1) * P],
                                           self.xq[sl][:, t, c * P:(c + 1) * P], ident[:, :])
                    ins.then_inc(self.turned, 1)

        def wait_parts(self, pe, b):
            pe.wait_ge(self.lo, 2 * KT + KT * b + KT)

    def combine_stats(v, sem, b, done, eps, negative=None):
        tiles = ds(b * TB, TB)
        even_mean, even_m2 = stats[:, tiles, 1], stats[:, tiles, 2]
        odd_mean, odd_m2 = stats[:, tiles, 4], stats[:, tiles, 5]
        dif, tot, m2, dd = (half_var[:, i, tiles] for i in range(4))
        v.tensor_tensor(dif, even_mean, odd_mean, ALU.subtract).then_inc(sem, 1)
        v.tensor_tensor(tot, even_mean, odd_mean, ALU.add).then_inc(sem, 1)
        v.scalar_tensor_tensor(m2, even_m2, D * eps, odd_m2, ALU.add, ALU.add).then_inc(sem, 1)
        v.wait_ge(sem, done + 2)
        out, half = (mean, 0.5) if negative is None else (negative, -0.5)
        v.tensor_scalar(out[:, tiles], tot, half, None, ALU.mult).then_inc(sem, 1)
        v.scalar_tensor_tensor(dd, dif, 0.25, dif, ALU.mult, ALU.mult).then_inc(sem, 1)
        v.wait_ge(sem, done + 5)
        return v.scalar_tensor_tensor(vareps[:, tiles], m2, 1.0 / D, dd, ALU.mult, ALU.add)

    s_x, s_cols, s_c, s_wmod = (k.sem(n) for n in ("x_in", "cols_in", "c_in", "wmod_in"))
    s_slp = k.sem("slopes_in")
    s_stage = [k.sem(f"stage_in{i}") for i in range(NSTAGE)]
    s_whi, s_wlo = k.sem("w_hi"), k.sem("w_lo")
    s_idx, s_lut = k.sem("idx_in"), k.sem("lut_in")
    s_const, s_sig, s_sil, s_modp, s_mod, s_gcol, s_gturn, s_grow, s_gout = (
        k.sem(n) for n in ("consts", "sigmoid", "silu", "mod_psum", "mod_done", "gate_cols", "gate_turned",
                           "gate_row", "gate_out"))
    s_vmm, s_vhi, s_vlo = (k.sem(n) for n in ("v_mm", "v_hi_done", "v_lo_done"))
    ln0 = LayerNorm("ln0", xq0, tq0, bank[2:4], 0, CA, SA)
    chunks = [(A["wv"], c, wv_hi, wv_lo, 1.0) for c in range(0, VW, CHUNK)]
    chunks += [(A["wqk"], c, wqk_hi, wqk_lo, -1.0 if c < H * HD else 1.0) for c in range(0, QKW, CHUNK)]
    chunks += [(A["wo"], c, wo_hi, wo_lo, 1.0) for c in range(0, H, H // 2)]

    MOD_GROUPS = ((0, (0, 1, 2, 3)), (0, tuple(range(4, 12))), (1, (4, 5, 10, 11)), (1, (0, 1, 2, 3, 6, 7, 8, 9)))

    def chunk_view(t, c):
        if t is wo_hi or t is wo_lo:
            return t[:, c:c + H // 2, :]
        return t[:, :, c:c + CHUNK]

    def stage_view(i, t):
        if t is wo_hi or t is wo_lo:
            return stage[i % NSTAGE][:, :].rearrange("p (h n) -> p h n", h=H // 2)
        return stage[i % NSTAGE][:, :].rearrange("p (k n) -> p k n", k=KT)

    with nc.Block() as block:
        @block.sync
        def _(sp):
            sp.dma_start(cT[:], A["cT"]).then_inc(s_c, 16)
            sp.dma_start(x[:], A["x"]).then_inc(s_x, 16)
            sp.dma_start(wmod[:], A["wmod"][:, 0]).then_inc(s_wmod, 16)
            for i, (src, c, hi, lo, sign) in enumerate(chunks):
                if i >= NSTAGE:
                    sp.wait_ge(s_wlo, i - NSTAGE + 1)
                view = src[:, c:c + H // 2, :] if hi is wo_hi else src[:, :, c:c + CHUNK]
                sp.dma_start(stage_view(i, hi), view).then_inc(s_stage[i % NSTAGE], 16)
                if i == NSTAGE + 1:
                    sp.wait_ge(s_modp, 2)
                    sp.dma_start(wmod[:], A["wmod"][:, 1]).then_inc(s_wmod, 16)
            sp.dma_start(cols[:], A["cols"]).then_inc(s_cols, 16)
            sp.dma_start(slopes[:], A["slopes"]).then_inc(s_slp, 16)
            sp.wait_ge(s_grow, 1)
            sp.dma_start(gate_rows, grow[:]).then_inc(s_gout, 16)
            sp.dma_start(idx32[:], A["idx"]).then_inc(s_idx, 16)
            sp.dma_start(lutb[:, 0, :], bass.AP(tensor=A["lut"].tensor, offset=0, ap=[[0, P], [1, LUTN]])
                         ).then_inc(s_lut, 16)
            sp.wait_ge(s_gout, 16)
            load_gate(sp, 0, 0, s_gout)
            sp.wait_ge(s_gout, 32)
            sp.wait_ge(s_slp, 16)
            sp.wait_ge(s_cols, 16)

        @block.gpsimd
        def _(g):
            g.memset(ident[:], 0.0).then_inc(s_const, 1)
            for i in range(LUTN):
                g.memset(entry[:, i:i + 1], float(i)).then_inc(s_const, 1)
            g.memset(ones16[:], 1.0).then_inc(s_const, 1)
            g.memset(mhalf[:], -0.5).then_inc(s_const, 1)
            g.wait_ge(s_const, LUTN + 3)
            g.affine_select(out=ident[:], in_=ident[:], pattern=[[-1, P]], compare_op=ALU.not_equal, fill=1.0,
                            base=0, channel_multiplier=1).then_inc(s_const, 1)
            for b0 in range(B // 2):
                ln0.gpsimd(g, b0)

        def chunk_parts(e, i):
            src, c, hi, lo, sign = chunks[i]
            if e is nc.scalar:
                e.wait_ge(s_stage[i % NSTAGE], 16 * (i // NSTAGE + 1))
                e.activation(chunk_view(hi, c), stage_view(i, hi), ACT.Copy, scale=sign * WS).then_inc(s_whi, 1)
            else:
                e.wait_ge(s_whi, i + 1)
                e.scalar_tensor_tensor(chunk_view(lo, c), stage_view(i, hi), sign * WS, chunk_view(hi, c),
                                       ALU.mult, ALU.subtract).then_inc(s_wlo, 1)
        VCH = 2
        first_values = [(u // TB, u % TB) for u in range(3 * TB)]

        @block.scalar
        def _(act):
            act.preload_act_table(ACT.Exp)
            act.wait_ge(s_c, 16)
            act.activation(sig[:], cT[:], ACT.Exp, scale=-1.0).then_inc(s_sig, 1)
            chunk_parts(act, 0)
            chunk_parts(act, 1)
            ln0.scalar(act, 0)
            chunk_parts(act, 2)
            ln0.scalar(act, 1)
            for i in range(VCH, len(chunks)):
                if i > 2:
                    chunk_parts(act, i)
                for u in (2 * (i - VCH), 2 * (i - VCH) + 1):
                    g, tt = first_values[u]
                    act.wait_ge(s_vmm, u + 1)
                    act.activation(v_hi[:, tt, g * 512:(g + 1) * 512], bank[u % 2][:, :], ACT.Copy
                                   ).then_inc(s_vhi, 1)

        @block.tensor
        def _(pe):
            def modulation(i):
                layer, tiles = MOD_GROUPS[i]
                pe.wait_ge(s_wmod, 16 * (layer + 1))
                for j in tiles:
                    for c in range(KT):
                        ins = pe.matmul(bank[4 + i][:, j * B:(j + 1) * B], wmod[:, c, j * P:(j + 1) * P],
                                        sil[:, (layer * KT + c) * B:(layer * KT + c + 1) * B],
                                        start=(c == 0), stop=(c == KT - 1))
                ins.then_inc(s_modp, 1)
            pe.wait_ge(s_sil, 1)
            modulation(0)
            pe.wait_ge(s_const, LUTN + 4)
            ln0.tensor(pe, 0)
            modulation(1)
            ln0.tensor(pe, 1)
            ln0.wait_parts(pe, 0)
            for u, (g, tt) in enumerate(first_values):
                if u == 4:
                    modulation(2)
                if u == 6:
                    pe.wait_ge(s_gcol, 1)
                    pe.transpose(bank[4][0:32, 0:P], gcol[:, :], ident[:, :]).then_inc(s_gturn, 1)
                pe.wait_ge(s_wlo, 1 + g // 2)
                if u >= 2:
                    pe.wait_ge(s_vlo, u - 1)
                split3(pe, bank[u % 2][:, :],
                       [((hT_hi[:, c, tt * P:(tt + 1) * P], hT_lo[:, c, tt * P:(tt + 1) * P]),
                         (wv_hi[:, c, g * 512:(g + 1) * 512], wv_lo[:, c, g * 512:(g + 1) * 512]))
                        for c in range(KT)]).then_inc(s_vmm, 1)
            modulation(3)

        @block.vector
        def _(v):
            v.wait_ge(s_sig, 1)
            v.tensor_scalar(sig[:], sig[:], 1.0, None, ALU.add).then_inc(s_sig, 1)
            v.wait_ge(s_sig, 2)
            v.reciprocal(sig[:], sig[:]).then_inc(s_sig, 1)
            v.wait_ge(s_sig, 3)
            v.tensor_tensor(sil[:], sig[:], cT[:], ALU.mult).then_inc(s_sil, 1)

            def modulation(i, done):
                layer, tiles = MOD_GROUPS[i]
                v.wait_ge(s_modp, i + 1)
                for j in tiles[::2]:
                    v.tensor_copy(modT[:, layer, j:j + 2, :].rearrange("p j b -> p (j b)"),
                                  bank[4 + i][:, j * B:(j + 2) * B]).then_inc(s_mod, 1)
                    done += 1
                for j in (CA, CB):
                    if j in tiles:
                        v.wait_ge(s_mod, done)
                        v.tensor_scalar(modT[:, layer, j:j + KT, :], modT[:, layer, j:j + KT, :], 1.0, None,
                                        ALU.add).then_inc(s_mod, 1)
                        done += 1
                v.wait_ge(s_mod, done)
                return done
            v.wait_ge(s_x, 16)
            v.wait_ge(s_const, LUTN + 4)
            ln0.free_slots(v)
            ln0.normalise(v, 0)
            chunk_parts(v, 0)
            done = modulation(0, 0)
            ln0.modulate(v, 0)
            chunk_parts(v, 1)
            ln0.normalise(v, 1)
            ln0.modulate(v, 1)
            done = modulation(1, done)

            def gates(done):
                for layer in range(2):
                    for n, j in enumerate((GA, GB)):
                        o = (layer * 2 + n) * B * KT
                        v.tensor_copy(gcol[:, o:o + B * KT].rearrange("p (b c) -> p b c", b=B),
                                      modT[:, layer, j:j + KT, :].rearrange("p c b -> p b c")).then_inc(s_mod, 1)
                done += 4
                v.wait_ge(s_mod, done)
                v.tensor_scalar(gsgn[:], gcol[:], 0.0, 2.0, ALU.is_ge, ALU.mult).then_inc(s_mod, 1)
                v.wait_ge(s_mod, done + 1)
                v.scalar_tensor_tensor(gcol[:], gsgn[:], -1.0, gcol[:], ALU.add, ALU.mult).then_inc(s_mod, 1)
                v.wait_ge(s_mod, done + 2)
                v.tensor_scalar(gcol[:], gcol[:], 0.25, None, ALU.max).then_inc(s_mod, 1)
                v.wait_ge(s_mod, done + 3)
                v.scalar_tensor_tensor(gcol[:], gsgn[:], -1.0, gcol[:], ALU.add, ALU.mult).then_inc(s_gcol, 1)
                return done + 3
            for i in range(VCH, len(chunks)):
                chunk_parts(v, i)
                for u in (2 * (i - VCH), 2 * (i - VCH) + 1):
                    g, tt = first_values[u]
                    v.wait_ge(s_vhi, u + 1)
                    v.tensor_tensor(v_lo[:, tt, g * 512:(g + 1) * 512], bank[u % 2][:, :],
                                    v_hi[:, tt, g * 512:(g + 1) * 512], ALU.subtract).then_inc(s_vlo, 1)
                if i == VCH + 1:
                    done = gates(modulation(2, done))
                if i == VCH + 2:
                    v.wait_ge(s_gturn, 1)
                    v.tensor_copy(grow[:], bank[4][0:32, 0:P]).then_inc(s_grow, 1)
            modulation(3, done)

    if upto == 0:
        s_dbg = k.sem("dbg")
        with nc.Block() as block:
            @block.sync
            def _(sp):
                sp.dma_start(A["dbg16"].rearrange("p (a n) -> p a n", a=4)[:, 0:2, :], hT_hi[:]).then_inc(s_dbg, 16)
                sp.dma_start(A["dbg16"].rearrange("p (a n) -> p a n", a=4)[:, 2:4, :], hT_lo[:]).then_inc(s_dbg, 16)
                sp.dma_start(A["out"], x[:]).then_inc(s_dbg, 16)
                sp.dma_start(A["dbg"], gate[:]).then_inc(s_dbg, 16)
                sp.wait_ge(s_dbg, 64)
        return

    pr, sc, tr, oa = bank[0:2], bank[2:4], bank[4:6], bank[6:8]
    turned_bank = (tr[1], pr[1], tr[0])
    score_out = {3: sc[0][:, 0:512], 2: sc[1][:, 0:384], 0: sc[1][:, 384:512], 1: tr[1][:, 0:256]}
    st1 = layout(STAGE)
    bcol = st1("bcol", [P, 3 * H], F32)
    idx16 = st1("idx16", [P, IDXW], F16)
    onehot = st1("onehot", [P, 2, DCHUNK], F16)
    outb = st1("outb", [P, D], F32)
    gob = st1("gob", [P, B, D], F32)
    osum = st1("osum", [P, TB, D], F32)
    s_dec = k.sem("decoded")
    s_rows, s_bcol, s_dist, s_gob = (k.sem(n) for n in ("outb_in", "bias_cols", "dist", "gate_bias"))
    (s_qmm, s_qhi, s_qlo, s_kmm, s_khi, s_klo) = (
        k.sem(n) for n in ("q_mm", "q_hi_done", "q_lo_done", "k_mm",
                           "k_hi_done", "k_lo_done"))
    (s_alibi, s_scored, s_masked, s_exp, s_inv, s_norm, s_turned, s_pthi, s_ptlo) = (
        k.sem(n) for n in ("alibi_ready", "scored", "masked", "exp_done", "sum_inverse", "normalised",
                           "prob_turned", "pt_hi_done", "pt_lo_done"))
    s_cmm, s_chi, s_clo, s_omm, s_oread, s_xadd = (
        k.sem(n) for n in ("ctx_mm", "ctx_hi_done", "ctx_lo_done", "out_mm", "out_read", "x_added"))

    def walk(step):
        def group(eng_n, b, g, r, kind):
            n = eng_n + r
            nxt_b, nxt_h = b, 4 * g + r + 1
            if r == 3 and kind in ("values", "last_loop"):
                nxt_b, nxt_h = (4 * b + g + 1) // 4, (4 * g + 4) % 16
            prev_h = 4 * g + r - 1
            values = None
            if kind == "values":
                values = (b + 1, g - 1)
            elif kind == "boundary":
                values = (b, 3)
                if r == 0:
                    prev_h = H - 1
            step(n, r % 2, nxt_b=nxt_b, nxt_h=nxt_h, prev_h=prev_h, values=values, tt=r,
                 boundary=(kind == "boundary" and r == 0), out_first=(kind == "boundary" and r == 1),
                 b=b, m=4 * b + g, no_values=(kind == "last_loop"))
        return group

    def run_steps(e, step):
        group = walk(step)
        for r in range(4):
            if r == 0:
                step(0, 0, nxt_b=0, nxt_h=1, prev_h=None, values=(0, 3), tt=0, boundary=False,
                     out_first=False, b=0, m=0, no_values=False)
            else:
                step(r, r % 2, nxt_b=0, nxt_h=r + 1, prev_h=r - 1, values=(0, 3), tt=r, boundary=False,
                     out_first=(r == 1), b=0, m=0, no_values=False)
        with e.Fori(0, B - 1) as b:
            with e.Fori(1, 4) as g:
                for r in range(4):
                    group(16 * b + 4 * g, b, g, r, "values")
            for r in range(4):
                group(16 * b + 16, b + 1, 0, r, "boundary")
        with e.Fori(1, 3) as g:
            for r in range(4):
                group(16 * (B - 1) + 4 * g, B - 1, g, r, "last_loop")
        for r in range(4):
            n = NSTEP - 4 + r
            step(n, r % 2, nxt_b=(B - 1 if r < 3 else None), nxt_h=13 + r, prev_h=11 + r, values=None, tt=r,
                 boundary=False, out_first=False, b=B - 1, m=LUTN - 1, no_values=True)
        step(NSTEP, 0, nxt_b=None, nxt_h=None, prev_h=H - 1, values=None, tt=0, boundary=True,
             out_first=False, b=B, m=None, no_values=True, last=True)

    def gate_pair():
        return gate[:].rearrange("p (b d) -> p b d", b=B)

    with nc.Block() as block:
        @block.sync
        def _(sp):
            sp.dma_start(outb[:], bass.AP(tensor=A["rows"].tensor, offset=R_OUTB * D, ap=[[0, P], [1, D]])
                         ).then_inc(s_rows, 16)
            sp.wait_ge(s_rows, 16)

        @block.gpsimd
        def _(g):
            g.iota(dist[:], pattern=[[-1, S]], base=S - P, channel_multiplier=1,
                   allow_small_or_imprecise_dtypes=True).then_inc(s_dist, 1)
            g.wait_ge(s_dist, 1)
            g.affine_select(out=dist[:], in_=dist[:], pattern=[[-1, S]], compare_op=ALU.is_ge, fill=MASKED,
                            base=S - P, channel_multiplier=1).then_inc(s_dist, 1)
            g.tensor_scalar(slopes[:], slopes[:], WS * WS, 1.0, ALU.mult, ALU.mult).then_inc(s_dist, 1)
            g.wait_ge(s_dist, 3)

            def alibi_of(head):
                g.tensor_tensor(alibi[:], dist[:], slopes[:, ds(head, 1)].broadcast_to([P, S]), ALU.mult
                                ).then_inc(s_alibi, 1)

            alibi_of(0)
            g.wait_ge(s_idx, 17)
            for w in (wdec_hi, wdec_lo):
                g.memset(w[:].bitcast(F32), 0.0).then_inc(s_idx, 1)
            g.wait_ge(s_rows, 16)
            for b in range(B):
                g.tensor_tensor(gob[:, b, :], gate[:, b * D:(b + 1) * D], outb[:], ALU.mult).then_inc(s_gob, 1)

            def step(n, s, nxt_b, nxt_h, prev_h, boundary, b, last=False, **_):
                if not last:
                    wait_apart(g, s_inv, n + 1, s_passed)
                    for t in QTILES:
                        part = prob[:, SOFF[t]:SOFF[t] + (t + 1) * P]
                        g.tensor_scalar(part, part, sinv[:, t:t + 1], PS, ALU.mult, ALU.mult
                                        ).then_inc(s_norm, 1)
                if nxt_b is not None:
                    alibi_of(nxt_h)
                if boundary:
                    xb = x[:, ds(TB * (b - 1), TB), :]
                    for t in range(TB):
                        xt = x[:, TB * (b - 1) + t, :]
                        if t == 0:
                            g.wait_ge(s_gob, B)
                        g.tensor_tensor(xt, xt, gob[:, b - 1, :], ALU.add).then_inc(s_xadd, 1)
                    g.wait_ge(s_oread, 2 * b)
                    wait_apart(g, s_xadd, 5 * (b - 1) + TB, s_passed)
                    g.tensor_tensor(xb, xb, osum[:], ALU.add).then_inc(s_xadd, 1)
            run_steps(g, step)

        @block.scalar
        def _(act):
            act.preload_act_table(ACT.Exp)
            act.wait_ge(s_bcol, 3)
            def value_parts(tt, g, u):
                act.wait_ge(s_vmm, u + 1)
                return lambda bk: act.activation(v_hi[:, tt, ds(g * 512, 512)], bk[:, :], ACT.Copy
                                                 ).then_inc(s_vhi, 1)
            def q_part(n1, head):
                act.wait_ge(s_qmm, n1 + 1)
                act.activation(q_hi[:], pr[1][:, :], ACT.Identity, bias=bcol[:, ds(head, 1)]).then_inc(s_qhi, 1)

            def k_part(n1, head):
                act.wait_ge(s_kmm, n1 + 1)
                act.activation(k_hi[:], pr[0][:, :], ACT.Identity, bias=bcol[:, ds(H + head, 1)]
                               ).then_inc(s_khi, 1)
            q_part(0, 0)
            k_part(0, 0)
            act.wait_ge(s_idx, 16)
            act.activation(idx16[:], idx32[:], ACT.Copy).then_inc(s_idx, 1)

            def step(n, s, nxt_b, nxt_h, prev_h, values, tt, last=False, **_):
                if not last:
                    for i, t in enumerate(QTILES):
                        act.wait_ge(s_masked, 4 * n + i + 1)
                        part = prob[:, SOFF[t]:SOFF[t] + (t + 1) * P]
                        act.activation(part, part, ACT.Exp, bias=smin[:, t:t + 1], scale=-1.0,
                                       accum_out=ssum[:, t:t + 1]).then_inc(s_exp, 1)
                if prev_h is not None:
                    act.wait_ge(s_cmm, n)
                    act.activation(ctx_hi[:], pr[0][:, :], ACT.Identity, bias=bcol[:, ds(2 * H + prev_h, 1)]
                                   ).then_inc(s_chi, 1)
                if nxt_b is not None:
                    q_part(n + 1, nxt_h)
                if values is not None:
                    value_parts(tt, values[1], n + 12)(tr[0])
                if nxt_b is not None:
                    k_part(n + 1, nxt_h)
                if not last:
                    for u, unit in enumerate(PT_UNITS):
                        act.wait_ge(s_turned, 3 * n + u + 1)
                        w = sum((4 - j) * P for j in unit)
                        act.activation(pt_hi[:, JOFF[unit[0]]:JOFF[unit[0]] + w], turned_bank[u][:, 0:w], ACT.Copy
                                       ).then_inc(s_pthi, 1)
            run_steps(act, step)

        @block.vector
        def _(v):
            v.tensor_scalar(bcol[:, 0:H], cols[:, C_QKVB:C_QKVB + H], -WS, None, ALU.mult).then_inc(s_bcol, 1)
            v.tensor_scalar(bcol[:, H:2 * H], cols[:, C_QKVB + H:C_QKVB + 2 * H], WS, None, ALU.mult
                            ).then_inc(s_bcol, 1)
            v.tensor_scalar(bcol[:, 2 * H:3 * H], cols[:, C_QKVB + 2 * H:C_QKVB + 3 * H], WS * PS, None,
                            ALU.mult).then_inc(s_bcol, 1)
            v.wait_ge(s_bcol, 3)

            def value_lo(tt, g, u, bk):
                v.wait_ge(s_vhi, u + 1)
                v.tensor_tensor(v_lo[:, tt, ds(g * 512, 512)], bk[:, :], v_hi[:, tt, ds(g * 512, 512)],
                                ALU.subtract).then_inc(s_vlo, 1)
            def q_low(n1, head):
                v.wait_ge(s_qhi, n1 + 1)
                v.scalar_tensor_tensor(q_lo[:], pr[1][:, :], bcol[:, ds(head, 1)], q_hi[:], ALU.add,
                                       ALU.subtract).then_inc(s_qlo, 1)

            def k_low(n1, head):
                v.wait_ge(s_khi, n1 + 1)
                v.scalar_tensor_tensor(k_lo[:], pr[0][:, :], bcol[:, ds(H + head, 1)], k_hi[:], ALU.add,
                                       ALU.subtract).then_inc(s_klo, 1)
            q_low(0, 0)
            k_low(0, 0)
            v.wait_ge(s_lut, 16)
            v.tensor_scalar(lutb[:, 0, :], lutb[:, 0, :], WS, None, ALU.mult).then_inc(s_lut, 1)
            v.wait_ge(s_lut, 17)
            v.tensor_copy(lut16[:], lutb[:, 0, :]).then_inc(s_lut, 1)
            v.wait_ge(s_lut, 18)
            v.tensor_copy(lutb[:, 1, :], lut16[:]).then_inc(s_lut, 1)
            v.wait_ge(s_lut, 19)
            v.tensor_tensor(lutb[:, 2, :], lutb[:, 0, :], lutb[:, 1, :], ALU.subtract).then_inc(s_lut, 1)
            v.wait_ge(s_lut, 20)
            v.wait_ge(s_idx, 19)

            def decode_hot(n, m, r):
                if not (isinstance(n, int) and n == 0):
                    v.wait_ge(s_dec, 4 * n)
                for part in range(2):
                    v.tensor_scalar(onehot[:, part, :], idx16[:, r * DCHUNK:(r + 1) * DCHUNK],
                                    entry[:, ds(m, 1)], lutb[:, 1 + part, ds(m, 1)], ALU.is_equal, ALU.mult
                                    ).then_inc(s_dec, 1)

            def decode_add(n, part, r):
                w = (wdec_hi, wdec_lo)[part][:, r * DCHUNK:(r + 1) * DCHUNK]
                v.wait_ge(s_dec, 4 * n + 2)
                v.tensor_tensor(w, w, onehot[:, part, :], ALU.add).then_inc(s_dec, 1)


            def step(n, s, nxt_b, nxt_h, prev_h, values, tt, boundary, b, m, last=False, **_):
                if not last:
                    v.wait_ge(s_alibi, n + 1)
                    for i, t in enumerate(QTILES):
                        w = (t + 1) * P
                        wait_apart(v, s_scored, 4 * n + (1, 3, 3, 4)[i], s_passed)
                        v.tensor_tensor_reduce(prob[:, SOFF[t]:SOFF[t] + w], score_out[t], alibi[:, S - w:S],
                                               1.0 / (WS * WS), 3e38, ALU.add, ALU.min, smin[:, t:t + 1]
                                               ).then_inc(s_masked, 1)
                    decode_hot(n, m, tt)
                    v.wait_ge(s_exp, 4 * n + 4)
                    v.reciprocal(sinv[:], ssum[:]).then_inc(s_inv, 1)
                if prev_h is not None:
                    v.wait_ge(s_chi, n)
                    v.scalar_tensor_tensor(ctx_lo[:], pr[0][:, :], bcol[:, ds(2 * H + prev_h, 1)], ctx_hi[:],
                                           ALU.add, ALU.subtract).then_inc(s_clo, 1)
                if nxt_b is not None:
                    q_low(n + 1, nxt_h)
                if not last:
                    decode_add(n, 0, tt)
                if values is not None:
                    value_lo(tt, values[1], n + 12, tr[0])
                if not last:
                    decode_add(n, 1, tt)
                if nxt_b is not None:
                    k_low(n + 1, nxt_h)
                if not last:
                    for u, unit in enumerate(PT_UNITS):
                        v.wait_ge(s_pthi, 3 * n + u + 1)
                        w = sum((4 - j) * P for j in unit)
                        o = JOFF[unit[0]]
                        v.tensor_tensor(pt_lo[:, o:o + w], turned_bank[u][:, 0:w], pt_hi[:, o:o + w], ALU.subtract
                                        ).then_inc(s_ptlo, 1)
                if boundary:
                    v.wait_ge(s_omm, n)
                    for i in range(2):
                        v.wait_ge(s_xadd, 5 * b - 4)
                        v.scalar_tensor_tensor(osum[:, 2 * i:2 * i + 2, :],
                                               oa[i][:, :].rearrange("p (t d) -> p t d", t=2),
                                               1.0 / (WS * PS * WS),
                                               gate[:, ds((b - 1) * D, D)].unsqueeze(1).broadcast_to([P, 2, D]),
                                               ALU.mult, ALU.mult).then_inc(s_oread, 1)
            run_steps(v, step)

        @block.tensor
        def _(pe):
            def project(out, hi, lo, col, b):
                return split3(pe, out, [((hi[:, c, ds(col, P)], lo[:, c, ds(col, P)]),
                                         (hT_hi[:, c, ds(b * S, S)], hT_lo[:, c, ds(b * S, S)]))
                                        for c in range(KT)])

            def values_of(b, tt, g, bk):
                tok = b * S + tt * P
                return split3(pe, bk[:, :], [((hT_hi[:, c, ds(tok, P)], hT_lo[:, c, ds(tok, P)]),
                                              (wv_hi[:, c, ds(g * 512, 512)], wv_lo[:, c, ds(g * 512, 512)]))
                                             for c in range(KT)]).then_inc(s_vmm, 1)

            project(pr[1][:, :], wqk_hi, wqk_lo, 0, 0).then_inc(s_qmm, 1)
            project(pr[0][:, :], wqk_hi, wqk_lo, H * HD, 0).then_inc(s_kmm, 1)

            def step(n, s, nxt_b, nxt_h, prev_h, values, tt, boundary, out_first, b, no_values, last=False, **_):
                def score(t):
                    w = (t + 1) * P
                    split3(pe, score_out[t], [((q_hi[:, t * P:w], q_lo[:, t * P:w]), (k_hi[:, 0:w], k_lo[:, 0:w]))]
                           ).then_inc(s_scored, 1)

                def turn(u):
                    o = 0
                    for j in PT_UNITS[u]:
                        for t in range(j, TB):
                            ins = pe.transpose(turned_bank[u][:, o:o + P],
                                               prob[:, SOFF[t] + j * P:SOFF[t] + (j + 1) * P], ident[:, :])
                            o += P
                    ins.then_inc(s_turned, 1)

                if not last:
                    pe.wait_ge(s_qlo, n + 1)
                    pe.wait_ge(s_klo, n + 1)
                    if prev_h is not None:
                        pe.wait_ge(s_masked, 4 * n)
                    for t in QTILES:
                        if t == 1 and prev_h is not None:
                            pe.wait_ge(s_ptlo, 3 * n - 2)
                        score(t)
                if prev_h is not None:
                    pe.wait_ge(s_ptlo, 3 * n)
                    col = prev_h * HD
                    terms = []
                    for j in range(TB):
                        o, w = JOFF[j], (TB - j) * P
                        for vp, pp in ((v_hi, pt_hi), (v_hi, pt_lo), (v_lo, pt_hi)):
                            terms.append((j, vp[:, j, ds(col, HD)], pp[:, o:o + w]))
                    for i, (j, a, p_) in enumerate(terms):
                        ins = pe.matmul(pr[0][:, j * P:512], a, p_, start=(i == 0), stop=(i == len(terms) - 1))
                    ins.then_inc(s_cmm, 1)
                if nxt_b is not None:
                    project(pr[1][:, :], wqk_hi, wqk_lo, nxt_h * HD, nxt_b).then_inc(s_qmm, 1)
                if values is not None:
                    values_of(values[0], tt, values[1], tr[0])
                if prev_h is not None:
                    pe.wait_ge(s_clo, n)
                if nxt_b is not None:
                    project(pr[0][:, :], wqk_hi, wqk_lo, (nxt_h + H) * HD, nxt_b).then_inc(s_kmm, 1)
                if not last:
                    pe.wait_ge(s_norm, 4 * n + 4)
                    turn(0)
                    if nxt_b is not None:
                        pe.wait_ge(s_qlo, n + 2)
                    turn(1)
                    if values is not None:
                        pe.wait_ge(s_vlo, n + 13)
                    turn(2)
                if prev_h is not None:
                    if out_first and not isinstance(n, int):
                        pe.wait_ge(s_oread, 2 * b)
                    for t in range(TB):
                        for i, (ch, wh) in enumerate(((ctx_hi, wo_hi), (ctx_hi, wo_lo), (ctx_lo, wo_hi))):
                            ins = pe.matmul(oa[t // 2][:, (t % 2) * D:(t % 2 + 1) * D], ch[:, t * P:(t + 1) * P],
                                            wh[:, prev_h, :], start=(out_first and t % 2 == 0 and i == 0),
                                            stop=False, skip_group_check=True)
                    ins.then_inc(s_omm, 1)
            run_steps(pe, step)

    def dump_x():
        s_dbg = k.sem("dbg")
        with nc.Block() as block:
            @block.sync
            def _(sp):
                sp.dma_start(A["out"], x[:]).then_inc(s_dbg, 16)
                sp.wait_ge(s_dbg, 16)
    if upto == 1:
        dump_x()
        return

    b2 = layout(BIG)
    amph = b2("amph", [P, 2, KT, D], F32)
    amph_hi = b2("amph_hi", [P, 2, KT, D], F16)
    amph_lo = b2("amph_lo", [P, 2, KT, D], F16)
    entwT = b2("entwT", [P, LE, EC, D], F32)
    entpw = b2("entpw", [P, LE, EC, D], F32)
    path = b2("path", [P, LE, PWN, KT, D], F32)
    rows = b2("rows", [P, 6, D], F32)
    brows = b2("brows", [1, 6, D], F32)
    wst = b2("wst", [P, KT, D], F32)
    wst_hi = b2("wst_hi", [P, 4, KT, D], F16)
    wst_lo = b2("wst_lo", [P, 4, KT, D], F16)
    wrow = b2("wrow", [1, D], F32)
    brow_hi = b2("brow_hi", [1, 4, D], F16)
    brow_lo = b2("brow_lo", [1, 4, D], F16)
    gg = b2("gg", [P, B, D], F32)
    NSL = 3
    xnq = [b2(f"xnq{i}", [P, TB, D], F32) for i in range(NSL)]
    hq = [b2(f"hq{i}", [P, KT, S], F32) for i in range(NSL)]
    tanh = b2("tanh", [P, KT, B * S], F32)
    turnm = b2("turnm", [P, LE * PWN, D], F32)
    nmr = b2("nmr", [P, NT], F32)
    nmean = b2("nmean", [P, NT], F32)
    wk2 = layout(WORK)
    sigm = wk2("sigm", [P, KT, B * S], F32)
    assert b2.pos[0] <= DEC and wk2.pos[0] <= end, (b2.pos[0] - DEC, wk2.pos[0] - end)
    ln1 = LayerNorm("ln1", xnq[0:2], hq[0:2], bank[6:8], 0, CB, SB)
    (s_amph, s_rows2, s_path, s_ent, s_gate2) = (k.sem(n) for n in ("amph_in", "rows_in", "path_in", "ent_in",
                                                                   "gate2_in"))
    (s_ahi, s_alo, s_ph, s_mod2, s_wp, s_whi2, s_wlo2, s_wmm, s_brow, s_wready, s_z, s_act2) = (
        k.sem(n) for n in ("amph_hi_done", "amph_lo_done", "phase_turns", "path_mod", "stage_w", "stage_w_hi",
                           "stage_w_lo", "ent_product", "bias_row", "stage_w_ready", "z_psum", "z_act"))
    (s_wrap, s_sin, s_gg, s_xb, s_h, s_hhi, s_hlo, s_mm, s_st, s_ve, s_rs, s_xn, s_tn, s_fin, s_xb2) = (
        k.sem(n) for n in ("wrapped", "sine", "gate_ln4", "x_bias", "h_new", "h_hi", "h_lo", "stage_mm",
                           "stage_stats", "stage_vareps", "stage_rstd", "stage_xn", "stage_turned",
                           "stage_gated", "x_stage_added"))
    SQRT2 = 2.0 ** 0.5
    TWO_PI = 6.283185
    PI_ = 3.1415925
    ROUND = 12582912.0
    g4, b4 = rows[:, 4, :], rows[:, 5, :]
    ORDER = (1, 3, 0, 2)
    NU = 4 * B
    LAST = 3 * B

    def units(e, first, body, last):
        first()
        with e.Fori(0, LAST // NSL) as i:
            for s in range(NSL):
                body(NSL * i + s, s)
        last()

    with nc.Block() as block:
        @block.sync
        def _(sp):
            sp.dma_start(amph[:], A["amph"]).then_inc(s_amph, 16)
            for r0, n in ((R_PHASE, 4), (R_LN4G, 2)):
                sp.dma_start(rows[:, r0 - R_PHASE:r0 - R_PHASE + n, :].rearrange("p r d -> p (r d)"),
                             bass.AP(tensor=A["rows"].tensor, offset=r0 * D, ap=[[0, P], [1, n * D]])
                             ).then_inc(s_rows2, 16)
            sp.dma_start(brows[:].rearrange("p r d -> p (r d)"), A["rows"][:, R_ENTPB * D:R_PHASE * D]
                         ).then_inc(s_rows2, 16)
            sp.dma_start(path[:], A["path"]).then_inc(s_path, 16)
            load_gate(sp, 0, 1, s_gate2)
            sp.dma_start(entwT[:], A["entwT"]).then_inc(s_ent, 16)
            sp.dma_start(entpw[:], A["entpw"]).then_inc(s_ent, 16)

        @block.gpsimd
        def _(g):
            ln1.gpsimd(g, 0)
            ln1.gpsimd(g, 1)
            g.wait_ge(s_gate2, 16)
            g.wait_ge(s_rows2, 48)
            for b in range(B):
                g.tensor_tensor(gg[:, b, :], gate[:, b * D:(b + 1) * D], g4, ALU.mult).then_inc(s_gg, 1)
            g.wait_ge(s_gg, B)
            for b in range(B):
                gb_ = gate[:, b * D:(b + 1) * D]
                g.tensor_tensor(gb_, gb_, b4, ALU.mult).then_inc(s_gg, 1)
            g.wait_ge(s_gg, 2 * B)
            g.wait_ge(ln1.xn, NT)
            with g.Fori(0, B) as b:
                for t in range(TB):
                    xt = x[:, b * TB + t, :]
                    g.tensor_tensor(xt, xt, gate[:, ds(b * D, D)], ALU.add).then_inc(s_xb, 1)

            with g.Fori(0, B) as b:
                for c in range(KT):
                    g.wait_ge(s_hhi, KT * b + c + 1)
                    g.tensor_tensor(hT_lo[:, c, ds(b * S, S)], sigm[:, c, ds(b * S, S)],
                                    hT_hi[:, c, ds(b * S, S)], ALU.subtract).then_inc(s_hlo, 1)

            def inverse(kk):
                tiles = ds((kk % B) * TB, TB)
                g.wait_ge(s_ve, kk + 1)
                g.tensor_tensor(rstd[:, tiles], vareps[:, tiles], mhalf[:, tiles], ALU.pow).then_inc(s_rs, 1)
                g.wait_ge(s_rs, 2 * kk + 1)
                g.tensor_tensor(nmr[:, tiles], nmean[:, tiles], rstd[:, tiles], ALU.mult).then_inc(s_rs, 1)

            def first():
                inverse(0)
                inverse(1)

            def body(j, s):
                inverse(j + 2)
                b = j % B
                for c in range(KT):
                    g.wait_ge(s_hhi, KT * (B + j) + c + 1)
                    g.tensor_tensor(hT_lo[:, c, ds(b * S, S)], hq[s][:, c, :], hT_hi[:, c, ds(b * S, S)],
                                    ALU.subtract).then_inc(s_hlo, 1)

            def add_x(b):
                xb = x[:, b * TB:(b + 1) * TB, :]
                g.wait_ge(s_fin, b + 1)
                g.tensor_tensor(xb, xb, xnq[(LAST + b) % NSL][:], ALU.add).then_inc(s_xb2, 1)

            def last():
                g.wait_ge(s_xb, NT)
                inverse(NU - 2)
                inverse(NU - 1)
                for b in range(B):
                    add_x(b)
            units(g, first, body, last)

        @block.scalar
        def _(act):
            act.preload_act_table(ACT.Sin)
            act.wait_ge(s_ph, 2)
            act.activation(turnm[:], turnm[:], ACT.Sin, scale=-TWO_PI).then_inc(s_ph, 1)
            act.preload_act_table(ACT.Sigmoid)
            act.wait_ge(s_amph, 16)
            act.activation(amph_hi[:], amph[:], ACT.Copy, scale=WS).then_inc(s_ahi, 1)
            ln1.scalar(act, 0)

            def z_act(b):
                for w in range(2):
                    for f in range(KT):
                        act.wait_ge(s_z, 4 * b + 2 * w + f + 1)
                        bc = (C_AMPB, C_PHB)[w] + f
                        act.activation((sigm, tanh)[w][:, f, ds(b * S, S)], bank[2 * w + f][:, :],
                                       (ACT.Sigmoid, ACT.Tanh)[w], bias=cols[:, bc:bc + 1], scale=1.0 / WS
                                       ).then_inc(s_act2, 1)

            def weight_hi(i):
                act.wait_ge(s_wp, i + 1)
                act.activation(wst_hi[:, ORDER[i], :, :], wst[:], ACT.Copy, scale=WS).then_inc(s_whi2, 1)
            z_act(0)
            ln1.scalar(act, 1)
            with act.Fori(1, B) as b:
                z_act(b)
            weight_hi(0)
            weight_hi(1)
            act.preload_act_table(ACT.Sin)

            def sine(b):
                act.wait_ge(s_wrap, 2 * b + 2)
                act.activation(tanh[:, :, ds(b * S, S)], tanh[:, :, ds(b * S, S)], ACT.Sin, scale=PI_
                               ).then_inc(s_sin, 1)

            def sine_hi(b):
                act.wait_ge(s_h, KT * b + KT)
                for c in range(KT):
                    act.activation(hT_hi[:, c, ds(b * S, S)], sigm[:, c, ds(b * S, S)], ACT.Copy
                                   ).then_inc(s_hhi, 1)
            sine(0)
            with act.Fori(1, B) as b:
                sine(b)
                sine_hi(b - 1)
            sine_hi(B - 1)
            weight_hi(2)
            weight_hi(3)

            def normalise(kk, s):
                act.wait_ge(s_rs, 2 * kk + 2)
                act.wait_ge(s_tn, KT * kk + KT)
                for t in range(TB):
                    col = ds((kk % B) * TB + t, 1)
                    act.activation(xnq[s][:, t, :], bank[2 * s + t // 2][:, (t % 2) * D:(t % 2 + 1) * D],
                                   ACT.Identity, bias=nmr[:, col], scale=rstd[:, col]).then_inc(s_xn, 1)

            def first():
                normalise(0, 0)
                normalise(1, 1)

            def body(j, s):
                b = j % B
                for c in range(KT):
                    act.wait_ge(s_h, KT * (B + j) + c + 1)
                    act.activation(hT_hi[:, c, ds(b * S, S)], hq[s][:, c, :], ACT.Copy).then_inc(s_hhi, 1)
                normalise(j + 2, (s + 2) % NSL)

            def last():
                normalise(NU - 2, (NU - 2) % NSL)
                act.wait_ge(s_xb2, 1)
                act.wait_ge(s_rs, 2 * NU)
                s = (NU - 1) % NSL
                for t in range(TB):
                    col = (B - 1) * TB + t
                    act.activation(xnq[s][:, t, :], bank[2 * s + t // 2][:, (t % 2) * D:(t % 2 + 1) * D],
                                   ACT.Identity, bias=nmr[:, col:col + 1], scale=rstd[:, col:col + 1]
                                   ).then_inc(s_xn, 1)
            units(act, first, body, last)

        @block.tensor
        def _(pe):
            def z(b):
                ln1.wait_parts(pe, b)
                for w in range(2):
                    for f in range(KT):
                        pe.wait_ge(s_act2, 4 * b + 2 * w + f + 1)
                        split3(pe, bank[2 * w + f][:, :],
                               [((amph_hi[:, w, c, f * P:(f + 1) * P], amph_lo[:, w, c, f * P:(f + 1) * P]),
                                 (hT_hi[:, c, ds(b * S, S)], hT_lo[:, c, ds(b * S, S)]))
                                for c in range(KT)]).then_inc(s_z, 1)
            ln1.tensor(pe, 0)
            pe.wait_ge(s_alo, 1)
            z(0)
            ln1.tensor(pe, 1)
            with pe.Fori(1, B) as b:
                z(b)
            pe.wait_ge(s_ent, 32)
            pe.wait_ge(s_act2, 4 + 4 * B)
            for l in range(LE):
                if l == 1:
                    pe.wait_ge(ln1.tmp, KT + KT * B)
                for dt in range(KT):
                    for kc in range(EC):
                        ins = pe.matmul(bank[5 * l + dt][:, 0:D], entwT[:, l, kc, dt * P:(dt + 1) * P],
                                        entpw[:, l, kc, :], start=(kc == 0), stop=(kc == EC - 1))
                for kc in range(EC):
                    ins = pe.matmul(bank[5 * l + 2][0:1, 0:D], cols[:, C_ENTB + l * EC + kc:C_ENTB + l * EC + kc + 1],
                                    entpw[:, l, kc, :], start=(kc == 0), stop=(kc == EC - 1))
                ins.then_inc(s_wmm, 1)

            def product(kk, s):
                st, b = kk // B, kk % B
                pe.wait_ge(s_hlo, KT * kk + KT)
                for t in range(TB):
                    if t % 2 == 0:
                        pe.wait_ge(s_xn, TB * kk + t + 2)
                    tok = b * S + t * P
                    out = bank[2 * s + t // 2][:, (t % 2) * D:(t % 2 + 1) * D]
                    terms = []
                    for c in range(KT):
                        hh, hl = hT_hi[:, c, ds(tok, P)], hT_lo[:, c, ds(tok, P)]
                        wh, wl = wst_hi[:, ds(st, 1), c, :], wst_lo[:, ds(st, 1), c, :]
                        wh, wl = (w.rearrange("p a d -> p (a d)") for w in (wh, wl))
                        terms += [(hh, wh), (hh, wl), (hl, wh)]
                    for br in (brow_hi, brow_lo):
                        terms.append((ones16[:, :], br[:, ds(st, 1), :].rearrange("p a d -> p (a d)")))
                    for i, (a, w) in enumerate(terms):
                        ins = pe.matmul(out, a, w, start=(i == 0), stop=(i == len(terms) - 1))
                    ins.then_inc(s_mm, 1)

            def first():
                pe.wait_ge(s_wready, LE + 1)
                product(0, 0)
                product(1, 1)
                pe.wait_ge(s_wready, 2 * LE)

            def body(j, s):
                product(j + 2, (s + 2) % NSL)
                pe.wait_ge(s_xn, NSL * TB + TB * j + TB)
                for c in range(KT):
                    pe.wait_ge(s_h, KT * (B + j - 1) + c + 1)
                    for t in range(TB):
                        ins = pe.transpose(bank[6 + c][:, t * P:(t + 1) * P], xnq[s][:, t, c * P:(c + 1) * P],
                                           ident[:, :])
                    ins.then_inc(s_tn, 1)

            def last():
                product(NU - 2, (NU - 2) % NSL)
                product(NU - 1, (NU - 1) % NSL)
            units(pe, first, body, last)

        @block.vector
        def _(v):
            ln1.free_slots(v)
            v.sem_inc(s_act2, 4)
            v.sem_inc(s_xn, NSL * TB)
            v.sem_inc(s_tn, NSL * KT)
            v.wait_ge(s_rows2, 48)
            ph = rows[:, 0:4, :]
            v.tensor_scalar(ph, ph, 1.0 / 6.283185307179586, 0.125, ALU.mult, ALU.add).then_inc(s_mod2, 1)
            v.wait_ge(s_mod2, 1)
            v.tensor_scalar(turnm[:], ph, ROUND, None, ALU.add).then_inc(s_ph, 1)
            v.wait_ge(s_ph, 1)
            v.scalar_tensor_tensor(turnm[:].rearrange("p a d -> p (a d)"), turnm[:].rearrange("p a d -> p (a d)"),
                                   -ROUND, ph.rearrange("p a d -> p (a d)"), ALU.add, ALU.subtract
                                   ).then_inc(s_ph, 1)
            ln1.normalise(v, 0)
            v.wait_ge(s_ahi, 1)
            v.scalar_tensor_tensor(amph_lo[:].rearrange("p a k d -> p (a k d)"),
                                   amph[:].rearrange("p a k d -> p (a k d)"), WS,
                                   amph_hi[:].rearrange("p a k d -> p (a k d)"),
                                   ALU.mult, ALU.subtract).then_inc(s_alo, 1)
            ln1.modulate(v, 0)
            ln1.vector(v, 1)
            v.wait_ge(s_ph, 3)
            v.wait_ge(s_path, 16)
            n = 1
            for l in range(LE):
                for p_ in range(PWN):
                    m = turnm[:, l * PWN + p_, :]
                    pw = path[:, l, p_, :, :]
                    for c in range(KT):
                        v.scalar_tensor_tensor(pw[:, c, :], m, SQRT2, pw[:, c, :], ALU.mult, ALU.mult
                                               ).then_inc(s_mod2, 1)
                    pb = brows[0:1, LE + l * PWN + p_, :]
                    v.scalar_tensor_tensor(pb, turnm[0:1, l * PWN + p_, :], SQRT2, pb, ALU.mult, ALU.mult
                                           ).then_inc(s_mod2, 1)
                    n += 3
            v.wait_ge(s_mod2, n)

            def stage_weight(i, n):
                st = ORDER[i]
                l = st // 2
                if st % 2:
                    v.tensor_tensor(wst[:], path[:, l, 0, :, :], path[:, l, 1, :, :], ALU.add).then_inc(s_mod2, 1)
                    v.tensor_tensor(wrow[:], brows[0:1, LE + 2 * l, :], brows[0:1, LE + 2 * l + 1, :], ALU.add
                                    ).then_inc(s_brow, 1)
                    n += 1
                else:
                    v.wait_ge(s_wmm, l + 1)
                    for c in range(KT):
                        v.tensor_copy(wst[:, c, :], bank[5 * l + c][:, 0:D]).then_inc(s_mod2, 1)
                    n += 2
                    v.tensor_tensor(wrow[:], bank[5 * l + 2][0:1, 0:D], brows[0:1, l, :], ALU.add
                                    ).then_inc(s_brow, 1)
                v.wait_ge(s_brow, 3 * i + 1)
                v.tensor_scalar(brow_hi[:, st, :], wrow[:], WS, None, ALU.mult).then_inc(s_brow, 1)
                v.wait_ge(s_mod2, n)
                for c in range(KT):
                    diag = wst[:, c, c * P:(c + 1) * P]
                    v.tensor_tensor(diag, diag, ident[:], ALU.add).then_inc((s_mod2, s_wp)[c], 1)
                v.wait_ge(s_brow, 3 * i + 2)
                v.scalar_tensor_tensor(brow_lo[:, st, :], wrow[:], WS, brow_hi[:, st, :], ALU.mult, ALU.subtract
                                       ).then_inc(s_brow, 1)
                v.wait_ge(s_whi2, i + 1)
                v.scalar_tensor_tensor(wst_lo[:, st, :, :].rearrange("p k d -> p (k d)"),
                                       wst[:].rearrange("p k d -> p (k d)"), WS,
                                       wst_hi[:, st, :, :].rearrange("p k d -> p (k d)"), ALU.mult, ALU.subtract
                                       ).then_inc(s_wlo2, 1)
                v.wait_ge(s_brow, 3 * i + 3)
                v.wait_ge(s_wlo2, i + 1)
                v.sem_inc(s_wready, 1)
                return n + 1
            n = stage_weight(0, n)
            n = stage_weight(1, n)

            def wrap(b):
                th = tanh[:, :, ds(b * S, S)]
                v.wait_ge(s_act2, 4 + 4 * b + 4)
                v.tensor_scalar(hq[2][:], th, 0.75, -2.0, ALU.is_gt, ALU.mult).then_inc(s_wrap, 1)
                v.wait_ge(s_wrap, 2 * b + 1)
                v.scalar_tensor_tensor(th, hq[2][:], 0.25, th, ALU.add, ALU.add).then_inc(s_wrap, 1)

            def sine_times(b):
                v.wait_ge(s_sin, b + 1)
                for c in range(KT):
                    sg = sigm[:, c, ds(b * S, S)]
                    v.scalar_tensor_tensor(sg, tanh[:, c, ds(b * S, S)], SQRT2, sg, ALU.mult, ALU.mult
                                           ).then_inc(s_h, 1)
            wrap(0)
            with v.Fori(1, B) as b:
                v.wait_ge(s_wrap, 2 * b)
                wrap(b)
                sine_times(b - 1)
            sine_times(B - 1)
            n = stage_weight(2, n)
            n = stage_weight(3, n)

            def statistics(kk, s):
                b = kk % B
                for t in range(TB):
                    v.wait_ge(s_mm, TB * kk + 2 * (t // 2) + 2)
                    v.bn_stats(stats[:, ds(b * TB + t, 1), :].rearrange("p a n -> p (a n)"),
                               bank[2 * s + t // 2][:, (t % 2) * D:(t % 2 + 1) * D]).then_inc(s_st, 1)
                v.wait_ge(s_st, (TB + 5) * kk + TB)
                combine_stats(v, s_st, b, (TB + 5) * kk + TB, EPS * WS * WS, nmean
                              ).then_inc(s_ve, 1)

            def first():
                statistics(0, 0)
                statistics(1, 1)

            def body(j, s):
                statistics(j + 2, (s + 2) % NSL)
                st = j // B
                for c in range(KT):
                    gc = C_LN + (st % 2) * 2 * LE * KT + (st // 2) * KT + c
                    v.wait_ge(s_tn, NSL * KT + KT * j + c + 1)
                    v.wait_ge(s_hlo, KT * (B + j - NSL) + c + 1)
                    v.tensor_scalar(hq[s][:, c, :], bank[6 + c][:, :], cols[:, ds(gc, 1)],
                                    cols[:, ds(gc + LE * KT, 1)], ALU.mult, ALU.add).then_inc(s_h, 1)

            def gated(b):
                v.wait_ge(s_xn, NSL * TB + TB * (LAST + b) + TB)
                xq = xnq[(LAST + b) % NSL]
                v.tensor_tensor(xq[:], xq[:], gg[:, b, :].unsqueeze(1).broadcast_to([P, TB, D]), ALU.mult
                                ).then_inc(s_fin, 1)

            def last():
                v.wait_ge(s_gg, B)
                gated(0)
                statistics(NU - 2, (NU - 2) % NSL)
                gated(1)
                statistics(NU - 1, (NU - 1) % NSL)
                gated(2)
                gated(3)
            units(v, first, body, last)

    if upto == 2:
        dump_x()
        return

    b3 = layout(BIG)
    P3 = b3.pos[0]
    wo1 = b3("wo1", [P, KT, D], F32)
    wo1_hi = b3("wo1_hi", [P, KT, D], F16)
    wo1_lo = b3("wo1_lo", [P, KT, D], F16)
    qk1_hi = b3("qk1_hi", [P, 2 * KT, B * S], F16)
    qk1_lo = b3("qk1_lo", [P, 2 * KT, B * S], F16)
    v1_hi = b3("v1_hi", [P, NT, D], F16)
    v1_lo = b3("v1_lo", [P, NT, D], F16)
    bcol1 = b3("bcol1", [P, 3 * KT], F32)
    boutb = b3("boutb", [P, D], F32)
    T3 = b3.pos[0]
    xq3 = [b3(f"xq3_{i}", [P, TB, D], F32) for i in range(2)]
    tq3 = [b3(f"tq3_{i}", [P, KT, S], F32) for i in range(2)]
    assert b3.pos[0] <= DEC, b3.pos[0] - DEC
    w3a = layout(b3.pos[0])
    wq1 = w3a("wq1", [P, KT, 3 * D], F32)
    wq1_hi = w3a("wq1_hi", [P, KT, 3 * D], F16)
    wq1_lo = w3a("wq1_lo", [P, KT, 3 * D], F16)
    assert w3a.pos[0] <= DEC, w3a.pos[0] - DEC
    t3 = layout(T3)
    prob1 = t3("prob1", [P, TB, S], F32)
    pt1_hi = t3("pt1_hi", [P, TB, S], F16)
    pt1_lo = t3("pt1_lo", [P, TB, S], F16)
    ctx1_hi = t3("ctx1_hi", [P, KT, S], F16)
    ctx1_lo = t3("ctx1_lo", [P, KT, S], F16)
    osum1 = t3("osum1", [P, TB, D], F32)
    gbo = t3("gbo", [P, B, D], F32)
    assert t3.pos[0] <= DEC
    t3c = layout(t3.pos[0])
    smin1 = t3c("smin1", [P, TB], F32)
    sminb = t3c("sminb", [P, TB], F32)
    ssum1 = t3c("ssum1", [P, TB], F32)
    sinv1 = t3c("sinv1", [P, TB], F32)
    assert t3c.pos[0] <= DEC, t3c.pos[0] - DEC
    ln2 = LayerNorm("ln2", xq3, tq3, bank[6:8], 1, CA, SA)
    (s_wq1, s_bout, s_gate3, s_whi3, s_wlo3, s_bc3, s_pmm, s_phi, s_plo) = (
        k.sem(n) for n in ("wq1_in", "bout_in", "gate3_in", "w1_hi", "w1_lo", "bias1_cols",
                           "proj1_mm", "proj1_hi", "proj1_lo"))

    with nc.Block() as block:
        @block.sync
        def _(sp):
            sp.dma_start(wq1[:], A["wqkv1"]).then_inc(s_wq1, 16)
            sp.dma_start(wo1[:], A["wout1"]).then_inc(s_wq1, 16)
            sp.dma_start(boutb[:], bass.AP(tensor=A["rows"].tensor, offset=R_BOUT * D, ap=[[0, P], [1, D]])
                         ).then_inc(s_bout, 16)
            load_gate(sp, 1, 0, s_gate3)
            sp.wait_ge(s_gate3, 16)
            sp.wait_ge(s_bout, 16)

        @block.gpsimd
        def _(g):
            ln2.inverse(g, 0)
            ln2.split_lo(g, 0)
            ln2.inverse(g, 1)
            ln2.split_lo(g, 1)

        @block.scalar
        def _(act):
            act.preload_act_table(ACT.Exp)
            act.wait_ge(s_wq1, 32)
            act.activation(wq1_hi[:, :, 0:D], wq1[:, :, 0:D], ACT.Copy, scale=-WS).then_inc(s_whi3, 1)
            act.activation(wq1_hi[:, :, D:3 * D], wq1[:, :, D:3 * D], ACT.Copy, scale=WS).then_inc(s_whi3, 1)
            act.activation(wo1_hi[:], wo1[:], ACT.Copy, scale=WS).then_inc(s_whi3, 1)
            ln2.scalar(act, 0)
            act.wait_ge(s_bc3, 3)

            def projections(b):
                for i in range(2 * KT):
                    act.wait_ge(s_pmm, 6 * b + i + 1)
                    act.activation(qk1_hi[:, i, ds(b * S, S)], bank[i][:, :], ACT.Identity,
                                   bias=bcol1[:, i:i + 1]).then_inc(s_phi, 1)
                for i in range(2):
                    act.wait_ge(s_pmm, 6 * b + 4 + i + 1)
                    act.activation(v1_hi[:, ds(b * TB + 2 * i, 2), :], bank[4 + i][:, :].rearrange(
                        "p (t d) -> p t d", t=2), ACT.Copy).then_inc(s_phi, 1)
            projections(0)
            ln2.scalar(act, 1)
            with act.Fori(1, B) as b:
                projections(b)

        @block.vector
        def _(v):
            ln2.free_slots(v)
            v.sem_inc(s_plo, 6)
            ln2.normalise(v, 0)
            for i, (o, w, sg) in enumerate(((0, D, -WS), (D, 2 * D, WS))):
                v.wait_ge(s_whi3, i + 1)
                v.scalar_tensor_tensor(wq1_lo[:, :, o:o + w], wq1[:, :, o:o + w], sg, wq1_hi[:, :, o:o + w],
                                       ALU.mult, ALU.subtract).then_inc(s_wlo3, 1)
            v.wait_ge(s_whi3, 3)
            v.scalar_tensor_tensor(wo1_lo[:], wo1[:], WS, wo1_hi[:], ALU.mult, ALU.subtract).then_inc(s_wlo3, 1)
            for i, sc_ in enumerate((-WS, WS, WS * PS)):
                v.tensor_scalar(bcol1[:, KT * i:KT * i + KT], cols[:, C_B1 + KT * i:C_B1 + KT * i + KT], sc_, None,
                                ALU.mult).then_inc(s_bc3, 1)
            v.wait_ge(s_bc3, 3)
            ln2.modulate(v, 0)
            ln2.normalise(v, 1)

            def projections(b):
                for i in range(2 * KT):
                    v.wait_ge(s_phi, 6 * b + i + 1)
                    v.scalar_tensor_tensor(qk1_lo[:, i, ds(b * S, S)], bank[i][:, :], bcol1[:, i:i + 1],
                                           qk1_hi[:, i, ds(b * S, S)], ALU.add, ALU.subtract).then_inc(s_plo, 1)
                for i in range(2):
                    v.wait_ge(s_phi, 6 * b + 4 + i + 1)
                    v.tensor_tensor(v1_lo[:, ds(b * TB + 2 * i, 2), :], bank[4 + i][:, :].rearrange(
                        "p (t d) -> p t d", t=2), v1_hi[:, ds(b * TB + 2 * i, 2), :], ALU.subtract
                        ).then_inc(s_plo, 1)
            projections(0)
            ln2.modulate(v, 1)
            with v.Fori(1, B) as b:
                projections(b)

        @block.tensor
        def _(pe):
            def projections(b):
                ln2.wait_parts(pe, b)
                for i in range(2 * KT):
                    pe.wait_ge(s_plo, 6 * b + i + 1)
                    split3(pe, bank[i][:, :], [((wq1_hi[:, c, i * P:(i + 1) * P], wq1_lo[:, c, i * P:(i + 1) * P]),
                                                (hT_hi[:, c, ds(b * S, S)], hT_lo[:, c, ds(b * S, S)]))
                                               for c in range(KT)]).then_inc(s_pmm, 1)
                for i in range(2):
                    pe.wait_ge(s_plo, 6 * b + 4 + i + 1)
                    for t in (2 * i, 2 * i + 1):
                        tok = b * S + t * P
                        ins = split3(pe, bank[4 + i][:, (t % 2) * D:(t % 2 + 1) * D],
                                     [((hT_hi[:, c, ds(tok, P)], hT_lo[:, c, ds(tok, P)]),
                                       (wq1_hi[:, c, 2 * D:3 * D], wq1_lo[:, c, 2 * D:3 * D])) for c in range(KT)])
                    ins.then_inc(s_pmm, 1)
            ln2.tensor(pe, 0)
            pe.wait_ge(s_wlo3, 2)
            projections(0)
            ln2.tensor(pe, 1)
            with pe.Fori(1, B) as b:
                projections(b)

    (s_sc1, s_mn1, s_mb1, s_ex1, s_iv1, s_nm1, s_tn1, s_th1, s_tl1, s_cm1, s_ch1, s_cl1, s_om1, s_or1, s_xa1,
     s_gb1) = (
        k.sem(n) for n in ("scored1", "min1", "min1_scaled", "exp1", "inverse1", "normalised1", "turned1",
                           "pt1_hi_done", "pt1_lo_done", "ctx1_mm", "ctx1_hi_done", "ctx1_lo_done", "out1_mm",
                           "out1_read", "x1_added", "gate_bout"))
    SCALE1 = 1.0 / (WS * WS * D ** 0.5)
    TRB = (4, 5, 0, 1)

    def run1(e, step):
        step(0, first=True, last=False)
        with e.Fori(1, B) as i:
            step(i, first=False, last=False)
        step(B, first=False, last=True)

    with nc.Block() as block:
        @block.gpsimd
        def _(g):
            for b in range(B):
                g.tensor_tensor(gbo[:, b, :], gate[:, b * D:(b + 1) * D], boutb[:], ALU.mult).then_inc(s_gb1, 1)
            g.wait_ge(s_gb1, B)

            def step(i, first, last):
                if not last:
                    wait_apart(g, s_iv1, i + 1, s_passed)
                    for t in range(TB):
                        g.tensor_scalar(prob1[:, t, :], prob1[:, t, :], sinv1[:, t:t + 1], PS, ALU.mult, ALU.mult
                                        ).then_inc(s_nm1, 1)
                if not first:
                    for t in range(TB):
                        xt = x[:, TB * (i - 1) + t, :]
                        g.tensor_tensor(xt, xt, gbo[:, i - 1, :], ALU.add).then_inc(s_xa1, 1)
                    g.wait_ge(s_xa1, 5 * i - 1)
                    wait_apart(g, s_or1, 2 * i + 2, s_passed)
                    xb = x[:, ds(TB * (i - 1), TB), :]
                    g.tensor_tensor(xb, xb, osum1[:], ALU.add).then_inc(s_xa1, 1)
            run1(g, step)

        @block.scalar
        def _(act):
            act.preload_act_table(ACT.Exp)

            def step(i, first, last):
                if not last:
                    for t in range(TB):
                        act.wait_ge(s_mb1, TB * i + t + 1)
                        act.activation(prob1[:, t, :], bank[t][:, :], ACT.Exp, bias=sminb[:, t:t + 1],
                                       scale=-SCALE1, accum_out=ssum1[:, t:t + 1]).then_inc(s_ex1, 1)
                if not first:
                    for c in range(KT):
                        act.wait_ge(s_cm1, KT * (i - 1) + c + 1)
                        act.activation(ctx1_hi[:, c, :], bank[6 + c][:, :], ACT.Identity,
                                       bias=bcol1[:, 2 * KT + c:2 * KT + c + 1]).then_inc(s_ch1, 1)
                if not last:
                    for j in range(TB):
                        act.wait_ge(s_tn1, TB * i + j + 1)
                        act.activation(pt1_hi[:, j, :], bank[TRB[j]][:, :], ACT.Copy).then_inc(s_th1, 1)
            run1(act, step)

        @block.vector
        def _(v):
            v.sem_inc(s_or1, 2)
            def step(i, first, last):
                if not last:
                    for t in range(TB):
                        v.wait_ge(s_sc1, TB * i + t + 1)
                        v.tensor_reduce(smin1[:, t:t + 1], bank[t][:, :], AX.X, ALU.min).then_inc(s_mn1, 1)
                        v.wait_ge(s_mn1, TB * i + t + 1)
                        v.tensor_scalar(sminb[:, t:t + 1], smin1[:, t:t + 1], SCALE1, None, ALU.mult
                                        ).then_inc(s_mb1, 1)
                    v.wait_ge(s_ex1, TB * i + TB)
                    v.reciprocal(sinv1[:], ssum1[:]).then_inc(s_iv1, 1)
                if not first:
                    for c in range(KT):
                        v.wait_ge(s_ch1, KT * (i - 1) + c + 1)
                        v.scalar_tensor_tensor(ctx1_lo[:, c, :], bank[6 + c][:, :],
                                               bcol1[:, 2 * KT + c:2 * KT + c + 1], ctx1_hi[:, c, :], ALU.add,
                                               ALU.subtract).then_inc(s_cl1, 1)
                    for q in range(2):
                        v.wait_ge(s_om1, 2 * (i - 1) + q + 1)
                        v.wait_ge(s_xa1, 5 * i - 1)
                        v.scalar_tensor_tensor(osum1[:, 2 * q:2 * q + 2, :],
                                               bank[2 + q][:, :].rearrange("p (t d) -> p t d", t=2),
                                               1.0 / (WS * PS * WS),
                                               gate[:, ds((i - 1) * D, D)].unsqueeze(1).broadcast_to([P, 2, D]),
                                               ALU.mult, ALU.mult).then_inc(s_or1, 1)
                if not last:
                    for j in range(TB):
                        v.wait_ge(s_th1, TB * i + j + 1)
                        v.tensor_tensor(pt1_lo[:, j, :], bank[TRB[j]][:, :], pt1_hi[:, j, :], ALU.subtract
                                        ).then_inc(s_tl1, 1)
            run1(v, step)

        @block.tensor
        def _(pe):
            def step(i, first, last):
                if not last:
                    for t in range(TB):
                        if not first and t < 2:
                            pe.wait_ge(s_tl1, TB * (i - 1) + 3 + t)
                        elif not first:
                            pe.wait_ge(s_or1, 2 * i)
                        split3(pe, bank[t][:, :],
                               [((qk1_hi[:, c, ds(i * S + t * P, P)], qk1_lo[:, c, ds(i * S + t * P, P)]),
                                 (qk1_hi[:, KT + c, ds(i * S, S)], qk1_lo[:, KT + c, ds(i * S, S)]))
                                for c in range(KT)]).then_inc(s_sc1, 1)
                if not first:
                    pe.wait_ge(s_tl1, TB * i)
                    for c in range(KT):
                        split3(pe, bank[6 + c][:, :],
                               [((v1_hi[:, (i - 1) * TB + j, c * P:(c + 1) * P],
                                  v1_lo[:, (i - 1) * TB + j, c * P:(c + 1) * P]),
                                 (pt1_hi[:, j, :], pt1_lo[:, j, :])) for j in range(TB)]).then_inc(s_cm1, 1)
                    pe.wait_ge(s_cl1, KT * i)
                    if not last:
                        pe.wait_ge(s_ex1, TB * i + TB)
                    for q in range(2):
                        for t in (2 * q, 2 * q + 1):
                            ins = split3(pe, bank[2 + q][:, (t % 2) * D:(t % 2 + 1) * D],
                                         [((ctx1_hi[:, c, t * P:(t + 1) * P], ctx1_lo[:, c, t * P:(t + 1) * P]),
                                           (wo1_hi[:, c, :], wo1_lo[:, c, :])) for c in range(KT)])
                        ins.then_inc(s_om1, 1)
                if not last:
                    pe.wait_ge(s_nm1, TB * i + TB)
                    for j in range(TB):
                        for t in range(TB):
                            ins = pe.transpose(bank[TRB[j]][:, t * P:(t + 1) * P],
                                               prob1[:, t, j * P:(j + 1) * P], ident[:, :])
                        ins.then_inc(s_tn1, 1)
            run1(pe, step)

    if upto == 3:
        dump_x()
        return

    b4_ = layout(P3)
    mT_hi = b4_("mT_hi", [P, IC, B * S], F16)
    mT_lo = b4_("mT_lo", [P, IC, B * S], F16)
    X4 = b4_.pos[0]
    xq4 = [b4_(f"xq4_{i}", [P, TB, D], F32) for i in range(2)]
    tq4 = [b4_(f"tq4_{i}", [P, KT, S], F32) for i in range(2)]
    silu = [b4_(f"silu{i}", [P, S], F32) for i in range(2)]
    prod = [b4_(f"prod{i}", [P, S], F32) for i in range(2)]
    osum4 = b4_("osum4", [P, TB, D], F32)
    assert b4_.pos[0] <= DEC, b4_.pos[0] - DEC
    ln3 = LayerNorm("ln3", xq4, tq4, bank[6:8], 1, CB, SB)
    (s_gate4, s_gmm, s_umm, s_silu, s_prod, s_mhi, s_mlo, s_dmm, s_dread, s_xout, s_stored) = (
        k.sem(n) for n in ("gate4_in", "gate_mm", "up_mm", "silu_done", "product", "m_hi", "m_lo", "down_mm",
                           "down_read", "x_final", "stored"))
    GW = KT * INTER

    def dec(w, which, c, o):
        if which < 2:
            a = which * GW + c * INTER + o * P
            return w[:, a:a + (P if o < IC - 1 else LASTI)]
        return w[0:(P if c < IC - 1 else LASTI), 2 * GW + c * D:2 * GW + (c + 1) * D]

    with nc.Block() as block:
        @block.sync
        def _(sp):
            load_gate(sp, 1, 1, s_gate4)
            with sp.Fori(0, B) as b:
                sp.wait_ge(s_xout, b + 2)
                sp.dma_start(A["out"][:, ds(b * TB, TB), :], x[:, ds(b * TB, TB), :]).then_inc(s_stored, 16)
            sp.wait_ge(s_stored, 16 * B)

        @block.gpsimd
        def _(g):
            ln3.inverse(g, 0)
            ln3.split_lo(g, 0)
            ln3.inverse(g, 1)

            def products(b):
                for oc in range(IC):
                    w = P if oc < IC - 1 else LASTI
                    g.wait_ge(s_mhi, IC * b + oc + 1)
                    g.tensor_tensor(mT_lo[0:w, oc, ds(b * S, S)], prod[oc % 2][0:w, :],
                                    mT_hi[0:w, oc, ds(b * S, S)], ALU.subtract).then_inc(s_mlo, 1)
            products(0)
            ln3.split_lo(g, 1)
            with g.Fori(1, B) as b:
                products(b)

        @block.scalar
        def _(act):
            act.preload_act_table(ACT.Silu)
            ln3.scalar(act, 0)

            def silu_of(b, oc):
                w = P if oc < IC - 1 else LASTI
                act.wait_ge(s_gmm, IC * b + oc + 1)
                act.wait_ge(s_prod, IC * b + oc + 1)
                act.activation(silu[oc % 2][0:w, :], bank[oc % 2][0:w, :], ACT.Silu, scale=1.0 / WS
                               ).then_inc(s_silu, 1)

            def hi_of(b, oc):
                w = P if oc < IC - 1 else LASTI
                act.wait_ge(s_prod, 2 + IC * b + oc + 1)
                act.activation(mT_hi[0:w, oc, ds(b * S, S)], prod[oc % 2][0:w, :], ACT.Copy).then_inc(s_mhi, 1)

            def products(b):
                silu_of(b, 0)
                for oc in range(1, IC):
                    silu_of(b, oc)
                    hi_of(b, oc - 1)
                hi_of(b, IC - 1)
            products(0)
            ln3.scalar(act, 1)
            with act.Fori(1, B) as b:
                products(b)

        @block.vector
        def _(v):
            ln3.free_slots(v)
            v.sem_inc(s_mlo, 2)
            v.sem_inc(s_prod, 2)
            v.sem_inc(s_dread, 2)
            v.sem_inc(s_xout, 1)
            ln3.vector(v, 0)
            ln3.normalise(v, 1)

            def products(b):
                for oc in range(IC):
                    w = P if oc < IC - 1 else LASTI
                    v.wait_ge(s_umm, IC * b + oc + 1)
                    v.wait_ge(s_silu, IC * b + oc + 1)
                    v.wait_ge(s_mlo, IC * b + oc + 1)
                    v.scalar_tensor_tensor(prod[oc % 2][0:w, :], bank[2 + oc % 2][0:w, :], 1.0 / WS,
                                           silu[oc % 2][0:w, :], ALU.mult, ALU.mult).then_inc(s_prod, 1)

            def down_out(b):
                v.wait_ge(s_xout, b + 1)
                for q in range(2):
                    v.wait_ge(s_dmm, 2 * b + q + 1)
                    v.scalar_tensor_tensor(osum4[:, 2 * q:2 * q + 2, :],
                                           bank[4 + q][:, :].rearrange("p (t d) -> p t d", t=2), 1.0 / WS,
                                           gate[:, ds(b * D, D)].unsqueeze(1).broadcast_to([P, 2, D]),
                                           ALU.mult, ALU.mult).then_inc(s_dread, 1)
                v.wait_ge(s_dread, 2 + 2 * b + 2)
                xb = x[:, ds(b * TB, TB), :]
                v.tensor_tensor(xb, xb, osum4[:], ALU.add).then_inc(s_xout, 1)
            products(0)
            ln3.modulate(v, 1)
            v.wait_ge(s_gate4, 16)
            with v.Fori(1, B) as b:
                products(b)
                down_out(b - 1)
            down_out(B - 1)

        @block.tensor
        def _(pe):
            def gate_up(b):
                ln3.wait_parts(pe, b)
                for oc in range(IC):
                    w = P if oc < IC - 1 else LASTI
                    wait_apart(pe, s_prod, IC * b + oc + 1, s_passed)
                    for which, sem in ((0, s_gmm), (1, s_umm)):
                        split3(pe, bank[2 * which + oc % 2][0:w, :],
                               [((dec(wdec_hi, which, c, oc), dec(wdec_lo, which, c, oc)),
                                 (hT_hi[:, c, ds(b * S, S)], hT_lo[:, c, ds(b * S, S)])) for c in range(KT)]
                               ).then_inc(sem, 1)

            def down(b):
                pe.wait_ge(s_mlo, 2 + IC * b + IC)
                for q in range(2):
                    pe.wait_ge(s_dread, 2 * b + q + 1)
                    for t in (2 * q, 2 * q + 1):
                        pairs = []
                        for oc in range(IC):
                            w = P if oc < IC - 1 else LASTI
                            tok = b * S + t * P
                            pairs.append(((mT_hi[0:w, oc, ds(tok, P)], mT_lo[0:w, oc, ds(tok, P)]),
                                          (dec(wdec_hi, 2, oc, 0), dec(wdec_lo, 2, oc, 0))))
                        ins = split3(pe, bank[4 + q][:, (t % 2) * D:(t % 2 + 1) * D], pairs)
                    ins.then_inc(s_dmm, 1)
            ln3.tensor(pe, 0)
            gate_up(0)
            ln3.tensor(pe, 1)
            with pe.Fori(1, B) as b:
                gate_up(b)
                down(b - 1)
            down(B - 1)


def host_layout(inputs):
    import numpy as np
    n = {key: np.asarray(v) for key, v in inputs.items()}

    def feat(w):
        return np.ascontiguousarray(w.reshape(-1, P, w.shape[-1]).transpose(1, 0, 2))

    def col(v):
        return v.reshape(-1, P).T

    a = {}
    a["x"] = np.ascontiguousarray(n["L0_attn_x"].reshape(NT, P, D).transpose(1, 0, 2))
    a["cT"] = np.ascontiguousarray(np.stack([n["L0_c"].T, n["L1_c"].T]).reshape(2, KT, P, B)
                                   .transpose(2, 0, 1, 3).reshape(P, -1))
    a["wmod"] = np.ascontiguousarray(np.stack([n["L0_wmod"], n["L1_wmod"]]).reshape(2, KT, P, 6 * D)
                                     .transpose(2, 0, 1, 3))
    qkv = n["L0_attn_qkv_w"]
    a["wqk"] = feat(qkv[:, :QKW])
    a["wv"] = feat(qkv[:, QKW:])
    a["wo"] = feat(n["L0_attn_out_w"])
    a["cols"] = np.ascontiguousarray(np.concatenate(
        [col(n["L0_attn_qkv_b"]), col(n["L0_ffn_amp_b"]), col(n["L0_ffn_ph_b"])]
        + [col(n[f"L0_ffn_{g}"].reshape(-1)) for g in ("ln3_g", "ln3_b", "ln4_g", "ln4_b")]
        + [col(n["L1_attn_b_qkv"]), col(n["L0_ffn_ent_b"].reshape(-1))], axis=1))
    a["slopes"] = np.tile(np.array([1.0 / 2.0 ** (i / 2.0) for i in range(H)], np.float32), (P, 1))
    a["rows"] = np.ascontiguousarray(np.concatenate(
        [n["L0_attn_out_b"], n["L0_ffn_ent_pb"].reshape(-1), n["L0_ffn_path_b"].reshape(-1),
         n["L0_ffn_phase"].reshape(-1), n["L0_ffn_ln4_g"][-1], n["L0_ffn_ln4_b"][-1], n["L1_attn_b_out"]])
        .reshape(1, -1))
    a["amph"] = np.ascontiguousarray(np.stack([feat(n["L0_ffn_amp_w"]), feat(n["L0_ffn_ph_w"])], axis=1))
    a["entwT"] = np.ascontiguousarray(np.stack([feat(w.T) for w in n["L0_ffn_ent_w"]], axis=1))
    a["entpw"] = np.ascontiguousarray(np.stack([feat(w) for w in n["L0_ffn_ent_pw"]], axis=1))
    a["path"] = np.ascontiguousarray(np.stack([np.stack([feat(w) for w in l], axis=1)
                                               for l in n["L0_ffn_path_w"]], axis=1))
    a["wqkv1"] = feat(n["L1_attn_w_qkv"].T)
    a["wout1"] = feat(n["L1_attn_w_out"].T)
    down = np.zeros((IC * P, D), np.int32)
    down[:INTER] = n["L1_ffn_down_idx"].T
    a["idx"] = np.ascontiguousarray(np.concatenate(
        [feat(n["L1_ffn_gate_idx"].T).reshape(P, -1), feat(n["L1_ffn_up_idx"].T).reshape(P, -1),
         feat(down).reshape(P, -1)], axis=1))
    a["lut"] = np.ascontiguousarray(n["L1_ffn_lut"].reshape(1, -1))
    return a


def kernel(**inputs):
    import concourse.bacc as bacc
    from concourse.bass_utils import run_bass_kernel_spmd

    nc = bacc.Bacc("TRN2", target_bir_lowering=False, num_devices=1)
    arrays = {f"in_{name}": a for name, a in host_layout(inputs).items()}
    aps = {name[3:]: nc.dram_tensor(name, a.shape, mybir.dt.from_np(a.dtype), kind="ExternalInput").ap()
           for name, a in arrays.items()}
    aps["out"] = nc.dram_tensor("out", (P, NT, D), F32, kind="ExternalOutput").ap()
    build(nc, aps)
    r = run_bass_kernel_spmd(nc, [arrays], core_ids=[0])
    y = r.results[0]["out"]
    return y.reshape(P, NT, D).transpose(1, 0, 2).reshape(B, S, D)
```

```python
import concourse.bass as bass
from concourse import mybir

F32 = mybir.dt.float32
F16 = mybir.dt.float16
I32 = mybir.dt.int32
ALU = mybir.AluOpType
ACT = mybir.ActivationFunctionType
AX = mybir.AxisListType
ds = bass.ds

P = 128
B, S, D = 4, 512, 256
KT = D // P
TB = S // P
NT = B * TB
H = 16
HD = 128
QKW, VW = 2 * H * HD, H * HD
LE, PWN, EW = 2, 2, 1024
EC = EW // P
INTER = 688
IC = -(-INTER // P)
LASTI = INTER - (IC - 1) * P
LUTN = 16
IDXW = 2 * KT * INTER + IC * D
EPS = 1e-5
WS = 16.0
PS = 16.0
MASKED = 1e30
VALUE_UNITS = B * H
NSTEP = B * H
CHUNK = 1024
C_QKVB = 0
C_AMPB = C_QKVB + 3 * H
C_PHB = C_AMPB + KT
C_LN = C_PHB + KT
C_B1 = C_LN + 4 * LE * KT
C_ENTB = C_B1 + 3 * KT
NCOL = C_ENTB + LE * EC
R_OUTB, R_ENTPB, R_PATHB, R_PHASE, R_LN4G, R_LN4B, R_BOUT = 0, 1, 3, 7, 11, 12, 13
NROW = 14
DCHUNK = IDXW // 4
QTILES = (3, 2, 0, 1)
SOFF = {3: 0, 2: 512, 0: 896, 1: 1024}
SW = 1280
JOFF = {0: 0, 1: 512, 2: 896, 3: 1152}
PT_UNITS = ((1,), (2, 3), (0,))


class Kit:

    def __init__(self, nc):
        self.nc = nc

    def sem(self, name):
        return self.nc.alloc_semaphore(name)

    def at(self, name, shape, dt, offset):
        return self.nc.alloc_sbuf_tensor_at(name, shape, dt, offset=offset)


def wait_apart(e, sem, value, passed):
    e.wait_ge(sem, value)
    if not isinstance(value, int):
        e.sem_inc(passed, 1)


def split3(pe, out, pairs, **kw):
    terms = []
    for (ah, al), (bh, bl) in pairs:
        terms += [(ah, bh), (ah, bl), (al, bh)]
    for i, (a, b) in enumerate(terms):
        ins = pe.matmul(out, a, b, start=(i == 0), stop=(i == len(terms) - 1), **kw)
    return ins


def build(nc, A):
    k = Kit(nc)
    base = nc.sbuf_base + 31 & ~31
    nc.alloc_sbuf_tensor("slab", [P, (nc.sbuf_usable_end - base) // 4 - 24], F32)
    cur = [base]

    def place(name, shape, dt, at=None):
        n = 1
        for d in shape[1:]:
            n *= d
        n *= 2 if dt == F16 else 4
        if at is None:
            at = cur[0]
            cur[0] = (at + n + 31) & ~31
        assert at + n <= nc.sbuf_usable_end, (name, at + n)
        t = k.at(name, shape, dt, at)
        return t, at, at + ((n + 31) & ~31)

    def new(name, shape, dt):
        return place(name, shape, dt)[0]

    def region(nbytes):
        at = cur[0]
        cur[0] = (at + nbytes + 31) & ~31
        return at

    x = new("x", [P, NT, D], F32)
    hT_hi = new("hT_hi", [P, KT, B * S], F16)
    hT_lo = new("hT_lo", [P, KT, B * S], F16)
    cols = new("cols", [P, NCOL], F32)
    modT = new("modT", [P, 2, 12, B], F32)
    ident = new("ident", [P, P], F32)
    ones16 = new("ones16", [1, P], F16)
    mhalf = new("mhalf", [P, NT], F32)
    stats = new("stats", [P, NT, 6], F32)
    mean = new("mean", [P, NT], F32)
    half_var = new("half_var", [P, 4, NT], F32)
    vareps = new("vareps", [P, NT], F32)
    rstd = new("rstd", [P, NT], F32)
    gate = new("gate", [P, B * D], F32)
    slopes = new("slopes", [P, H], F32)
    bcol1 = new("bcol1", [P, 3 * KT], F32)
    entry = new("entry", [P, LUTN], F32)
    lutb = new("lutb", [P, 3, LUTN], F32)
    lut16 = new("lut16", [P, LUTN], F16)

    BIG = region(128 * 1024)
    DEC = region(2 * IDXW * 2)
    WORK = region(21 * 1024)
    end = cur[0]
    assert end <= nc.sbuf_usable_end, end - nc.sbuf_usable_end

    def layout(start):
        p = [start]

        def f(name, shape, dt):
            t, _, p[0] = place(name, shape, dt, p[0])
            return t
        f.pos = p
        return f

    big0 = layout(BIG)
    wqk_hi = big0("wqk_hi", [P, KT, QKW], F16)
    wqk_lo = big0("wqk_lo", [P, KT, QKW], F16)
    WV = big0.pos[0]
    wv_hi = big0("wv_hi", [P, KT, VW], F16)
    wv_lo = big0("wv_lo", [P, KT, VW], F16)
    WO = big0.pos[0]
    wo_hi = big0("wo_hi", [P, H, D], F16)
    wo_lo = big0("wo_lo", [P, H, D], F16)
    v_hi = big0("v_hi", [P, TB, VW], F16)
    v_lo = big0("v_lo", [P, TB, VW], F16)
    STAGE = big0.pos[0]
    stg = layout(STAGE)
    NSTAGE = 4
    stage = [stg(f"stage{i}", [P, KT * CHUNK], F32) for i in range(NSTAGE)]

    decoded = layout(DEC)
    wdec_hi = decoded("wdec_hi", [P, IDXW], F16)
    wdec_lo = decoded("wdec_lo", [P, IDXW], F16)
    idx32 = layout(DEC)("idx32", [P, IDXW], I32)
    wk0 = layout(WORK)
    q_hi = wk0("q_hi", [P, S], F16)
    q_lo = wk0("q_lo", [P, S], F16)
    k_hi = wk0("k_hi", [P, S], F16)
    k_lo = wk0("k_lo", [P, S], F16)
    prob = wk0("prob", [P, SW], F32)
    pt_hi = wk0("pt_hi", [P, SW], F16)
    pt_lo = wk0("pt_lo", [P, SW], F16)
    ctx_hi = wk0("ctx_hi", [P, S], F16)
    ctx_lo = wk0("ctx_lo", [P, S], F16)
    alibi = wk0("alibi", [P, S], F32)
    dist = wk0("dist", [P, S], F32)
    smin = wk0("smin", [P, TB], F32)
    ssum = wk0("ssum", [P, TB], F32)
    sinv = wk0("sinv", [P, TB], F32)
    assert wk0.pos[0] <= end, wk0.pos[0] - end
    before = layout(DEC)
    xq0 = [before(f"xq0_{i}", [P, TB, D], F32) for i in range(2)]
    wkm = layout(WORK)
    wmod = wkm("wmod", [P, KT, 6 * D], F32)
    cT = wkm("cT", [P, 2 * KT * B], F32)
    sil = wkm("sil", [P, 2 * KT * B], F32)
    sig = wkm("sig", [P, 2 * KT * B], F32)
    gcol = wkm("gcol", [P, 2 * 2 * B * KT], F32)
    gsgn = wkm("gsgn", [P, 2 * 2 * B * KT], F32)
    grow = wkm("grow", [2 * 2 * B * KT, P], F32)
    tq0 = [wkm(f"tq0_{i}", [P, KT, S], F32) for i in range(2)]
    assert wkm.pos[0] <= end, wkm.pos[0] - end
    bank = [nc.alloc_psum_tensor(f"bank{i}", [P, 512], F32) for i in range(8)]
    gate_rows = nc.dram_tensor("gate_rows", [2 * 2 * B * KT, P], F32, kind="Internal").ap()

    SA, CA, GA, SB, CB, GB = (KT * i for i in range(6))

    s_passed = k.sem("waits_passed")

    def load_gate(sp, layer, which, sem):
        r0 = (layer * 2 + which) * B * KT
        src = gate_rows[r0:r0 + B * KT, :].rearrange("r d -> (r d)")
        return sp.dma_start(gate[:], bass.AP(tensor=src.tensor, offset=src.offset, ap=[[0, P], [1, B * D]])
                            ).then_inc(sem, 16)

    class LayerNorm:

        def __init__(self, tag, xq, tq, banks, layer, scale, shift):
            self.xq, self.tq, self.banks = xq, tq, banks
            self.layer, self.scale, self.shift = layer, scale, shift
            self.stats, self.vareps, self.rstd, self.xn, self.turned, self.tmp, self.hi, self.lo = (
                k.sem(f"{tag}_{n}") for n in ("stats", "vareps", "rstd", "xn", "turned", "modulated", "hi", "lo"))

        def free_slots(self, v):
            v.sem_inc(self.turned, 2 * KT)
            v.sem_inc(self.tmp, KT)
            v.sem_inc(self.lo, 2 * KT)

        def vector(self, v, b0):
            self.normalise(v, b0)
            self.modulate(v, b0)

        def normalise(self, v, b0):
            for sl in range(2):
                b = 2 * b0 + sl
                for t in range(TB):
                    v.bn_stats(stats[:, b * TB + t, :], x[:, b * TB + t, :]).then_inc(self.stats, 1)
                v.wait_ge(self.stats, (TB + 5) * b + TB)
                combine_stats(v, self.stats, b, (TB + 5) * b + TB, EPS).then_inc(self.vareps, 1)
            for sl in range(2):
                b = 2 * b0 + sl
                v.wait_ge(self.rstd, b + 1)
                v.wait_ge(self.turned, KT * b + KT)
                for t in range(TB):
                    v.tensor_scalar(self.xq[sl][:, t, :], x[:, b * TB + t, :], mean[:, ds(b * TB + t, 1)],
                                    rstd[:, ds(b * TB + t, 1)], ALU.subtract, ALU.mult).then_inc(self.xn, 1)

        def modulate(self, v, b0):
            for sl in range(2):
                b = 2 * b0 + sl
                for c in range(KT):
                    v.wait_ge(self.turned, 2 * KT + KT * b + c + 1)
                    v.wait_ge(self.lo, KT * b + c + 1)
                    v.tensor_scalar(self.tq[sl][:, c, :], self.banks[c][:, :],
                                    modT[:, self.layer, self.scale + c, ds(b, 1)],
                                    modT[:, self.layer, self.shift + c, ds(b, 1)], ALU.mult, ALU.add
                                    ).then_inc(self.tmp, 1)

        def gpsimd(self, g, b0):
            self.inverse(g, b0)
            self.split_lo(g, b0)

        def inverse(self, g, b0):
            for sl in range(2):
                b = 2 * b0 + sl
                g.wait_ge(self.vareps, b + 1)
                g.tensor_tensor(rstd[:, ds(b * TB, TB)], vareps[:, ds(b * TB, TB)], mhalf[:, ds(b * TB, TB)],
                                ALU.pow).then_inc(self.rstd, 1)

        def split_lo(self, g, b0):
            for sl in range(2):
                b = 2 * b0 + sl
                for c in range(KT):
                    g.wait_ge(self.hi, KT * b + c + 1)
                    g.tensor_tensor(hT_lo[:, c, ds(b * S, S)], self.tq[sl][:, c, :],
                                    hT_hi[:, c, ds(b * S, S)], ALU.subtract).then_inc(self.lo, 1)

        def scalar(self, act, b0):
            for sl in range(2):
                b = 2 * b0 + sl
                for c in range(KT):
                    act.wait_ge(self.tmp, KT + KT * b + c + 1)
                    act.activation(hT_hi[:, c, ds(b * S, S)], self.tq[sl][:, c, :], ACT.Copy).then_inc(self.hi, 1)

        def tensor(self, pe, b0):
            for sl in range(2):
                b = 2 * b0 + sl
                for c in range(KT):
                    pe.wait_ge(self.tmp, KT * b + c + 1)
                    for t in range(TB):
                        if c == 0:
                            pe.wait_ge(self.xn, b * TB + t + 1)
                        ins = pe.transpose(self.banks[c][:, t * P:(t + 1) * P],
                                           self.xq[sl][:, t, c * P:(c + 1) * P], ident[:, :])
                    ins.then_inc(self.turned, 1)

        def wait_parts(self, pe, b):
            pe.wait_ge(self.lo, 2 * KT + KT * b + KT)

    def combine_stats(v, sem, b, done, eps, negative=None):
        tiles = ds(b * TB, TB)
        even_mean, even_m2 = stats[:, tiles, 1], stats[:, tiles, 2]
        odd_mean, odd_m2 = stats[:, tiles, 4], stats[:, tiles, 5]
        dif, tot, m2, dd = (half_var[:, i, tiles] for i in range(4))
        v.tensor_tensor(dif, even_mean, odd_mean, ALU.subtract).then_inc(sem, 1)
        v.tensor_tensor(tot, even_mean, odd_mean, ALU.add).then_inc(sem, 1)
        v.scalar_tensor_tensor(m2, even_m2, D * eps, odd_m2, ALU.add, ALU.add).then_inc(sem, 1)
        v.wait_ge(sem, done + 2)
        out, half = (mean, 0.5) if negative is None else (negative, -0.5)
        v.tensor_scalar(out[:, tiles], tot, half, None, ALU.mult).then_inc(sem, 1)
        v.scalar_tensor_tensor(dd, dif, 0.25, dif, ALU.mult, ALU.mult).then_inc(sem, 1)
        v.wait_ge(sem, done + 5)
        return v.scalar_tensor_tensor(vareps[:, tiles], m2, 1.0 / D, dd, ALU.mult, ALU.add)

    s_x, s_cols, s_c, s_wmod = (k.sem(n) for n in ("x_in", "cols_in", "c_in", "wmod_in"))
    s_wlog = k.sem("w_lo_gpsimd")
    s_wmod0 = k.sem("wmod_first_in")
    s_stage = [k.sem(f"stage_in{i}") for i in range(NSTAGE)]
    s_whi, s_wlo = k.sem("w_hi"), k.sem("w_lo")
    s_idx, s_lut, s_mread = k.sem("idx_in"), k.sem("lut_in"), k.sem("mod_group_read")
    s_const, s_sig, s_sil, s_modp, s_mod, s_gcol, s_gturn, s_grow, s_gout = (
        k.sem(n) for n in ("consts", "sigmoid", "silu", "mod_psum", "mod_done", "gate_cols", "gate_turned",
                           "gate_row", "gate_out"))
    s_vmm, s_vhi, s_vlo = (k.sem(n) for n in ("v_mm", "v_hi_done", "v_lo_done"))
    ln0 = LayerNorm("ln0", xq0, tq0, bank[2:4], 0, CA, SA)
    chunks = [(A["wv"], c, wv_hi, wv_lo, 1.0) for c in range(0, VW, CHUNK)]
    chunks += [(A["wqk"], c, wqk_hi, wqk_lo, -1.0 if c < H * HD else 1.0) for c in range(0, QKW, CHUNK)]
    chunks[3:3] = [(A["wo"], c, wo_hi, wo_lo, 1.0) for c in range(0, H, H // 2)]
    ON_GPSIMD = (3, 4)

    MOD_GROUPS = ((0, (0, 1, 2, 3)), (0, tuple(range(4, 12))), (1, (4, 5, 10, 11)), (1, (0, 1, 2, 3, 6, 7, 8, 9)))

    def chunk_view(t, c):
        if t is wo_hi or t is wo_lo:
            return t[:, c:c + H // 2, :]
        return t[:, :, c:c + CHUNK]

    def stage_view(i, t):
        if t is wo_hi or t is wo_lo:
            return stage[i % NSTAGE][:, :].rearrange("p (h n) -> p h n", h=H // 2)
        return stage[i % NSTAGE][:, :].rearrange("p (k n) -> p k n", k=KT)

    with nc.Block() as block:
        @block.sync
        def _(sp):
            sp.dma_start(cT[:], A["cT"]).then_inc(s_c, 16)
            early = len(MOD_GROUPS[0][1]) * P
            sp.dma_start(wmod[:, :, 0:early], A["wmod"][:, 0, :, 0:early]).then_inc(s_wmod0, 16)
            sp.dma_start(x[:], A["x"]).then_inc(s_x, 16)
            for i, (src, c, hi, lo, sign) in enumerate(chunks):
                if i >= NSTAGE:
                    if i - NSTAGE in ON_GPSIMD:
                        sp.wait_ge(s_wlog, 2 + 2 * ON_GPSIMD.index(i - NSTAGE))
                    else:
                        sp.wait_ge(s_wlo, 1 + sum(j not in ON_GPSIMD for j in range(i - NSTAGE)))
                view = src[:, c:c + H // 2, :] if hi is wo_hi else src[:, :, c:c + CHUNK]
                sp.dma_start(stage_view(i, hi), view).then_inc(s_stage[i % NSTAGE], 16)
                if i == 0:
                    sp.dma_start(wmod[:, :, early:], A["wmod"][:, 0, :, early:]).then_inc(s_wmod, 16)
                if i == NSTAGE + 1:
                    sp.wait_ge(s_modp, 2)
                    sp.dma_start(wmod[:], A["wmod"][:, 1]).then_inc(s_wmod, 16)
            sp.dma_start(cols[:], A["cols"]).then_inc(s_cols, 16)
            sp.dma_start(slopes[:], A["slopes"]).then_inc(s_cols, 16)
            sp.wait_ge(ln0.turned, 2 * KT + KT * B)
            sp.dma_start(idx32[:], A["idx"]).then_inc(s_idx, 16)
            sp.dma_start(lutb[:, 0, :], bass.AP(tensor=A["lut"].tensor, offset=0, ap=[[0, P], [1, LUTN]])
                         ).then_inc(s_lut, 16)
            sp.wait_ge(s_grow, 1)
            sp.dma_start(gate_rows, grow[:]).then_inc(s_gout, 16)
            sp.wait_ge(s_gout, 16)
            load_gate(sp, 0, 0, s_gout)
            sp.wait_ge(s_gout, 32)
            sp.wait_ge(s_cols, 32)

        @block.gpsimd
        def _(g):
            g.memset(ident[:], 0.0).then_inc(s_const, 1)
            for i in range(LUTN):
                g.memset(entry[:, i:i + 1], float(i)).then_inc(s_const, 1)
            g.memset(ones16[:], 1.0).then_inc(s_const, 1)
            g.memset(mhalf[:], -0.5).then_inc(s_const, 1)
            g.wait_ge(s_const, LUTN + 3)
            g.affine_select(out=ident[:], in_=ident[:], pattern=[[-1, P]], compare_op=ALU.not_equal, fill=1.0,
                            base=0, channel_multiplier=1).then_inc(s_const, 1)

            def chunk_lo(n):
                i = ON_GPSIMD[n]
                src, c, hi, lo, sign = chunks[i]
                g.wait_ge(s_whi, i + 1)
                g.tensor_scalar(stage_view(i, hi), stage_view(i, hi), sign * WS, 1.0, ALU.mult, ALU.mult
                                ).then_inc(s_wlog, 1)
                g.wait_ge(s_wlog, 2 * n + 1)
                g.tensor_tensor(chunk_view(lo, c), stage_view(i, hi), chunk_view(hi, c), ALU.subtract
                                ).then_inc(s_wlog, 1)
            ln0.gpsimd(g, 0)
            ln0.inverse(g, 1)
            chunk_lo(0)
            ln0.split_lo(g, 1)
            chunk_lo(1)

        def chunk_parts(e, i):
            src, c, hi, lo, sign = chunks[i]
            if e is nc.scalar:
                e.wait_ge(s_stage[i % NSTAGE], 16 * (i // NSTAGE + 1))
                e.activation(chunk_view(hi, c), stage_view(i, hi), ACT.Copy, scale=sign * WS).then_inc(s_whi, 1)
            else:
                e.wait_ge(s_whi, i + 1)
                e.scalar_tensor_tensor(chunk_view(lo, c), stage_view(i, hi), sign * WS, chunk_view(hi, c),
                                       ALU.mult, ALU.subtract).then_inc(s_wlo, 1)
        vring = bank[0:2] + bank[6:8]
        VCH = 2
        LATE = 4
        first_values = [(u // TB, u % TB) for u in range(3 * TB)]

        @block.scalar
        def _(act):
            act.preload_act_table(ACT.Exp)
            act.wait_ge(s_c, 16)
            act.activation(sig[:], cT[:], ACT.Exp, scale=-1.0).then_inc(s_sig, 1)
            chunk_parts(act, 0)
            chunk_parts(act, 1)
            ln0.scalar(act, 0)
            for i in range(VCH, len(chunks)):
                chunk_parts(act, i)
                if i == LATE:
                    ln0.scalar(act, 1)
                for u in (2 * (i - VCH), 2 * (i - VCH) + 1):
                    g, tt = first_values[u]
                    act.wait_ge(s_vmm, u + 1)
                    act.activation(v_hi[:, tt, g * 512:(g + 1) * 512], vring[u % 4][:, :], ACT.Copy
                                   ).then_inc(s_vhi, 1)

        @block.tensor
        def _(pe):
            def modulation(i):
                layer, tiles = MOD_GROUPS[i]
                pe.wait_ge(*((s_wmod, 16 * (layer + 1)) if i > 0 else (s_wmod0, 16)))
                if i >= 2:
                    pe.wait_ge(s_mread, i - 1)
                for j in tiles:
                    for c in range(KT):
                        ins = pe.matmul(bank[4 + i % 2][:, j * B:(j + 1) * B], wmod[:, c, j * P:(j + 1) * P],
                                        sil[:, (layer * KT + c) * B:(layer * KT + c + 1) * B],
                                        start=(c == 0), stop=(c == KT - 1))
                ins.then_inc(s_modp, 1)
            pe.wait_ge(s_sil, 1)
            modulation(0)
            pe.wait_ge(s_const, LUTN + 4)
            ln0.tensor(pe, 0)
            modulation(1)
            ln0.wait_parts(pe, 0)
            for u, (g, tt) in enumerate(first_values):
                if u == 4:
                    modulation(2)
                if u == 6:
                    pe.wait_ge(s_gcol, 1)
                    pe.transpose(bank[4][0:32, 0:P], gcol[:, :], ident[:, :]).then_inc(s_gturn, 1)
                if u == 2 * (LATE - VCH):
                    ln0.tensor(pe, 1)
                pe.wait_ge(s_wlo, 1 + g // 2)
                if u >= 4:
                    pe.wait_ge(s_vlo, u - 3)
                split3(pe, vring[u % 4][:, :],
                       [((hT_hi[:, c, tt * P:(tt + 1) * P], hT_lo[:, c, tt * P:(tt + 1) * P]),
                         (wv_hi[:, c, g * 512:(g + 1) * 512], wv_lo[:, c, g * 512:(g + 1) * 512]))
                        for c in range(KT)]).then_inc(s_vmm, 1)
            modulation(3)

        @block.vector
        def _(v):
            v.wait_ge(s_sig, 1)
            v.tensor_scalar(sig[:], sig[:], 1.0, None, ALU.add).then_inc(s_sig, 1)
            v.wait_ge(s_sig, 2)
            v.reciprocal(sig[:], sig[:]).then_inc(s_sig, 1)
            v.wait_ge(s_sig, 3)
            v.tensor_tensor(sil[:], sig[:], cT[:], ALU.mult).then_inc(s_sil, 1)

            def modulation(i, done):
                layer, tiles = MOD_GROUPS[i]
                v.wait_ge(s_modp, i + 1)
                for j in tiles[::2]:
                    v.tensor_copy(modT[:, layer, j:j + 2, :].rearrange("p j b -> p (j b)"),
                                  bank[4 + i % 2][:, j * B:(j + 2) * B]).then_inc(s_mod, 1)
                    done += 1
                for j in (CA, CB):
                    if j in tiles:
                        v.wait_ge(s_mod, done)
                        v.tensor_scalar(modT[:, layer, j:j + KT, :], modT[:, layer, j:j + KT, :], 1.0, None,
                                        ALU.add).then_inc(s_mod, 1)
                        done += 1
                v.wait_ge(s_mod, done)
                v.sem_inc(s_mread, 1)
                return done
            v.wait_ge(s_x, 16)
            v.wait_ge(s_const, LUTN + 4)
            ln0.free_slots(v)
            ln0.normalise(v, 0)
            done = modulation(0, 0)
            ln0.modulate(v, 0)
            chunk_parts(v, 0)
            chunk_parts(v, 1)
            chunk_parts(v, 2)
            ln0.normalise(v, 1)
            done = modulation(1, done)

            def gates(done):
                for layer in range(2):
                    for n, j in enumerate((GA, GB)):
                        o = (layer * 2 + n) * B * KT
                        v.tensor_copy(gcol[:, o:o + B * KT].rearrange("p (b c) -> p b c", b=B),
                                      modT[:, layer, j:j + KT, :].rearrange("p c b -> p b c")).then_inc(s_mod, 1)
                done += 4
                v.wait_ge(s_mod, done)
                v.tensor_scalar(gsgn[:], gcol[:], 0.0, 2.0, ALU.is_ge, ALU.mult).then_inc(s_mod, 1)
                v.wait_ge(s_mod, done + 1)
                v.scalar_tensor_tensor(gcol[:], gsgn[:], -1.0, gcol[:], ALU.add, ALU.mult).then_inc(s_mod, 1)
                v.wait_ge(s_mod, done + 2)
                v.tensor_scalar(gcol[:], gcol[:], 0.25, None, ALU.max).then_inc(s_mod, 1)
                v.wait_ge(s_mod, done + 3)
                v.scalar_tensor_tensor(gcol[:], gsgn[:], -1.0, gcol[:], ALU.add, ALU.mult).then_inc(s_gcol, 1)
                return done + 3
            for i in range(VCH, len(chunks)):
                if i > 2 and i not in ON_GPSIMD:
                    chunk_parts(v, i)
                if i == LATE:
                    ln0.modulate(v, 1)
                for u in (2 * (i - VCH), 2 * (i - VCH) + 1):
                    g, tt = first_values[u]
                    v.wait_ge(s_vhi, u + 1)
                    v.tensor_tensor(v_lo[:, tt, g * 512:(g + 1) * 512], vring[u % 4][:, :],
                                    v_hi[:, tt, g * 512:(g + 1) * 512], ALU.subtract).then_inc(s_vlo, 1)
                if i == VCH + 1:
                    done = gates(modulation(2, done))
                if i == VCH + 2:
                    v.wait_ge(s_gturn, 1)
                    v.tensor_copy(grow[:], bank[4][0:32, 0:P]).then_inc(s_grow, 1)
            modulation(3, done)

    pr, sc, tr, oa = bank[0:2], bank[2:4], bank[4:6], bank[6:8]
    turned_bank = (tr[1], pr[1], tr[0])
    score_out = {3: sc[0][:, 0:512], 2: sc[1][:, 0:384], 0: sc[1][:, 384:512], 1: tr[1][:, 0:256]}
    st1 = layout(STAGE)
    bcol = st1("bcol", [P, 3 * H], F32)
    idx16 = st1("idx16", [P, IDXW], F16)
    onehot = st1("onehot", [P, 2, DCHUNK], F16)
    outb = st1("outb", [P, D], F32)
    gob = st1("gob", [P, B, D], F32)
    osum = st1("osum", [P, TB, D], F32)
    early = layout(WV)
    entwT = [early("entwT0", [P, EC, D], F32)]
    entpw = [early("entpw0", [P, EC, D], F32)]
    assert early.pos[0] <= WO
    tail = layout(st1.pos[0])
    rows = tail("rows", [P, 6, D], F32)
    amph = tail("amph", [P, 2, KT, D], F32)
    assert tail.pos[0] <= DEC
    s_rows2, s_amph = (k.sem(n) for n in ("rows_in", "amph_in"))
    s_ent = [k.sem(f"ent{l}_in") for l in range(LE)]

    s_dec = k.sem("decoded")
    s_rows, s_bcol, s_dist, s_gob = (k.sem(n) for n in ("outb_in", "bias_cols", "dist", "gate_bias"))
    (s_qmm, s_qhi, s_qlo, s_kmm, s_khi, s_klo) = (
        k.sem(n) for n in ("q_mm", "q_hi_done", "q_lo_done", "k_mm",
                           "k_hi_done", "k_lo_done"))
    (s_alibi, s_scored, s_masked, s_exp, s_inv, s_norm, s_turned, s_pthi, s_ptlo) = (
        k.sem(n) for n in ("alibi_ready", "scored", "masked", "exp_done", "sum_inverse", "normalised",
                           "prob_turned", "pt_hi_done", "pt_lo_done"))
    s_cmm, s_chi, s_clo, s_omm, s_oread, s_xadd = (
        k.sem(n) for n in ("ctx_mm", "ctx_hi_done", "ctx_lo_done", "out_mm", "out_read", "x_added"))

    FIRST = 0

    def run_steps(e, step):
        def group(b, g):
            known = isinstance(g, int)
            if known and g == 0:
                values = (b, 3)
            elif isinstance(b, int) and b == B - 1:
                values = None
            else:
                values = (b + 1, g - 1)
            for r in range(4):
                n = H * b + 4 * g + r
                next_of = (b, 4 * g + r + 1)
                if r == 3 and not (known and g == 0):
                    next_of = ((4 * b + g + 1) // 4, (4 * g + 4) % H)
                prev_h = 4 * g + r - 1
                if known and g == 0 and r == 0:
                    prev_h = H - 1
                if isinstance(n, int) and n == 0:
                    prev_h = None
                if isinstance(n, int) and n == NSTEP - 1:
                    next_of = None
                step(n, r, b=b, m=4 * b + g, next_of=next_of, prev_h=prev_h, values=values,
                     boundary=known and g == 0 and r == 0 and prev_h is not None,
                     out_first=known and g == 0 and r == 1, last=False)

        group(0, 0)
        with e.Fori(0, B - 1) as b:
            with e.Fori(1, 4) as g:
                group(b, g)
            group(b + 1, 0)
        with e.Fori(1, 3) as g:
            group(B - 1, g)
        group(B - 1, 3)
        step(NSTEP, 0, b=B, m=None, next_of=None, prev_h=H - 1, values=None, boundary=True, out_first=False,
             last=True)

    with nc.Block() as block:
        @block.sync
        def _(sp):
            sp.dma_start(outb[:], bass.AP(tensor=A["rows"].tensor, offset=R_OUTB * D, ap=[[0, P], [1, D]])
                         ).then_inc(s_rows, 16)
            sp.wait_ge(s_rows, 16)
            for r0, n in ((R_PHASE, 4), (R_LN4G, 2)):
                sp.dma_start(rows[:, r0 - R_PHASE:r0 - R_PHASE + n, :].rearrange("p r d -> p (r d)"),
                             bass.AP(tensor=A["rows"].tensor, offset=r0 * D, ap=[[0, P], [1, n * D]])
                             ).then_inc(s_rows2, 16)
            sp.dma_start(amph[:], A["amph"]).then_inc(s_amph, 16)
            sp.wait_ge(s_vlo, VALUE_UNITS)
            sp.dma_start(entwT[0][:], A["entwT"][:, 0]).then_inc(s_ent[0], 16)
            sp.dma_start(entpw[0][:], A["entpw"][:, 0]).then_inc(s_ent[0], 16)

        @block.gpsimd
        def _(g):
            g.iota(dist[:], pattern=[[-1, S]], base=S - P, channel_multiplier=1,
                   allow_small_or_imprecise_dtypes=True).then_inc(s_dist, 1)
            g.wait_ge(s_dist, 1)
            g.affine_select(out=dist[:], in_=dist[:], pattern=[[-1, S]], compare_op=ALU.is_ge, fill=MASKED,
                            base=S - P, channel_multiplier=1).then_inc(s_dist, 1)
            g.tensor_scalar(slopes[:], slopes[:], WS * WS, 1.0, ALU.mult, ALU.mult).then_inc(s_dist, 1)
            g.wait_ge(s_dist, 3)

            def alibi_of(head):
                g.tensor_tensor(alibi[:], dist[:], slopes[:, ds(head, 1)].broadcast_to([P, S]), ALU.mult
                                ).then_inc(s_alibi, 1)

            alibi_of(0)
            g.wait_ge(s_rows, 16)
            for b in range(B):
                g.tensor_tensor(gob[:, b, :], gate[:, b * D:(b + 1) * D], outb[:], ALU.mult).then_inc(s_gob, 1)

            def step(n, r, b, next_of, boundary, last, **_):
                if not last:
                    wait_apart(g, s_inv, n + 1, s_passed)
                    for t in QTILES:
                        part = prob[:, SOFF[t]:SOFF[t] + (t + 1) * P]
                        g.tensor_scalar(part, part, sinv[:, t:t + 1], PS, ALU.mult, ALU.mult
                                        ).then_inc(s_norm, 1)
                if next_of is not None:
                    alibi_of(next_of[1])
                if boundary:
                    xb = x[:, ds(TB * (b - 1), TB), :]
                    for t in range(TB):
                        xt = x[:, TB * (b - 1) + t, :]
                        if t == 0:
                            g.wait_ge(s_gob, B)
                        g.tensor_tensor(xt, xt, gob[:, b - 1, :], ALU.add).then_inc(s_xadd, 1)
                    g.wait_ge(s_oread, 2 * b)
                    wait_apart(g, s_xadd, 5 * (b - 1) + TB, s_passed)
                    g.tensor_tensor(xb, xb, osum[:], ALU.add).then_inc(s_xadd, 1)
            run_steps(g, step)

        @block.scalar
        def _(act):
            act.preload_act_table(ACT.Exp)
            act.wait_ge(s_bcol, 3)
            def value_parts(tt, g, u):
                act.wait_ge(s_vmm, u + 1)
                return lambda bk: act.activation(v_hi[:, tt, ds(g * 512, 512)], bk[:, :], ACT.Copy
                                                 ).then_inc(s_vhi, 1)
            def q_part(n1, head):
                act.wait_ge(s_qmm, n1 + 1)
                act.activation(q_hi[:], pr[1][:, :], ACT.Identity, bias=bcol[:, ds(head, 1)]).then_inc(s_qhi, 1)

            def k_part(n1, head):
                act.wait_ge(s_kmm, n1 + 1)
                act.activation(k_hi[:], pr[0][:, :], ACT.Identity, bias=bcol[:, ds(H + head, 1)]
                               ).then_inc(s_khi, 1)
            q_part(0, 0)
            k_part(0, 0)
            act.wait_ge(s_idx, 16)
            act.activation(idx16[:], idx32[:], ACT.Copy).then_inc(s_idx, 1)

            def step(n, r, next_of, prev_h, values, last, **_):
                if not last:
                    for i, t in enumerate(QTILES):
                        act.wait_ge(s_masked, 4 * n + i + 1)
                        part = prob[:, SOFF[t]:SOFF[t] + (t + 1) * P]
                        act.activation(part, part, ACT.Exp, bias=smin[:, t:t + 1], scale=-1.0,
                                       accum_out=ssum[:, t:t + 1]).then_inc(s_exp, 1)
                if prev_h is not None:
                    act.wait_ge(s_cmm, n)
                    act.activation(ctx_hi[:], pr[0][:, :], ACT.Identity, bias=bcol[:, ds(2 * H + prev_h, 1)]
                                   ).then_inc(s_chi, 1)
                if next_of is not None:
                    q_part(n + 1, next_of[1])
                if values is not None:
                    value_parts(r, values[1], n + 12)(tr[0])
                if next_of is not None:
                    k_part(n + 1, next_of[1])
                if not last:
                    for u, unit in enumerate(PT_UNITS):
                        act.wait_ge(s_turned, 3 * n + u + 1)
                        w = sum((4 - j) * P for j in unit)
                        act.activation(pt_hi[:, JOFF[unit[0]]:JOFF[unit[0]] + w], turned_bank[u][:, 0:w], ACT.Copy
                                       ).then_inc(s_pthi, 1)
            run_steps(act, step)

        @block.vector
        def _(v):
            v.tensor_scalar(bcol[:, 0:H], cols[:, C_QKVB:C_QKVB + H], -WS, None, ALU.mult).then_inc(s_bcol, 1)
            v.tensor_scalar(bcol[:, H:2 * H], cols[:, C_QKVB + H:C_QKVB + 2 * H], WS, None, ALU.mult
                            ).then_inc(s_bcol, 1)
            v.tensor_scalar(bcol[:, 2 * H:3 * H], cols[:, C_QKVB + 2 * H:C_QKVB + 3 * H], WS * PS, None,
                            ALU.mult).then_inc(s_bcol, 1)
            v.wait_ge(s_bcol, 3)

            def value_lo(tt, g, u, bk):
                v.wait_ge(s_vhi, u + 1)
                v.tensor_tensor(v_lo[:, tt, ds(g * 512, 512)], bk[:, :], v_hi[:, tt, ds(g * 512, 512)],
                                ALU.subtract).then_inc(s_vlo, 1)
            def q_low(n1, head):
                v.wait_ge(s_qhi, n1 + 1)
                v.scalar_tensor_tensor(q_lo[:], pr[1][:, :], bcol[:, ds(head, 1)], q_hi[:], ALU.add,
                                       ALU.subtract).then_inc(s_qlo, 1)

            def k_low(n1, head):
                v.wait_ge(s_khi, n1 + 1)
                v.scalar_tensor_tensor(k_lo[:], pr[0][:, :], bcol[:, ds(H + head, 1)], k_hi[:], ALU.add,
                                       ALU.subtract).then_inc(s_klo, 1)
            q_low(0, 0)
            k_low(0, 0)
            v.wait_ge(s_lut, 16)
            v.tensor_scalar(lutb[:, 0, :], lutb[:, 0, :], WS, None, ALU.mult).then_inc(s_lut, 1)
            v.wait_ge(s_lut, 17)
            v.tensor_copy(lut16[:], lutb[:, 0, :]).then_inc(s_lut, 1)
            v.wait_ge(s_lut, 18)
            v.tensor_copy(lutb[:, 1, :], lut16[:]).then_inc(s_lut, 1)
            v.wait_ge(s_lut, 19)
            v.tensor_tensor(lutb[:, 2, :], lutb[:, 0, :], lutb[:, 1, :], ALU.subtract).then_inc(s_lut, 1)
            v.wait_ge(s_lut, 20)

            def weights(part, r):
                return (wdec_hi, wdec_lo)[part][:, r * DCHUNK:(r + 1) * DCHUNK]

            def decode_hot(n, m, r):
                if isinstance(m, int) and m == FIRST:
                    v.wait_ge(s_idx, 17)
                else:
                    v.wait_ge(s_dec, 4 * n - 8)
                for part in range(2):
                    out = onehot[:, part, :] if not (isinstance(m, int) and m == FIRST) else weights(part, r)
                    v.tensor_scalar(out, idx16[:, r * DCHUNK:(r + 1) * DCHUNK],
                                    entry[:, ds(m, 1)], lutb[:, 1 + part, ds(m, 1)], ALU.is_equal, ALU.mult
                                    ).then_inc(s_dec, 1)

            def decode_add(n, m, part, r):
                if not (isinstance(m, int) and m == FIRST):
                    w = weights(part, r)
                    v.wait_ge(s_dec, 4 * n - 8 + 2)
                    v.tensor_tensor(w, w, onehot[:, part, :], ALU.add).then_inc(s_dec, 1)


            def step(n, r, b, m, next_of, prev_h, values, boundary, last, **_):
                if not last:
                    v.wait_ge(s_alibi, n + 1)
                    for i, t in enumerate(QTILES):
                        w = (t + 1) * P
                        wait_apart(v, s_scored, 4 * n + (1, 3, 3, 4)[i], s_passed)
                        v.tensor_tensor_reduce(prob[:, SOFF[t]:SOFF[t] + w], score_out[t], alibi[:, S - w:S],
                                               1.0 / (WS * WS), 3e38, ALU.add, ALU.min, smin[:, t:t + 1]
                                               ).then_inc(s_masked, 1)
                    decode_hot(n, m, r)
                    v.wait_ge(s_exp, 4 * n + 4)
                    v.reciprocal(sinv[:], ssum[:]).then_inc(s_inv, 1)
                if prev_h is not None:
                    v.wait_ge(s_chi, n)
                    v.scalar_tensor_tensor(ctx_lo[:], pr[0][:, :], bcol[:, ds(2 * H + prev_h, 1)], ctx_hi[:],
                                           ALU.add, ALU.subtract).then_inc(s_clo, 1)
                if next_of is not None:
                    q_low(n + 1, next_of[1])
                if not last:
                    decode_add(n, m, 0, r)
                if values is not None:
                    value_lo(r, values[1], n + 12, tr[0])
                if not last:
                    decode_add(n, m, 1, r)
                if next_of is not None:
                    k_low(n + 1, next_of[1])
                if not last:
                    for u, unit in enumerate(PT_UNITS):
                        v.wait_ge(s_pthi, 3 * n + u + 1)
                        w = sum((4 - j) * P for j in unit)
                        o = JOFF[unit[0]]
                        v.tensor_tensor(pt_lo[:, o:o + w], turned_bank[u][:, 0:w], pt_hi[:, o:o + w], ALU.subtract
                                        ).then_inc(s_ptlo, 1)
                if boundary:
                    v.wait_ge(s_omm, n)
                    for i in range(2):
                        v.wait_ge(s_xadd, 5 * b - 4)
                        v.scalar_tensor_tensor(osum[:, 2 * i:2 * i + 2, :],
                                               oa[i][:, :].rearrange("p (t d) -> p t d", t=2),
                                               1.0 / (WS * PS * WS),
                                               gate[:, ds((b - 1) * D, D)].unsqueeze(1).broadcast_to([P, 2, D]),
                                               ALU.mult, ALU.mult).then_inc(s_oread, 1)
            run_steps(v, step)

        @block.tensor
        def _(pe):
            def project(out, hi, lo, col, b):
                return split3(pe, out, [((hi[:, c, ds(col, P)], lo[:, c, ds(col, P)]),
                                         (hT_hi[:, c, ds(b * S, S)], hT_lo[:, c, ds(b * S, S)]))
                                        for c in range(KT)])

            def values_of(b, tt, g, bk):
                tok = b * S + tt * P
                return split3(pe, bk[:, :], [((hT_hi[:, c, ds(tok, P)], hT_lo[:, c, ds(tok, P)]),
                                              (wv_hi[:, c, ds(g * 512, 512)], wv_lo[:, c, ds(g * 512, 512)]))
                                             for c in range(KT)]).then_inc(s_vmm, 1)

            project(pr[1][:, :], wqk_hi, wqk_lo, 0, 0).then_inc(s_qmm, 1)
            project(pr[0][:, :], wqk_hi, wqk_lo, H * HD, 0).then_inc(s_kmm, 1)

            def step(n, r, b, next_of, prev_h, values, out_first, last, **_):
                def score(t):
                    w = (t + 1) * P
                    split3(pe, score_out[t], [((q_hi[:, t * P:w], q_lo[:, t * P:w]), (k_hi[:, 0:w], k_lo[:, 0:w]))]
                           ).then_inc(s_scored, 1)

                def turn(u):
                    o = 0
                    for j in PT_UNITS[u]:
                        for t in range(j, TB):
                            ins = pe.transpose(turned_bank[u][:, o:o + P],
                                               prob[:, SOFF[t] + j * P:SOFF[t] + (j + 1) * P], ident[:, :])
                            o += P
                    ins.then_inc(s_turned, 1)

                if not last:
                    pe.wait_ge(s_qlo, n + 1)
                    pe.wait_ge(s_klo, n + 1)
                    if prev_h is not None:
                        pe.wait_ge(s_masked, 4 * n)
                    for t in QTILES:
                        if t == 1 and prev_h is not None:
                            pe.wait_ge(s_ptlo, 3 * n - 2)
                        score(t)
                if prev_h is not None:
                    pe.wait_ge(s_ptlo, 3 * n)
                    col = prev_h * HD
                    terms = []
                    for j in range(TB):
                        o, w = JOFF[j], (TB - j) * P
                        for vp, pp in ((v_hi, pt_hi), (v_hi, pt_lo), (v_lo, pt_hi)):
                            terms.append((j, vp[:, j, ds(col, HD)], pp[:, o:o + w]))
                    for i, (j, a, p_) in enumerate(terms):
                        ins = pe.matmul(pr[0][:, j * P:512], a, p_, start=(i == 0), stop=(i == len(terms) - 1))
                    ins.then_inc(s_cmm, 1)
                if next_of is not None:
                    project(pr[1][:, :], wqk_hi, wqk_lo, next_of[1] * HD, next_of[0]).then_inc(s_qmm, 1)
                if values is not None:
                    values_of(values[0], r, values[1], tr[0])
                if prev_h is not None:
                    pe.wait_ge(s_clo, n)
                if next_of is not None:
                    project(pr[0][:, :], wqk_hi, wqk_lo, (next_of[1] + H) * HD, next_of[0]).then_inc(s_kmm, 1)
                if not last:
                    pe.wait_ge(s_norm, 4 * n + 4)
                    turn(0)
                    if next_of is not None:
                        pe.wait_ge(s_qlo, n + 2)
                    turn(1)
                    if values is not None:
                        pe.wait_ge(s_vlo, n + 13)
                    turn(2)
                if prev_h is not None:
                    if out_first and not isinstance(n, int):
                        pe.wait_ge(s_oread, 2 * b)
                    for t in range(TB):
                        for i, (ch, wh) in enumerate(((ctx_hi, wo_hi), (ctx_hi, wo_lo), (ctx_lo, wo_hi))):
                            ins = pe.matmul(oa[t // 2][:, (t % 2) * D:(t % 2 + 1) * D], ch[:, t * P:(t + 1) * P],
                                            wh[:, prev_h, :], start=(out_first and t % 2 == 0 and i == 0),
                                            stop=False, skip_group_check=True)
                    ins.then_inc(s_omm, 1)
            run_steps(pe, step)

    b2a = layout(BIG)
    entwT.append(b2a("entwT1", [P, EC, D], F32))
    entpw.append(b2a("entpw1", [P, EC, D], F32))
    path = b2a("path", [P, LE, PWN, KT, D], F32)
    brows = b2a("brows", [1, 6, D], F32)
    wst = b2a("wst", [P, KT, D], F32)
    assert b2a.pos[0] <= WV
    b2 = layout(WO)
    amph_hi = b2("amph_hi", [P, 2, KT, D], F16)
    amph_lo = b2("amph_lo", [P, 2, KT, D], F16)
    wst_hi = b2("wst_hi", [P, 4, KT, D], F16)
    wst_lo = b2("wst_lo", [P, 4, KT, D], F16)
    wrow = b2("wrow", [1, D], F32)
    brow_hi = b2("brow_hi", [1, 4, D], F16)
    brow_lo = b2("brow_lo", [1, 4, D], F16)
    NSL = 3
    hq = [b2(f"hq{i}", [P, KT, S], F32) for i in range(NSL)]
    AFTER = b2.pos[0]
    gg = b2("gg", [P, B, D], F32)
    xnq = [b2(f"xnq{i}", [P, TB, D], F32) for i in range(NSL)]
    TANH = b2.pos[0]
    tanh = b2("tanh", [P, KT, B * S], F32)
    assert b2.pos[0] <= st1.pos[0], b2.pos[0] - st1.pos[0]
    wk2 = layout(WORK)
    nmr = wk2("nmr", [P, NT], F32)
    nmean = wk2("nmean", [P, NT], F32)
    turnm = wk2("turnm", [P, LE * PWN, D], F32)
    sigm = wk2("sigm", [P, KT, B * S], F32)
    assert wk2.pos[0] <= end, wk2.pos[0] - end
    w3 = layout(BIG)
    wq1 = w3("wq1", [P, KT, 3 * D], F32)
    wq1_hi = w3("wq1_hi", [P, KT, 3 * D], F16)
    wq1_lo = w3("wq1_lo", [P, KT, 3 * D], F16)
    wo1 = w3("wo1", [P, KT, D], F32)
    wo1_hi = w3("wo1_hi", [P, KT, D], F16)
    wo1_lo = w3("wo1_lo", [P, KT, D], F16)
    boutb = w3("boutb", [P, D], F32)
    assert w3.pos[0] <= BIG + 24 * 1024
    n3 = layout(TANH)
    xq3 = [n3(f"xq3_{i}", [P, TB, D], F32) for i in range(2)]
    tq3 = [n3(f"tq3_{i}", [P, KT, S], F32) for i in range(2)]
    ln2 = LayerNorm("ln2", xq3, tq3, bank[6:8], 1, CA, SA)
    s_wq1, s_bout, s_gate3, s_whi3, s_wlo3 = (k.sem(n) for n in ("wq1_in", "bout_in", "gate3_in", "w1_hi", "w1_lo"))
    ln1 = LayerNorm("ln1", xnq[0:2], hq[0:2], bank[6:8], 0, CB, SB)
    s_path, s_gate2 = (k.sem(n) for n in ("path_in", "gate2_in"))
    (s_ahi, s_alo, s_ph, s_mod2, s_wp, s_whi2, s_wlo2, s_wmm, s_brow, s_wready, s_z, s_act2) = (
        k.sem(n) for n in ("amph_hi_done", "amph_lo_done", "phase_turns", "path_mod", "stage_w", "stage_w_hi",
                           "stage_w_lo", "ent_product", "bias_row", "stage_w_ready", "z_psum", "z_act"))
    (s_wrap, s_sin, s_gg, s_xb, s_h, s_hhi, s_hlo, s_mm, s_st, s_ve, s_rs, s_xn, s_tn, s_fin, s_xb2, s_hlo1, s_hsine) = (
        k.sem(n) for n in ("wrapped", "sine", "gate_ln4", "x_bias", "h_new", "h_hi", "h_lo", "stage_mm",
                           "stage_stats", "stage_vareps", "stage_rstd", "stage_xn", "stage_turned",
                           "stage_gated", "x_stage_added", "h_lo_tile1", "sine_lo_tile1"))
    SQRT2 = 2.0 ** 0.5
    TWO_PI = 6.283185
    PI_ = 3.1415925
    ROUND = 12582912.0
    g4, b4 = rows[:, 4, :], rows[:, 5, :]
    ORDER = (0, 1, 3, 2)
    NU = 4 * B
    LAST = 3 * B

    def units(e, first, body, last):
        first()
        with e.Fori(0, LAST // NSL) as i:
            for s in range(NSL):
                body(NSL * i + s, s)
        last()

    STAT = (2, 1, 3)

    def into_x(v, b, add):
        v.wait_ge(s_xn, NSL * TB + TB * (LAST + b) + TB)
        xq = xnq[(LAST + b) % NSL]
        v.tensor_tensor(xq[:], xq[:], gg[:, b, :].unsqueeze(1).broadcast_to([P, TB, D]), ALU.mult
                        ).then_inc(s_fin, 1)
        if add:
            into_x_sum(v, b)

    def into_x_sum(e, b):
        xb = x[:, b * TB:(b + 1) * TB, :]
        e.wait_ge(s_fin, b + 1)
        e.tensor_tensor(xb, xb, xnq[(LAST + b) % NSL][:], ALU.add).then_inc(s_xb2, 1)

    b3 = layout(w3.pos[0])
    P3 = BIG
    qk1_hi = b3("qk1_hi", [P, 2 * KT, B * S], F16)
    qk1_lo = b3("qk1_lo", [P, 2 * KT, B * S], F16)
    v1_hi = b3("v1_hi", [P, NT, D], F16)
    v1_lo = b3("v1_lo", [P, NT, D], F16)
    T3 = b3.pos[0]
    assert T3 <= AFTER
    t3 = layout(T3)
    prob1 = t3("prob1", [P, TB, S], F32)
    pt1_hi = t3("pt1_hi", [P, TB, S], F16)
    pt1_lo = t3("pt1_lo", [P, TB, S], F16)
    ctx1_hi = t3("ctx1_hi", [P, KT, S], F16)
    ctx1_lo = t3("ctx1_lo", [P, KT, S], F16)
    osum1 = t3("osum1", [P, TB, D], F32)
    gbo = t3("gbo", [P, B, D], F32)
    assert t3.pos[0] <= DEC
    t3c = layout(t3.pos[0])
    smin1 = t3c("smin1", [P, TB], F32)
    sminb = t3c("sminb", [P, TB], F32)
    ssum1 = t3c("ssum1", [P, TB], F32)
    sinv1 = t3c("sinv1", [P, TB], F32)
    assert t3c.pos[0] <= DEC, t3c.pos[0] - DEC
    NEXT = t3c.pos[0]
    n4 = layout(NEXT)
    xq4 = [n4(f"xq4_{i}", [P, TB, D], F32) for i in range(2)]
    tq4 = [n4(f"tq4_{i}", [P, KT, S], F32) for i in range(2)]
    assert n4.pos[0] <= DEC
    ln3 = LayerNorm("ln3", xq4, tq4, bank[4:6], 1, CB, SB)
    s_bc3, s_pmm, s_phi, s_plo = (k.sem(n) for n in ("bias1_cols", "proj1_mm", "proj1_hi", "proj1_lo"))

    with nc.Block() as block:
        @block.sync
        def _(sp):
            sp.dma_start(brows[:].rearrange("p r d -> p (r d)"), A["rows"][:, R_ENTPB * D:R_PHASE * D]
                         ).then_inc(s_path, 16)
            sp.dma_start(path[:], A["path"]).then_inc(s_path, 16)
            load_gate(sp, 0, 1, s_gate2)
            sp.dma_start(entwT[1][:], A["entwT"][:, 1]).then_inc(s_ent[1], 16)
            sp.dma_start(entpw[1][:], A["entpw"][:, 1]).then_inc(s_ent[1], 16)
            sp.wait_ge(s_wready, 2 * LE)
            sp.dma_start(wq1[:], A["wqkv1"]).then_inc(s_wq1, 16)
            sp.dma_start(wo1[:], A["wout1"]).then_inc(s_wq1, 16)
            sp.dma_start(boutb[:], bass.AP(tensor=A["rows"].tensor, offset=R_BOUT * D, ap=[[0, P], [1, D]])
                         ).then_inc(s_bout, 16)
            sp.wait_ge(s_xb, NT)
            load_gate(sp, 1, 0, s_gate3)
            sp.wait_ge(s_gate3, 16)
            sp.wait_ge(s_bout, 16)

        @block.gpsimd
        def _(g):
            ln1.gpsimd(g, 0)
            ln1.gpsimd(g, 1)
            g.wait_ge(s_gate2, 16)
            g.wait_ge(s_rows2, 32)
            for b in range(B):
                g.tensor_tensor(gg[:, b, :], gate[:, b * D:(b + 1) * D], g4, ALU.mult).then_inc(s_gg, 1)
            g.wait_ge(s_gg, B)
            for b in range(B):
                gb_ = gate[:, b * D:(b + 1) * D]
                g.tensor_tensor(gb_, gb_, b4, ALU.mult).then_inc(s_gg, 1)
            g.wait_ge(s_gg, 2 * B)
            g.wait_ge(ln1.xn, NT)
            with g.Fori(0, B) as b:
                for t in range(TB):
                    xt = x[:, b * TB + t, :]
                    g.tensor_tensor(xt, xt, gate[:, ds(b * D, D)], ALU.add).then_inc(s_xb, 1)

            with g.Fori(0, B) as b:
                for c in range(KT):
                    g.wait_ge(s_hhi, KT * b + c + 1)
                    g.tensor_tensor(hT_lo[:, c, ds(b * S, S)], sigm[:, c, ds(b * S, S)],
                                    hT_hi[:, c, ds(b * S, S)], ALU.subtract).then_inc((s_hlo, s_hsine)[c], 1)

            def inverse(kk, s):
                tiles = ds(STAT[s] * TB, TB)
                g.wait_ge(s_ve, kk + 1)
                g.tensor_tensor(rstd[:, tiles], vareps[:, tiles], mhalf[:, tiles], ALU.pow).then_inc(s_rs, 1)
                g.wait_ge(s_rs, 2 * kk + 1)
                g.tensor_tensor(nmr[:, tiles], nmean[:, tiles], rstd[:, tiles], ALU.mult).then_inc(s_rs, 1)

            def first():
                inverse(0, 0)
                inverse(1, 1)

            def body(j, s):
                b = j % B
                g.wait_ge(s_hhi, KT * (B + j) + 1)
                g.tensor_tensor(hT_lo[:, 0, ds(b * S, S)], hq[s][:, 0, :], hT_hi[:, 0, ds(b * S, S)],
                                ALU.subtract).then_inc(s_hlo, 1)
                inverse(j + 2, (s + 2) % NSL)

            def last():
                g.wait_ge(s_xb, NT)
                inverse(NU - 2, (NU - 2) % NSL)
                inverse(NU - 1, (NU - 1) % NSL)
                ln2.gpsimd(g, 0)
            units(g, first, body, last)

            into_x_sum(g, 2)
            into_x_sum(g, 3)
            ln2.inverse(g, 1)
            ln2.split_lo(g, 1)

        @block.scalar
        def _(act):
            act.preload_act_table(ACT.Sin)
            act.wait_ge(s_amph, 16)
            act.activation(amph_hi[:], amph[:], ACT.Copy, scale=WS).then_inc(s_ahi, 1)
            act.wait_ge(s_ph, 2)
            act.activation(turnm[:], turnm[:], ACT.Sin, scale=-TWO_PI).then_inc(s_ph, 1)
            act.preload_act_table(ACT.Sigmoid)
            ln1.scalar(act, 0)

            def z_act(b):
                for w in range(2):
                    for f in range(KT):
                        act.wait_ge(s_z, 4 * b + 2 * w + f + 1)
                        bc = (C_AMPB, C_PHB)[w] + f
                        act.activation((sigm, tanh)[w][:, f, ds(b * S, S)], bank[2 * w + f][:, :],
                                       (ACT.Sigmoid, ACT.Tanh)[w], bias=cols[:, bc:bc + 1], scale=1.0 / WS
                                       ).then_inc(s_act2, 1)

            def weight_hi(i):
                act.wait_ge(s_wp, i + 1)
                act.activation(wst_hi[:, ORDER[i], :, :], wst[:], ACT.Copy, scale=WS).then_inc(s_whi2, 1)
            z_act(0)
            ln1.scalar(act, 1)
            for b in range(1, B):
                weight_hi(b - 1)
                z_act(b)
            act.preload_act_table(ACT.Sin)

            def sine(b):
                act.wait_ge(s_wrap, 2 * b + 2)
                act.activation(tanh[:, :, ds(b * S, S)], tanh[:, :, ds(b * S, S)], ACT.Sin, scale=PI_
                               ).then_inc(s_sin, 1)

            def sine_hi(b):
                act.wait_ge(s_h, KT * b + KT)
                for c in range(KT):
                    act.activation(hT_hi[:, c, ds(b * S, S)], sigm[:, c, ds(b * S, S)], ACT.Copy
                                   ).then_inc(s_hhi, 1)
            sine(0)
            with act.Fori(1, B) as b:
                sine(b)
                sine_hi(b - 1)
            sine_hi(B - 1)
            weight_hi(3)

            def normalise(kk, s):
                act.wait_ge(s_rs, 2 * kk + 2)
                act.wait_ge(s_tn, KT * kk + KT)
                for t in range(TB):
                    col = ds(STAT[s] * TB + t, 1)
                    act.activation(xnq[s][:, t, :], bank[2 * s + t // 2][:, (t % 2) * D:(t % 2 + 1) * D],
                                   ACT.Identity, bias=nmr[:, col], scale=rstd[:, col]).then_inc(s_xn, 1)

            def first():
                normalise(0, 0)
                normalise(1, 1)

            def body(j, s):
                b = j % B
                for c in range(KT):
                    act.wait_ge(s_h, KT * (B + j) + c + 1)
                    act.activation(hT_hi[:, c, ds(b * S, S)], hq[s][:, c, :], ACT.Copy).then_inc(s_hhi, 1)
                normalise(j + 2, (s + 2) % NSL)

            def last():
                act.wait_ge(s_wq1, 32)
                act.activation(wq1_hi[:, :, 0:D], wq1[:, :, 0:D], ACT.Copy, scale=-WS).then_inc(s_whi3, 1)
                act.activation(wq1_hi[:, :, D:3 * D], wq1[:, :, D:3 * D], ACT.Copy, scale=WS).then_inc(s_whi3, 1)
                act.activation(wo1_hi[:], wo1[:], ACT.Copy, scale=WS).then_inc(s_whi3, 1)
                normalise(NU - 2, (NU - 2) % NSL)
                act.wait_ge(s_xb2, 1)
                act.wait_ge(s_rs, 2 * NU)
                s = (NU - 1) % NSL
                for t in range(TB):
                    col = ds(STAT[s] * TB + t, 1)
                    act.activation(xnq[s][:, t, :], bank[2 * s + t // 2][:, (t % 2) * D:(t % 2 + 1) * D],
                                   ACT.Identity, bias=nmr[:, col], scale=rstd[:, col]
                                   ).then_inc(s_xn, 1)
                ln2.scalar(act, 0)
            units(act, first, body, last)

            act.wait_ge(s_bc3, 3)

            def projections(b):
                for i in range(2 * KT):
                    act.wait_ge(s_pmm, 6 * b + i + 1)
                    act.activation(qk1_hi[:, i, ds(b * S, S)], bank[i][:, :], ACT.Identity,
                                   bias=bcol1[:, i:i + 1]).then_inc(s_phi, 1)
                for i in range(2):
                    act.wait_ge(s_pmm, 6 * b + 4 + i + 1)
                    act.activation(v1_hi[:, ds(b * TB + 2 * i, 2), :], bank[4 + i][:, :].rearrange(
                        "p (t d) -> p t d", t=2), ACT.Copy).then_inc(s_phi, 1)
            projections(0)
            projections(1)
            ln2.scalar(act, 1)
            with act.Fori(2, B) as b:
                projections(b)

        @block.tensor
        def _(pe):
            def z(b):
                ln1.wait_parts(pe, b)
                for w in range(2):
                    for f in range(KT):
                        pe.wait_ge(s_act2, 4 * b + 2 * w + f + 1)
                        split3(pe, bank[2 * w + f][:, :],
                               [((amph_hi[:, w, c, f * P:(f + 1) * P], amph_lo[:, w, c, f * P:(f + 1) * P]),
                                 (hT_hi[:, c, ds(b * S, S)], hT_lo[:, c, ds(b * S, S)]))
                                for c in range(KT)]).then_inc(s_z, 1)

            def ent_product(l):
                pe.wait_ge(s_ent[l], 32)
                for dt in range(KT):
                    for kc in range(EC):
                        ins = pe.matmul(bank[4][:, dt * D:(dt + 1) * D], entwT[l][:, kc, dt * P:(dt + 1) * P],
                                        entpw[l][:, kc, :], start=(kc == 0), stop=(kc == EC - 1))
                for kc in range(EC):
                    ins = pe.matmul(bank[5][0:1, 0:D], cols[:, C_ENTB + l * EC + kc:C_ENTB + l * EC + kc + 1],
                                    entpw[l][:, kc, :], start=(kc == 0), stop=(kc == EC - 1))
                ins.then_inc(s_wmm, 1)
            ent_product(0)
            ln1.tensor(pe, 0)
            pe.wait_ge(s_alo, 1)
            z(0)
            ln1.tensor(pe, 1)
            with pe.Fori(1, B) as b:
                z(b)
            pe.wait_ge(s_wready, 1)
            ent_product(1)
            pe.wait_ge(s_act2, 4 + 4 * B)

            def product(kk, s, turn=None):
                st, b = kk // B, kk % B
                pe.wait_ge(s_hlo, kk + 1)
                pe.wait_ge(s_hlo1, kk + 1)
                for t in range(TB):
                    if t == 2 and turn is not None:
                        turn()
                    if t % 2 == 0:
                        pe.wait_ge(s_xn, TB * kk + t + 2)
                    tok = b * S + t * P
                    out = bank[2 * s + t // 2][:, (t % 2) * D:(t % 2 + 1) * D]
                    terms = []
                    for c in range(KT):
                        hh, hl = hT_hi[:, c, ds(tok, P)], hT_lo[:, c, ds(tok, P)]
                        wh, wl = wst_hi[:, ds(st, 1), c, :], wst_lo[:, ds(st, 1), c, :]
                        wh, wl = (w.rearrange("p a d -> p (a d)") for w in (wh, wl))
                        terms += [(hh, wh), (hh, wl), (hl, wh)]
                    for br in (brow_hi, brow_lo):
                        terms.append((ones16[:, :], br[:, ds(st, 1), :].rearrange("p a d -> p (a d)")))
                    for i, (a, w) in enumerate(terms):
                        ins = pe.matmul(out, a, w, start=(i == 0), stop=(i == len(terms) - 1))
                    ins.then_inc(s_mm, 1)

            def first():
                pe.wait_ge(s_wready, 2 * LE - 1)
                pe.wait_ge(s_hsine, 1)
                product(0, 0)
                pe.wait_ge(s_hsine, 2)
                product(1, 1)
                pe.wait_ge(s_hsine, B)
                pe.wait_ge(s_wready, 2 * LE)

            def body(j, s):
                def turn():
                    pe.wait_ge(s_xn, NSL * TB + TB * j + TB)
                    for c in range(KT):
                        pe.wait_ge(s_h, KT * (B + j - 1) + c + 1)
                        for t in range(TB):
                            ins = pe.transpose(bank[6 + c][:, t * P:(t + 1) * P],
                                               xnq[s][:, t, c * P:(c + 1) * P], ident[:, :])
                        ins.then_inc(s_tn, 1)
                product(j + 2, (s + 2) % NSL, turn)

            def last():
                product(NU - 2, (NU - 2) % NSL)
                product(NU - 1, (NU - 1) % NSL)
                ln2.tensor(pe, 0)
            units(pe, first, body, last)

            def projections(b):
                ln2.wait_parts(pe, b)
                for i in range(2 * KT):
                    pe.wait_ge(s_plo, 6 * b + i + 1)
                    split3(pe, bank[i][:, :], [((wq1_hi[:, c, i * P:(i + 1) * P], wq1_lo[:, c, i * P:(i + 1) * P]),
                                                (hT_hi[:, c, ds(b * S, S)], hT_lo[:, c, ds(b * S, S)]))
                                               for c in range(KT)]).then_inc(s_pmm, 1)
                for i in range(2):
                    pe.wait_ge(s_plo, 6 * b + 4 + i + 1)
                    for t in (2 * i, 2 * i + 1):
                        tok = b * S + t * P
                        ins = split3(pe, bank[4 + i][:, (t % 2) * D:(t % 2 + 1) * D],
                                     [((hT_hi[:, c, ds(tok, P)], hT_lo[:, c, ds(tok, P)]),
                                       (wq1_hi[:, c, 2 * D:3 * D], wq1_lo[:, c, 2 * D:3 * D])) for c in range(KT)])
                    ins.then_inc(s_pmm, 1)
            pe.wait_ge(s_wlo3, 2)
            pe.wait_ge(s_xn, TB * (NSL + NU))
            projections(0)
            projections(1)
            ln2.tensor(pe, 1)
            with pe.Fori(2, B) as b:
                projections(b)

        @block.vector
        def _(v):
            ln1.free_slots(v)
            v.sem_inc(s_act2, 4)
            v.sem_inc(s_xn, NSL * TB)
            v.sem_inc(s_tn, NSL * KT)
            v.sem_inc(s_hlo1, B)
            for i, sc_ in enumerate((-WS, WS, WS * PS)):
                v.tensor_scalar(bcol1[:, KT * i:KT * i + KT], cols[:, C_B1 + KT * i:C_B1 + KT * i + KT], sc_, None,
                                ALU.mult).then_inc(s_bc3, 1)
            ln1.normalise(v, 0)
            v.wait_ge(s_rows2, 32)
            ph = rows[:, 0:4, :]
            v.tensor_scalar(ph, ph, 1.0 / 6.283185307179586, 0.125, ALU.mult, ALU.add).then_inc(s_mod2, 1)
            v.wait_ge(s_mod2, 1)
            v.tensor_scalar(turnm[:], ph, ROUND, None, ALU.add).then_inc(s_ph, 1)
            v.wait_ge(s_ph, 1)
            v.scalar_tensor_tensor(turnm[:].rearrange("p a d -> p (a d)"), turnm[:].rearrange("p a d -> p (a d)"),
                                   -ROUND, ph.rearrange("p a d -> p (a d)"), ALU.add, ALU.subtract
                                   ).then_inc(s_ph, 1)
            v.wait_ge(s_ahi, 1)
            v.scalar_tensor_tensor(amph_lo[:].rearrange("p a k d -> p (a k d)"),
                                   amph[:].rearrange("p a k d -> p (a k d)"), WS,
                                   amph_hi[:].rearrange("p a k d -> p (a k d)"),
                                   ALU.mult, ALU.subtract).then_inc(s_alo, 1)
            ln1.modulate(v, 0)
            ln1.vector(v, 1)
            v.wait_ge(s_ph, 3)
            v.wait_ge(s_path, 32)
            n = 1
            for l in range(LE):
                for p_ in range(PWN):
                    m = turnm[:, l * PWN + p_, :]
                    pw = path[:, l, p_, :, :]
                    for c in range(KT):
                        v.scalar_tensor_tensor(pw[:, c, :], m, SQRT2, pw[:, c, :], ALU.mult, ALU.mult
                                               ).then_inc(s_mod2, 1)
                    pb = brows[0:1, LE + l * PWN + p_, :]
                    v.scalar_tensor_tensor(pb, turnm[0:1, l * PWN + p_, :], SQRT2, pb, ALU.mult, ALU.mult
                                           ).then_inc(s_mod2, 1)
                    n += 3
            v.wait_ge(s_mod2, n)

            def stage_weight(i, n):
                st = ORDER[i]
                l = st // 2
                if st % 2:
                    v.tensor_tensor(wst[:], path[:, l, 0, :, :], path[:, l, 1, :, :], ALU.add).then_inc(s_mod2, 1)
                    v.tensor_tensor(wrow[:], brows[0:1, LE + 2 * l, :], brows[0:1, LE + 2 * l + 1, :], ALU.add
                                    ).then_inc(s_brow, 1)
                    n += 1
                else:
                    v.wait_ge(s_wmm, l + 1)
                    for c in range(KT):
                        v.tensor_copy(wst[:, c, :], bank[4][:, c * D:(c + 1) * D]).then_inc(s_mod2, 1)
                    n += 2
                    v.tensor_tensor(wrow[:], bank[5][0:1, 0:D], brows[0:1, l, :], ALU.add
                                    ).then_inc(s_brow, 1)
                v.wait_ge(s_brow, 3 * i + 1)
                v.tensor_scalar(brow_hi[:, st, :], wrow[:], WS, None, ALU.mult).then_inc(s_brow, 1)
                v.wait_ge(s_mod2, n)
                for c in range(KT):
                    diag = wst[:, c, c * P:(c + 1) * P]
                    v.tensor_tensor(diag, diag, ident[:], ALU.add).then_inc((s_mod2, s_wp)[c], 1)
                v.wait_ge(s_brow, 3 * i + 2)
                v.scalar_tensor_tensor(brow_lo[:, st, :], wrow[:], WS, brow_hi[:, st, :], ALU.mult, ALU.subtract
                                       ).then_inc(s_brow, 1)
                v.wait_ge(s_whi2, i + 1)
                v.scalar_tensor_tensor(wst_lo[:, st, :, :].rearrange("p k d -> p (k d)"),
                                       wst[:].rearrange("p k d -> p (k d)"), WS,
                                       wst_hi[:, st, :, :].rearrange("p k d -> p (k d)"), ALU.mult, ALU.subtract
                                       ).then_inc(s_wlo2, 1)
                v.wait_ge(s_brow, 3 * i + 3)
                v.wait_ge(s_wlo2, i + 1)
                v.sem_inc(s_wready, 1)
                return n + 1
            for i in range(3):
                n = stage_weight(i, n)

            def wrap(b):
                th = tanh[:, :, ds(b * S, S)]
                v.wait_ge(s_act2, 4 + 4 * b + 4)
                v.tensor_scalar(hq[2][:], th, 0.75, -2.0, ALU.is_gt, ALU.mult).then_inc(s_wrap, 1)
                v.wait_ge(s_wrap, 2 * b + 1)
                v.scalar_tensor_tensor(th, hq[2][:], 0.25, th, ALU.add, ALU.add).then_inc(s_wrap, 1)

            def sine_times(b):
                v.wait_ge(s_sin, b + 1)
                for c in range(KT):
                    sg = sigm[:, c, ds(b * S, S)]
                    v.scalar_tensor_tensor(sg, tanh[:, c, ds(b * S, S)], SQRT2, sg, ALU.mult, ALU.mult
                                           ).then_inc(s_h, 1)
            wrap(0)
            with v.Fori(1, B) as b:
                v.wait_ge(s_wrap, 2 * b)
                wrap(b)
                sine_times(b - 1)
            sine_times(B - 1)
            stage_weight(3, n)

            def statistics(kk, s, halfway=None):
                for t in range(TB):
                    if t == 2 and halfway is not None:
                        halfway()
                    v.wait_ge(s_mm, TB * kk + 2 * (t // 2) + 2)
                    v.bn_stats(stats[:, STAT[s] * TB + t, :],
                               bank[2 * s + t // 2][:, (t % 2) * D:(t % 2 + 1) * D]).then_inc(s_st, 1)
                v.wait_ge(s_st, (TB + 5) * kk + TB)
                combine_stats(v, s_st, STAT[s], (TB + 5) * kk + TB, EPS * WS * WS, nmean
                              ).then_inc(s_ve, 1)

            def first():
                statistics(0, 0)
                statistics(1, 1)

            def body(j, s):
                st = j // B

                def modulate():
                    for c in range(KT):
                        gc = C_LN + (st % 2) * 2 * LE * KT + (st // 2) * KT + c
                        v.wait_ge(s_tn, NSL * KT + KT * j + c + 1)
                        v.wait_ge((s_hlo, s_hlo1)[c], j + B - NSL + 1)
                        v.tensor_scalar(hq[s][:, c, :], bank[6 + c][:, :], cols[:, ds(gc, 1)],
                                        cols[:, ds(gc + LE * KT, 1)], ALU.mult, ALU.add).then_inc(s_h, 1)
                statistics(j + 2, (s + 2) % NSL, modulate)
                b = j % B
                v.wait_ge(s_hhi, KT * (B + j) + 2)
                v.tensor_tensor(hT_lo[:, 1, ds(b * S, S)], hq[s][:, 1, :], hT_hi[:, 1, ds(b * S, S)],
                                ALU.subtract).then_inc(s_hlo1, 1)

            def last():
                v.wait_ge(s_gg, B)
                v.wait_ge(s_xb, NT)
                into_x(v, 0, True)
                statistics(NU - 2, (NU - 2) % NSL)
                into_x(v, 1, True)
                statistics(NU - 1, (NU - 1) % NSL)
                v.wait_ge(s_xb2, 2)
                ln2.free_slots(v)
                ln2.normalise(v, 0)
                ln2.modulate(v, 0)
                for i, (o, w, sg) in enumerate(((0, D, -WS), (D, 2 * D, WS))):
                    v.wait_ge(s_whi3, i + 1)
                    v.scalar_tensor_tensor(wq1_lo[:, :, o:o + w], wq1[:, :, o:o + w], sg, wq1_hi[:, :, o:o + w],
                                           ALU.mult, ALU.subtract).then_inc(s_wlo3, 1)
            units(v, first, body, last)

            v.sem_inc(s_plo, 6)
            into_x(v, 2, False)
            into_x(v, 3, False)
            v.wait_ge(s_whi3, 3)
            v.wait_ge(s_bc3, 3)
            v.scalar_tensor_tensor(wo1_lo[:], wo1[:], WS, wo1_hi[:], ALU.mult, ALU.subtract).then_inc(s_wlo3, 1)

            def projections(b):
                for i in range(2 * KT):
                    v.wait_ge(s_phi, 6 * b + i + 1)
                    v.scalar_tensor_tensor(qk1_lo[:, i, ds(b * S, S)], bank[i][:, :], bcol1[:, i:i + 1],
                                           qk1_hi[:, i, ds(b * S, S)], ALU.add, ALU.subtract).then_inc(s_plo, 1)
                for i in range(2):
                    v.wait_ge(s_phi, 6 * b + 4 + i + 1)
                    v.tensor_tensor(v1_lo[:, ds(b * TB + 2 * i, 2), :], bank[4 + i][:, :].rearrange(
                        "p (t d) -> p t d", t=2), v1_hi[:, ds(b * TB + 2 * i, 2), :], ALU.subtract
                        ).then_inc(s_plo, 1)
            projections(0)
            v.wait_ge(s_xb2, B)
            ln2.normalise(v, 1)
            ln2.modulate(v, 1)
            projections(1)
            with v.Fori(2, B) as b:
                projections(b)

    (s_sc1, s_mn1, s_mb1, s_ex1, s_iv1, s_nm1, s_tn1, s_th1, s_tl1, s_cm1, s_ch1, s_cl1, s_om1, s_or1, s_xa1,
     s_gb1) = (
        k.sem(n) for n in ("scored1", "min1", "min1_scaled", "exp1", "inverse1", "normalised1", "turned1",
                           "pt1_hi_done", "pt1_lo_done", "ctx1_mm", "ctx1_hi_done", "ctx1_lo_done", "out1_mm",
                           "out1_read", "x1_added", "gate_bout"))
    SCALE1 = 1.0 / (WS * WS * D ** 0.5)
    TURNS = ((2, 0), (3, 1), (0, 4), (1, 5))

    def run1(e, step):
        step(0, first=True, last=False)
        with e.Fori(1, B) as i:
            step(i, first=False, last=False)
        step(B, first=False, last=True)

    with nc.Block() as block:
        @block.gpsimd
        def _(g):
            for b in range(B):
                g.tensor_tensor(gbo[:, b, :], gate[:, b * D:(b + 1) * D], boutb[:], ALU.mult).then_inc(s_gb1, 1)
            g.wait_ge(s_gb1, B)

            def step(i, first, last):
                if not last:
                    wait_apart(g, s_iv1, i + 1, s_passed)
                    for t in range(TB):
                        g.tensor_scalar(prob1[:, t, :], prob1[:, t, :], sinv1[:, t:t + 1], PS, ALU.mult, ALU.mult
                                        ).then_inc(s_nm1, 1)
                if last:
                    ln3.inverse(g, 0)
                if not first:
                    for t in range(TB):
                        xt = x[:, TB * (i - 1) + t, :]
                        g.tensor_tensor(xt, xt, gbo[:, i - 1, :], ALU.add).then_inc(s_xa1, 1)
                if not first and not last:
                    g.wait_ge(s_xa1, 5 * i - 1)
                    wait_apart(g, s_or1, 2 * i + 2, s_passed)
                    xb = x[:, ds(TB * (i - 1), TB), :]
                    g.tensor_tensor(xb, xb, osum1[:], ALU.add).then_inc(s_xa1, 1)
            run1(g, step)
            ln3.split_lo(g, 0)

        @block.scalar
        def _(act):
            act.preload_act_table(ACT.Exp)

            def step(i, first, last):
                if not last:
                    for t in range(TB):
                        act.wait_ge(s_mb1, TB * i + t + 1)
                        act.activation(prob1[:, t, :], bank[t][:, :], ACT.Exp, bias=sminb[:, t:t + 1],
                                       scale=-SCALE1, accum_out=ssum1[:, t:t + 1]).then_inc(s_ex1, 1)
                if not first:
                    for c in range(KT):
                        act.wait_ge(s_cm1, KT * (i - 1) + c + 1)
                        act.activation(ctx1_hi[:, c, :], bank[6 + c][:, :], ACT.Identity,
                                       bias=bcol1[:, 2 * KT + c:2 * KT + c + 1]).then_inc(s_ch1, 1)
                if last:
                    ln3.scalar(act, 0)
                if not last:
                    for n, (j, bk) in enumerate(TURNS):
                        act.wait_ge(s_tn1, TB * i + n + 1)
                        act.activation(pt1_hi[:, j, :], bank[bk][:, :], ACT.Copy).then_inc(s_th1, 1)
            run1(act, step)

        @block.vector
        def _(v):
            v.sem_inc(s_or1, 2)
            def step(i, first, last):
                if not last:
                    for t in range(TB):
                        v.wait_ge(s_sc1, TB * i + t + 1)
                        v.tensor_reduce(smin1[:, t:t + 1], bank[t][:, :], AX.X, ALU.min).then_inc(s_mn1, 1)
                        v.wait_ge(s_mn1, TB * i + t + 1)
                        v.tensor_scalar(sminb[:, t:t + 1], smin1[:, t:t + 1], SCALE1, None, ALU.mult
                                        ).then_inc(s_mb1, 1)
                    v.wait_ge(s_ex1, TB * i + TB)
                    v.reciprocal(sinv1[:], ssum1[:]).then_inc(s_iv1, 1)
                if last:
                    v.wait_ge(s_xa1, 2 * 5)
                    ln3.free_slots(v)
                    ln3.normalise(v, 0)
                if not first:
                    for c in range(KT):
                        v.wait_ge(s_ch1, KT * (i - 1) + c + 1)
                        v.scalar_tensor_tensor(ctx1_lo[:, c, :], bank[6 + c][:, :],
                                               bcol1[:, 2 * KT + c:2 * KT + c + 1], ctx1_hi[:, c, :], ALU.add,
                                               ALU.subtract).then_inc(s_cl1, 1)
                if not last:
                    for n, (j, bk) in enumerate(TURNS):
                        v.wait_ge(s_th1, TB * i + n + 1)
                        v.tensor_tensor(pt1_lo[:, j, :], bank[bk][:, :], pt1_hi[:, j, :], ALU.subtract
                                        ).then_inc(s_tl1, 1)
                if last:
                    ln3.modulate(v, 0)
                if not first:
                    for q in range(2):
                        v.wait_ge(s_om1, 2 * (i - 1) + q + 1)
                        v.wait_ge(s_xa1, 5 * i - 1)
                        v.scalar_tensor_tensor(osum1[:, 2 * q:2 * q + 2, :],
                                               bank[2 + q][:, :].rearrange("p (t d) -> p t d", t=2),
                                               1.0 / (WS * PS * WS),
                                               gate[:, ds((i - 1) * D, D)].unsqueeze(1).broadcast_to([P, 2, D]),
                                               ALU.mult, ALU.mult).then_inc(s_or1, 1)
            run1(v, step)
            xb = x[:, TB * (B - 1):, :]
            v.wait_ge(s_xa1, 5 * B - 1)
            v.wait_ge(s_or1, 2 * B + 2)
            v.tensor_tensor(xb, xb, osum1[:], ALU.add).then_inc(s_xa1, 1)

        @block.tensor
        def _(pe):
            def step(i, first, last):
                if not last:
                    for t in range(TB):
                        if not first and t < 2:
                            pe.wait_ge(s_tl1, TB * (i - 1) + 1 + t)
                        elif not first:
                            pe.wait_ge(s_or1, 2 * i)
                        split3(pe, bank[t][:, :],
                               [((qk1_hi[:, c, ds(i * S + t * P, P)], qk1_lo[:, c, ds(i * S + t * P, P)]),
                                 (qk1_hi[:, KT + c, ds(i * S, S)], qk1_lo[:, KT + c, ds(i * S, S)]))
                                for c in range(KT)]).then_inc(s_sc1, 1)
                if not first:
                    pe.wait_ge(s_tl1, TB * i)
                    for c in range(KT):
                        split3(pe, bank[6 + c][:, :],
                               [((v1_hi[:, (i - 1) * TB + j, c * P:(c + 1) * P],
                                  v1_lo[:, (i - 1) * TB + j, c * P:(c + 1) * P]),
                                 (pt1_hi[:, j, :], pt1_lo[:, j, :])) for j in range(TB)]).then_inc(s_cm1, 1)
                if not last:
                    pe.wait_ge(s_nm1, TB * i + TB)
                    for j, bk in TURNS:
                        for t in range(TB):
                            ins = pe.transpose(bank[bk][:, t * P:(t + 1) * P], prob1[:, t, j * P:(j + 1) * P],
                                               ident[:, :])
                        ins.then_inc(s_tn1, 1)
                if last:
                    ln3.tensor(pe, 0)
                if not first:
                    pe.wait_ge(s_cl1, KT * i)
                    if not last:
                        pe.wait_ge(s_ex1, TB * i + TB)
                    for q in range(2):
                        for t in (2 * q, 2 * q + 1):
                            ins = split3(pe, bank[2 + q][:, (t % 2) * D:(t % 2 + 1) * D],
                                         [((ctx1_hi[:, c, t * P:(t + 1) * P], ctx1_lo[:, c, t * P:(t + 1) * P]),
                                           (wo1_hi[:, c, :], wo1_lo[:, c, :])) for c in range(KT)])
                        ins.then_inc(s_om1, 1)
            run1(pe, step)

    b4t = layout(P3)
    mT_hi = b4t("mT_hi", [P, IC, B * S], F16)
    mT_lo = b4t("mT_lo", [P, IC, B * S], F16)
    silu = [b4t(f"silu{i}", [P, S], F32) for i in range(2)]
    prod = [b4t(f"prod{i}", [P, S], F32) for i in range(2)]
    osum4 = b4t("osum4", [P, TB, D], F32)
    assert b4t.pos[0] <= NEXT
    (s_gate4, s_gmm, s_umm, s_silu, s_prod, s_mhi, s_mlo, s_dmm, s_dread, s_xout, s_stored) = (
        k.sem(n) for n in ("gate4_in", "gate_mm", "up_mm", "silu_done", "product", "m_hi", "m_lo", "down_mm",
                           "down_read", "x_final", "stored"))
    GW = KT * INTER

    def dec(w, which, c, o):
        if which < 2:
            a = which * GW + c * INTER + o * P
            return w[:, a:a + (P if o < IC - 1 else LASTI)]
        return w[0:(P if c < IC - 1 else LASTI), 2 * GW + c * D:2 * GW + (c + 1) * D]

    with nc.Block() as block:
        @block.sync
        def _(sp):
            load_gate(sp, 1, 1, s_gate4)
            with sp.Fori(0, B - 1) as b:
                sp.wait_ge(s_xout, b + 2)
                sp.dma_start(A["out"][:, ds(b * TB, TB), :], x[:, ds(b * TB, TB), :]).then_inc(s_stored, 16)
            for q in range(2):
                tiles = slice((B - 1) * TB + 2 * q, (B - 1) * TB + 2 * q + 2)
                sp.wait_ge(s_xout, B + 1 + q)
                sp.dma_start(A["out"][:, tiles, :], x[:, tiles, :]).then_inc(s_stored, 16)
            sp.wait_ge(s_stored, 16 * (B + 1))

        @block.gpsimd
        def _(g):
            ln3.inverse(g, 1)

            def products(b):
                for oc in range(IC):
                    w = P if oc < IC - 1 else LASTI
                    g.wait_ge(s_mhi, IC * b + oc + 1)
                    g.tensor_tensor(mT_lo[0:w, oc, ds(b * S, S)], prod[oc % 2][0:w, :],
                                    mT_hi[0:w, oc, ds(b * S, S)], ALU.subtract).then_inc(s_mlo, 1)
            products(0)
            ln3.split_lo(g, 1)
            with g.Fori(1, B) as b:
                products(b)

        @block.scalar
        def _(act):
            act.preload_act_table(ACT.Silu)

            def silu_of(b, oc):
                w = P if oc < IC - 1 else LASTI
                act.wait_ge(s_gmm, IC * b + oc + 1)
                act.wait_ge(s_prod, IC * b + oc + 1)
                act.activation(silu[oc % 2][0:w, :], bank[oc % 2][0:w, :], ACT.Silu, scale=1.0 / WS
                               ).then_inc(s_silu, 1)

            def hi_of(b, oc):
                w = P if oc < IC - 1 else LASTI
                act.wait_ge(s_prod, 2 + IC * b + oc + 1)
                act.activation(mT_hi[0:w, oc, ds(b * S, S)], prod[oc % 2][0:w, :], ACT.Copy).then_inc(s_mhi, 1)

            def products(b):
                silu_of(b, 0)
                for oc in range(1, IC):
                    silu_of(b, oc)
                    hi_of(b, oc - 1)
                hi_of(b, IC - 1)
            products(0)
            ln3.scalar(act, 1)
            with act.Fori(1, B) as b:
                products(b)

        @block.vector
        def _(v):
            v.sem_inc(s_mlo, 2)
            v.sem_inc(s_prod, 2)
            v.sem_inc(s_dread, 2)
            v.sem_inc(s_xout, 1)
            ln3.normalise(v, 1)

            def products(b):
                for oc in range(IC):
                    w = P if oc < IC - 1 else LASTI
                    v.wait_ge(s_umm, IC * b + oc + 1)
                    v.wait_ge(s_silu, IC * b + oc + 1)
                    v.wait_ge(s_mlo, IC * b + oc + 1)
                    v.scalar_tensor_tensor(prod[oc % 2][0:w, :], bank[2 + oc % 2][0:w, :], 1.0 / WS,
                                           silu[oc % 2][0:w, :], ALU.mult, ALU.mult).then_inc(s_prod, 1)

            def down_out(b):
                v.wait_ge(s_xout, b + 1)
                for q in range(2):
                    v.wait_ge(s_dmm, 2 * b + q + 1)
                    v.scalar_tensor_tensor(osum4[:, 2 * q:2 * q + 2, :],
                                           bank[6 + q][:, :].rearrange("p (t d) -> p t d", t=2), 1.0 / WS,
                                           gate[:, ds(b * D, D)].unsqueeze(1).broadcast_to([P, 2, D]),
                                           ALU.mult, ALU.mult).then_inc(s_dread, 1)
                v.wait_ge(s_dread, 2 + 2 * b + 2)
                xb = x[:, ds(b * TB, TB), :]
                v.tensor_tensor(xb, xb, osum4[:], ALU.add).then_inc(s_xout, 1)
            products(0)
            ln3.modulate(v, 1)
            v.wait_ge(s_gate4, 16)
            with v.Fori(1, B) as b:
                products(b)
                down_out(b - 1)
            v.wait_ge(s_xout, B)
            for q in range(2):
                v.wait_ge(s_dmm, 2 * (B - 1) + q + 1)
                v.scalar_tensor_tensor(osum4[:, 2 * q:2 * q + 2, :],
                                       bank[6 + q][:, :].rearrange("p (t d) -> p t d", t=2), 1.0 / WS,
                                       gate[:, (B - 1) * D:B * D].unsqueeze(1).broadcast_to([P, 2, D]),
                                       ALU.mult, ALU.mult).then_inc(s_dread, 1)
                v.wait_ge(s_dread, 2 * B + q + 1)
                xb = x[:, (B - 1) * TB + 2 * q:(B - 1) * TB + 2 * q + 2, :]
                v.tensor_tensor(xb, xb, osum4[:, 2 * q:2 * q + 2, :], ALU.add).then_inc(s_xout, 1)

        @block.tensor
        def _(pe):
            def gate_up(b):
                ln3.wait_parts(pe, b)
                for oc in range(IC):
                    w = P if oc < IC - 1 else LASTI
                    wait_apart(pe, s_prod, IC * b + oc + 1, s_passed)
                    for which, sem in ((0, s_gmm), (1, s_umm)):
                        split3(pe, bank[2 * which + oc % 2][0:w, :],
                               [((dec(wdec_hi, which, c, oc), dec(wdec_lo, which, c, oc)),
                                 (hT_hi[:, c, ds(b * S, S)], hT_lo[:, c, ds(b * S, S)])) for c in range(KT)]
                               ).then_inc(sem, 1)

            def down(b):
                pe.wait_ge(s_mlo, 2 + IC * b + IC)
                for q in range(2):
                    pe.wait_ge(s_dread, 2 * b + q + 1)
                    for t in (2 * q, 2 * q + 1):
                        pairs = []
                        for oc in range(IC):
                            w = P if oc < IC - 1 else LASTI
                            tok = b * S + t * P
                            pairs.append(((mT_hi[0:w, oc, ds(tok, P)], mT_lo[0:w, oc, ds(tok, P)]),
                                          (dec(wdec_hi, 2, oc, 0), dec(wdec_lo, 2, oc, 0))))
                        ins = split3(pe, bank[6 + q][:, (t % 2) * D:(t % 2 + 1) * D], pairs)
                    ins.then_inc(s_dmm, 1)
            gate_up(0)
            ln3.tensor(pe, 1)
            with pe.Fori(1, B) as b:
                gate_up(b)
                down(b - 1)
            down(B - 1)


def host_layout(inputs):
    import numpy as np
    n = {key: np.asarray(v) for key, v in inputs.items()}

    def feat(w):
        return np.ascontiguousarray(w.reshape(-1, P, w.shape[-1]).transpose(1, 0, 2))

    def col(v):
        return v.reshape(-1, P).T

    a = {}
    a["x"] = np.ascontiguousarray(n["L0_attn_x"].reshape(NT, P, D).transpose(1, 0, 2))
    a["cT"] = np.ascontiguousarray(np.stack([n["L0_c"].T, n["L1_c"].T]).reshape(2, KT, P, B)
                                   .transpose(2, 0, 1, 3).reshape(P, -1))
    a["wmod"] = np.ascontiguousarray(np.stack([n["L0_wmod"], n["L1_wmod"]]).reshape(2, KT, P, 6 * D)
                                     .transpose(2, 0, 1, 3))
    qkv = n["L0_attn_qkv_w"]
    a["wqk"] = feat(qkv[:, :QKW])
    a["wv"] = feat(qkv[:, QKW:])
    a["wo"] = feat(n["L0_attn_out_w"])
    a["cols"] = np.ascontiguousarray(np.concatenate(
        [col(n["L0_attn_qkv_b"]), col(n["L0_ffn_amp_b"]), col(n["L0_ffn_ph_b"])]
        + [col(n[f"L0_ffn_{g}"].reshape(-1)) for g in ("ln3_g", "ln3_b", "ln4_g", "ln4_b")]
        + [col(n["L1_attn_b_qkv"]), col(n["L0_ffn_ent_b"].reshape(-1))], axis=1))
    a["slopes"] = np.tile(np.array([1.0 / 2.0 ** (i / 2.0) for i in range(H)], np.float32), (P, 1))
    a["rows"] = np.ascontiguousarray(np.concatenate(
        [n["L0_attn_out_b"], n["L0_ffn_ent_pb"].reshape(-1), n["L0_ffn_path_b"].reshape(-1),
         n["L0_ffn_phase"].reshape(-1), n["L0_ffn_ln4_g"][-1], n["L0_ffn_ln4_b"][-1], n["L1_attn_b_out"]])
        .reshape(1, -1))
    a["amph"] = np.ascontiguousarray(np.stack([feat(n["L0_ffn_amp_w"]), feat(n["L0_ffn_ph_w"])], axis=1))
    a["entwT"] = np.ascontiguousarray(np.stack([feat(w.T) for w in n["L0_ffn_ent_w"]], axis=1))
    a["entpw"] = np.ascontiguousarray(np.stack([feat(w) for w in n["L0_ffn_ent_pw"]], axis=1))
    a["path"] = np.ascontiguousarray(np.stack([np.stack([feat(w) for w in l], axis=1)
                                               for l in n["L0_ffn_path_w"]], axis=1))
    a["wqkv1"] = feat(n["L1_attn_w_qkv"].T)
    a["wout1"] = feat(n["L1_attn_w_out"].T)
    down = np.zeros((IC * P, D), np.int32)
    down[:INTER] = n["L1_ffn_down_idx"].T
    a["idx"] = np.ascontiguousarray(np.concatenate(
        [feat(n["L1_ffn_gate_idx"].T).reshape(P, -1), feat(n["L1_ffn_up_idx"].T).reshape(P, -1),
         feat(down).reshape(P, -1)], axis=1))
    a["lut"] = np.ascontiguousarray(n["L1_ffn_lut"].reshape(1, -1))
    return a


def kernel(**inputs):
    import concourse.bacc as bacc
    from concourse.bass_utils import run_bass_kernel_spmd

    nc = bacc.Bacc("TRN2", target_bir_lowering=False, num_devices=1)
    arrays = {f"in_{name}": a for name, a in host_layout(inputs).items()}
    aps = {name[3:]: nc.dram_tensor(name, a.shape, mybir.dt.from_np(a.dtype), kind="ExternalInput").ap()
           for name, a in arrays.items()}
    aps["out"] = nc.dram_tensor("out", (P, NT, D), F32, kind="ExternalOutput").ap()
    build(nc, aps)
    r = run_bass_kernel_spmd(nc, [arrays], core_ids=[0])
    y = r.results[0]["out"]
    return y.reshape(P, NT, D).transpose(1, 0, 2).reshape(B, S, D)
```
